# Optimizing a Trainium2 kernel written in Bass

```python
import numpy as np
import jax
import jax.numpy as jnp

def _softmax(x, axis=-1):
    return jax.nn.softmax(x, axis=axis)

def _gelu(x):
    return jax.nn.gelu(x, approximate=True)

def _silu(x):
    return jax.nn.silu(x)

def _sigmoid(x):
    return jax.nn.sigmoid(x)

def _layernorm(x, axis=-1, eps=1e-05):
    m = jnp.mean(x, axis=axis, keepdims=True)
    v = jnp.var(x, axis=axis, keepdims=True)
    return (x - m) / jnp.sqrt(v + eps)

def _scatter_add(tgt, idx, src, axis=0):
    return tgt.at[idx].add(src)

def _segment_sum(src, seg, n):
    return jax.ops.segment_sum(src, seg, n)
kernel_name = 'mk_early_fusion_embed_d1_tok_img768_r4_3965bc'

def setup_inputs(seed: int=0):
    np.random.seed(seed)
    _w = jnp.asarray

    def _rec_inputs():
        import jax
        import jax.numpy as jnp
        _rk = jax.random.key(seed)
        x = 7.57192e-06 + 1.00007 * jax.random.normal(jax.random.fold_in(_rk, 1), (16, 3, 224, 224), jnp.float32)
        x_txt = jax.random.randint(jax.random.fold_in(_rk, 51), (16, 32), 0, 31983, jnp.int32)
        return (x, x_txt)
    x, x_txt = _rec_inputs()

    def _L0_tok_setup():
        import jax, jax.numpy as jnp
        import numpy as np
        from jax import lax
        P = 16
        S = 8
        key = jax.random.key(seed)
        k1, k2, k3, k4, k5 = jax.random.split(key, 5)
        B, C, H, W = (64, 3, 224, 224)
        D = 192
        patch_dim = C * P * P
        out = (H - P) // S + 1
        n_tok = out * out + 1
        return {'x': jax.random.normal(k1, (B, C, H, W), dtype=jnp.float32), 'w': jax.random.normal(k2, (D, patch_dim), dtype=jnp.float32) * 0.02, 'b': jax.random.normal(k3, (D,), dtype=jnp.float32) * 0.02, 'cls_token': jax.random.normal(k4, (1, 1, D), dtype=jnp.float32), 'pos_embedding': jax.random.normal(k5, (1, n_tok, D), dtype=jnp.float32)}
    _L0_tok_all = _L0_tok_setup()
    _L0_tok_in = {k: v for k, v in _L0_tok_all.items() if k in ('w', 'b', 'cls_token', 'pos_embedding')}
    del _L0_tok_all

    def _L0_txt_setup():
        import jax, jax.numpy as jnp
        import numpy as np
        NUM_EMBEDDINGS = 8000
        EMBED_DIM = 192
        BATCH, POS = (2, 512)
        INIT_RANGE = 0.02
        key = jax.random.key(seed)
        kx, kw = jax.random.split(key)
        x = jax.random.randint(kx, (BATCH, POS), 0, NUM_EMBEDDINGS, dtype=jnp.int64 if jax.config.jax_enable_x64 else jnp.int32)
        W = jax.random.normal(kw, (NUM_EMBEDDINGS, EMBED_DIM), dtype=jnp.float32) * INIT_RANGE
        return {'x': x, 'W': W}
    _L0_txt_all = _L0_txt_setup()
    _L0_txt_in = {k: v for k, v in _L0_txt_all.items() if k in ('W',)}
    del _L0_txt_all

    def _L0_attn_setup():
        import jax, jax.numpy as jnp
        import numpy as np
        B, L, D, M = (1, 512, 192, 64)
        key = jax.random.key(seed)
        ks = jax.random.split(key, 9)

        def w(k, shape):
            return jax.random.normal(k, shape, jnp.float32) * shape[0] ** (-0.5)
        x = jax.random.normal(ks[0], (B, L, D), jnp.float32)
        Wq = w(ks[1], (D, M))
        Wk = w(ks[2], (D, M))
        Wv = w(ks[3], (D, D))
        Wf = w(ks[4], (D, M))
        bf = jnp.zeros((M,), jnp.float32)
        Wo = w(ks[5], (D, D))
        gamma = jnp.ones((D,), jnp.float32)
        beta = jnp.zeros((D,), jnp.float32)
        return {'x': x, 'Wq': Wq, 'Wk': Wk, 'Wv': Wv, 'Wf': Wf, 'bf': bf, 'Wo': Wo, 'gamma': gamma, 'beta': beta}
    _L0_attn_all = _L0_attn_setup()
    _L0_attn_in = {k: v for k, v in _L0_attn_all.items() if k in ('Wq', 'Wk', 'Wv', 'Wf', 'bf', 'Wo', 'gamma', 'beta')}
    del _L0_attn_all

    def _L0_ffn_setup():
        import jax, jax.numpy as jnp
        import numpy as np
        B, S, H, D, E = (4, 512, 192, 256, 8)
        TOP_K = 2
        EPS = 1e-08
        LN_EPS = 1e-05

        def _gelu(t):
            return jax.nn.gelu(t, approximate=False)

        def _layer_norm(t, gamma, beta):
            mu = jnp.mean(t, axis=-1, keepdims=True)
            var = jnp.mean(jnp.square(t - mu), axis=-1, keepdims=True)
            return (t - mu) * jax.lax.rsqrt(var + LN_EPS) * gamma + beta
        key = jax.random.key(seed)
        ks = jax.random.split(key, 8)
        x = jax.random.normal(ks[0], (B, S, H), dtype=jnp.float32)
        w1 = jax.random.normal(ks[1], (H, H // 2), dtype=jnp.float32) * 0.02
        b1 = jnp.zeros((H // 2,), dtype=jnp.float32)
        w2 = jax.random.normal(ks[2], (H // 2, E), dtype=jnp.float32) * 0.02
        b2 = jnp.zeros((E,), dtype=jnp.float32)
        a_dn = float(np.sqrt(6.0 / (H + D)))
        a_up = float(np.sqrt(6.0 / (D + H)))
        down_w = jax.random.uniform(ks[3], (E, H, D), dtype=jnp.float32, minval=-a_dn, maxval=a_dn)
        down_b = jnp.zeros((E, D), dtype=jnp.float32)
        up_w = jax.random.uniform(ks[4], (E, D, H), dtype=jnp.float32, minval=-a_up, maxval=a_up)
        gamma = jnp.ones((H,), dtype=jnp.float32)
        beta = jnp.zeros((H,), dtype=jnp.float32)
        return {'x': x, 'w1': w1, 'b1': b1, 'w2': w2, 'b2': b2, 'down_w': down_w, 'down_b': down_b, 'up_w': up_w, 'gamma': gamma, 'beta': beta}
    _L0_ffn_all = _L0_ffn_setup()
    _L0_ffn_in = {k: v for k, v in _L0_ffn_all.items() if k in ('w1', 'b1', 'w2', 'b2', 'down_w', 'down_b', 'up_w', 'gamma', 'beta')}
    del _L0_ffn_all
    return {'x': x, 'x_txt': x_txt, 'L0_tok_w': _L0_tok_in['w'], 'L0_tok_b': _L0_tok_in['b'], 'L0_tok_cls_token': _L0_tok_in['cls_token'], 'L0_tok_pos_embedding': _L0_tok_in['pos_embedding'], 'L0_txt_W': _L0_txt_in['W'], 'L0_attn_Wq': _L0_attn_in['Wq'], 'L0_attn_Wk': _L0_attn_in['Wk'], 'L0_attn_Wv': _L0_attn_in['Wv'], 'L0_attn_Wf': _L0_attn_in['Wf'], 'L0_attn_bf': _L0_attn_in['bf'], 'L0_attn_Wo': _L0_attn_in['Wo'], 'L0_attn_gamma': _L0_attn_in['gamma'], 'L0_attn_beta': _L0_attn_in['beta'], 'L0_ffn_w1': _L0_ffn_in['w1'], 'L0_ffn_b1': _L0_ffn_in['b1'], 'L0_ffn_w2': _L0_ffn_in['w2'], 'L0_ffn_b2': _L0_ffn_in['b2'], 'L0_ffn_down_w': _L0_ffn_in['down_w'], 'L0_ffn_down_b': _L0_ffn_in['down_b'], 'L0_ffn_up_w': _L0_ffn_in['up_w'], 'L0_ffn_gamma': _L0_ffn_in['gamma'], 'L0_ffn_beta': _L0_ffn_in['beta']}

def reference(x, x_txt, L0_tok_w, L0_tok_b, L0_tok_cls_token, L0_tok_pos_embedding, L0_txt_W, L0_attn_Wq, L0_attn_Wk, L0_attn_Wv, L0_attn_Wf, L0_attn_bf, L0_attn_Wo, L0_attn_gamma, L0_attn_beta, L0_ffn_w1, L0_ffn_b1, L0_ffn_w2, L0_ffn_b2, L0_ffn_down_w, L0_ffn_down_b, L0_ffn_up_w, L0_ffn_gamma, L0_ffn_beta):
    import jax
    import jax.numpy as jnp

    def _L0_tok_ref(x, w, b, cls_token, pos_embedding):
        import jax, jax.numpy as jnp
        import numpy as np
        from jax import lax
        P = 16
        S = 8
        B = x.shape[0]
        patches = lax.conv_general_dilated_patches(x, filter_shape=(P, P), window_strides=(S, S), padding='VALID', dimension_numbers=('NCHW', 'OIHW', 'NCHW'))
        pd = patches.shape[1]
        patches = patches.reshape(B, pd, -1).transpose(0, 2, 1)
        tok = jnp.einsum('bnp,dp->bnd', patches, w) + b
        cls = jnp.broadcast_to(cls_token, (B, 1, tok.shape[-1]))
        out = jnp.concatenate([cls, tok], axis=1) + pos_embedding
        return out

    def _L0_txt_ref(x, W):
        import jax, jax.numpy as jnp
        import numpy as np
        NUM_EMBEDDINGS = 8000
        EMBED_DIM = 192
        BATCH, POS = (2, 512)
        INIT_RANGE = 0.02
        onehot = jax.nn.one_hot(x, NUM_EMBEDDINGS, dtype=W.dtype)
        return jnp.einsum('bpn,nd->bpd', onehot, W)

    def _L0_attn_ref(x, Wq, Wk, Wv, Wf, bf, Wo, gamma, beta):
        import jax, jax.numpy as jnp
        import numpy as np
        B, L, D, M = (1, 512, 192, 64)
        m_dim = Wq.shape[1]
        scale = m_dim ** (-0.5)
        q = (jax.nn.elu(x @ Wq) + 1.0) * scale
        k = jax.nn.elu(x @ Wk) + 1.0
        v = x @ Wv
        forget = jax.nn.sigmoid(x @ Wf + bf)
        log_f = jnp.log(jnp.clip(forget, 1e-06, None))
        log_f_cum = jnp.clip(jnp.cumsum(log_f, axis=1), -20.0, 20.0)
        exp_neg = jnp.exp(-log_f_cum)
        exp_pos = jnp.exp(log_f_cum)
        kv = k[..., :, None] * v[..., None, :]
        cum_kv = jnp.cumsum(exp_neg[..., None] * kv, axis=1)
        Mstate = exp_pos[..., None] * cum_kv
        z = exp_pos * jnp.cumsum(exp_neg * k, axis=1)
        numerator = jnp.einsum('blm,blmd->bld', q, Mstate)
        denominator = jnp.einsum('blm,blm->bl', q, z)[..., None] + 1e-06
        h = numerator / denominator
        mu = jnp.mean(h, axis=-1, keepdims=True)
        var = jnp.var(h, axis=-1, keepdims=True)
        normed = (h - mu) / jnp.sqrt(var + 1e-05) * gamma + beta
        return normed @ Wo

    def _L0_ffn_ref(x, w1, b1, w2, b2, down_w, down_b, up_w, gamma, beta):
        import jax, jax.numpy as jnp
        import numpy as np
        B, S, H, D, E = (4, 512, 192, 256, 8)
        TOP_K = 2
        EPS = 1e-08
        LN_EPS = 1e-05

        def _gelu(t):
            return jax.nn.gelu(t, approximate=False)

        def _layer_norm(t, gamma, beta):
            mu = jnp.mean(t, axis=-1, keepdims=True)
            var = jnp.mean(jnp.square(t - mu), axis=-1, keepdims=True)
            return (t - mu) * jax.lax.rsqrt(var + LN_EPS) * gamma + beta
        logits = _gelu(x @ w1 + b1) @ w2 + b2
        routing = jax.nn.softmax(logits, axis=-1)
        topv, topi = jax.lax.top_k(routing, TOP_K)
        sparse = jnp.sum(jax.nn.one_hot(topi, E, dtype=routing.dtype) * topv[..., None], axis=-2)
        sparse = sparse / (jnp.sum(sparse, axis=-1, keepdims=True) + EPS)
        z = _gelu(jnp.einsum('bsh,ehd->bsed', x, down_w) + down_b)
        expert_out = jnp.einsum('bsed,edh->bseh', z, up_w)
        moe_out = jnp.einsum('bseh,bse->bsh', expert_out, sparse)
        return _layer_norm(x + moe_out, gamma, beta)
    h = _L0_tok_ref(x, L0_tok_w, L0_tok_b, L0_tok_cls_token, L0_tok_pos_embedding)
    h = jnp.concatenate([h, _L0_txt_ref(x_txt, L0_txt_W)], axis=1)
    h = h + _L0_attn_ref(_layernorm(h, axis=-1), L0_attn_Wq, L0_attn_Wk, L0_attn_Wv, L0_attn_Wf, L0_attn_bf, L0_attn_Wo, L0_attn_gamma, L0_attn_beta)
    h = h + _L0_ffn_ref(_layernorm(h, axis=-1), L0_ffn_w1, L0_ffn_b1, L0_ffn_w2, L0_ffn_b2, L0_ffn_down_w, L0_ffn_down_b, L0_ffn_up_w, L0_ffn_gamma, L0_ffn_beta)
    return h

_drawn_inputs = setup_inputs


def setup_inputs(seed=0):
    import zlib

    import numpy as np

    out = dict(_drawn_inputs(seed))
    spreads = {'L0_attn_bf': (0.0, 2.0),
     'L0_attn_gamma': (1.0, 0.2),
     'L0_attn_beta': (0.0, 0.1),
     'L0_ffn_b1': (0.0, 0.1),
     'L0_ffn_b2': (0.0, 0.1),
     'L0_ffn_down_b': (0.0, 0.448),
     'L0_ffn_gamma': (1.0, 0.2),
     'L0_ffn_beta': (0.0, 0.1)}
    factors = {'L0_txt_W': 17.023, 'L0_attn_Wf': 10.564}
    for name, (base, spread) in spreads.items():
        noise = np.random.default_rng([zlib.crc32(name.encode()), seed]).standard_normal(out[name].shape)
        drawn = base * np.exp(spread * noise) if base else spread * noise
        out[name] = jnp.asarray(drawn.astype(out[name].dtype))
    for name, factor in factors.items():
        out[name] = (out[name] * factor).astype(out[name].dtype)
    return out
```

```python
import concourse.bass as bass
from concourse import mybir
from contextlib import ExitStack

BATCH, D = 16, 192
GRID, BLK = 27, 28
TOK_IMG = GRID * GRID + 1
TXT = 32
L = TOK_IMG + TXT
CH = 127
NCH = L // CH
NPAIR = NCH // 2
HALF = L // 2
KA, KB = 128, D - 128
M_DIM = 64
VOCAB = 8000
NPROJ = 4 * M_DIM + D
NE, DH = 8, 256
HT = NE * DH // 128
H1 = D // 2
GCH = 4
GT = GCH * CH
NG = BATCH * NCH // GCH
XW = 790
WS = 1024.0
PROB_CLAMP = 1e6 - 1.0
Z_BANKS = 4
Z_RING = 4


def embed_fuse_moe(nc, xblk, ids, wtok, pos, cls, rows, cols, table, wproj, wout, wr1, wr2, wdown, wup, out):
    fp32, fp16, i32 = mybir.dt.float32, mybir.dt.float16, mybir.dt.int32
    ALU = mybir.AluOpType
    ACT = mybir.ActivationFunctionType
    AX = mybir.AxisListType.X

    ctx = ExitStack()
    with ctx:
        def sem(name, scope=ctx):
            return scope.enter_context(nc.semaphore(name))

        def sb(name, shape, dt=fp32, scope=ctx):
            return scope.enter_context(nc.sbuf_tensor(name, shape, dt))

        def need(eng, s, value):
            if not isinstance(value, int) or value > 0:
                eng.wait_ge(s, value)

        banks = [ctx.enter_context(nc.psum_tensor(f"bank{i}", [128, 512], fp32)) for i in range(8)]

        H = sb("H", [128, BATCH * NCH, D])
        ident = sb("ident", [128, 128])
        minus_half = sb("minus_half", [CH, NCH])
        epsilon = sb("epsilon", [CH, NCH])
        colv = sb("colv", [128, 22])
        rowv = sb("rowv", [CH, 3 * D + NE])
        down_h = sb("down_h", [128, 2, NE * DH], fp16)
        down_l = sb("down_l", [128, 2, NE * DH], fp16)
        up_h = sb("up_h", [128, HT, D], fp16)
        up_l = sb("up_l", [128, HT, D], fp16)
        r1_h = sb("r1_h", [128, 2, H1], fp16)
        r1_l = sb("r1_l", [128, 2, H1], fp16)
        r2 = sb("r2", [H1, NE])
        forget_bias, down_b, router_b1 = colv[:, 0:1], colv[:, 5:21], colv[0:H1, 21:22]
        tok_b, ffn_gamma, ffn_beta, router_b2 = (
            rowv[:, 0:D], rowv[:, D:2 * D], rowv[:, 2 * D:3 * D], rowv[:, 3 * D:3 * D + NE])

        def mm_features(pe, dst, w_h, w_l, lo, hi, x_h, x_l, x_s, c0, c1):
            pe.matmul(dst, w_h[:, 0, lo:hi], x_h[:, c0:c1], start=True, stop=False)
            pe.matmul(dst, w_h[:, 0, lo:hi], x_l[:, c0:c1], start=False, stop=False)
            pe.matmul(dst, w_l[:, 0, lo:hi], x_h[:, c0:c1], start=False, stop=False)
            pe.matmul(dst, w_h[:, 1, lo:hi], x_s[:, c0:c1], start=False, stop=False)
            return pe.matmul(dst, w_l[:, 1, lo:hi], x_s[:, c0:c1], start=False, stop=True)

        def mm_tokens(pe, dst, w_h, w_l, lo, hi, x_h, x_l, x_s, c0):
            c1 = c0 + 128
            pe.matmul(dst, x_h[:, c0:c1], w_h[:, 0, lo:hi], start=True, stop=False)
            pe.matmul(dst, x_h[:, c0:c1], w_l[:, 0, lo:hi], start=False, stop=False)
            pe.matmul(dst, x_l[:, c0:c1], w_h[:, 0, lo:hi], start=False, stop=False)
            pe.matmul(dst, x_s[:, c0:c1], w_h[:, 1, lo:hi], start=False, stop=False)
            return pe.matmul(dst, x_s[:, c0:c1], w_l[:, 1, lo:hi], start=False, stop=True)

        ctxa = ExitStack()
        with ctxa:
            def sa(name, shape, dt=fp32):
                return sb(name, shape, dt, ctxa)

            def sema(name):
                return sem(name, ctxa)

            xa = sa("xa", [128, BLK * BLK])
            xb = sa("xb", [128, BLK * BLK])
            pa_h = [sa(f"pa_h{i}", [128, 2, XW], fp16) for i in range(2)]
            pa_l = [sa(f"pa_l{i}", [128, 2, XW], fp16) for i in range(2)]
            pb_h = [sa(f"pb_h{i}", [128, XW], fp16) for i in range(2)]
            pb_l = [sa(f"pb_l{i}", [128, XW], fp16) for i in range(2)]
            wt_h = sa("wt_h", [128, 6, D], fp16)
            wt_l = sa("wt_l", [128, 6, D], fp16)
            wp_h = sa("wp_h", [128, 2, NPROJ], fp16)
            wp_l = sa("wp_l", [128, 2, NPROJ], fp16)
            wo_h = sa("wo_h", [128, 2, D], fp16)
            wo_l = sa("wo_l", [128, 2, D], fp16)
            base = sa("base", [128, NCH - 1 + BATCH, D])
            patch_rows = sa("patch_rows", [CH, NCH])
            causal = sa("causal", [CH, CH + M_DIM])
            gate_sign = sa("gate_sign", [128, 1])
            beta_cols = sa("beta_cols", [128, 2, CH])
            beta_out = sa("beta_out", [CH, D])
            badd0 = sa("badd0", [CH, D])
            idx = sa("idx", [128, 4], i32)
            idx_ok = sa("idx_ok", [128, 4])
            idx_hi = sa("idx_hi", [128, 4])
            idx_c = sa("idx_c", [128, 4], i32)
            xn = [sa(f"xn{i}", [CH, 2, D]) for i in range(2)]
            x_h = sa("x_h", [128, L + 2], fp16)
            x_l = sa("x_l", [128, L + 2], fp16)
            x_s = sa("x_s", [128, L + 2], fp16)
            stat1 = sa("stat1", [CH, NCH, 6])
            mv1 = sa("mv1", [CH, NCH, 2])
            rstd1 = sa("rstd1", [CH, NCH])
            var1 = sa("var1", [CH, NCH])
            qk = sa("qk", [128, L])
            qk_e = sa("qk_e", [128, L])
            gate = sa("gate", [128, L])
            cum = sa("cum", [128, L])
            qT = [sa(f"qT{i}", [M_DIM, L]) for i in range(2)]
            kT = [sa(f"kT{i}", [M_DIM, L]) for i in range(2)]
            v = [sa(f"v{i}", [CH, NCH, D + 1]) for i in range(2)]
            pk = [sa(f"pk{i}", [CH, CH + M_DIM]) for i in range(2)]
            state = [sa(f"state{i}", [M_DIM, D + 1]) for i in range(2)]
            num = sa("num", [CH, 2, D + 1])
            stat2 = sa("stat2", [CH, NCH, 6])
            mv2 = sa("mv2", [CH, NCH, 2])
            den = sa("den", [CH, NCH])
            rden = sa("rden", [CH, NCH])
            vn = sa("vn", [CH, NCH])
            hs = sa("hs", [CH, NCH])
            hscale = sa("hscale", [CH, NCH])
            y = sa("y", [CH, 2, D])
            y_h = [sa(f"y_h{i}", [128, 256], fp16) for i in range(2)]
            y_l = [sa(f"y_l{i}", [128, 256], fp16) for i in range(2)]
            y_s = [sa(f"y_s{i}", [128, 256], fp16) for i in range(2)]

            Hflat = H[:, :, :].rearrange("p c d -> p (c d)")
            at = [40 * D]

            def staged(n):
                at[0] += n
                return Hflat[:, at[0] - n:at[0]]
            raw_tok = staged(6 * D).rearrange("p (k n) -> p k n", k=6)
            raw_proj = staged(2 * NPROJ).rearrange("p (k n) -> p k n", k=2)
            raw_out = staged(2 * D).rearrange("p (k n) -> p k n", k=2)
            raw_r1 = staged(2 * H1).rearrange("p (k n) -> p k n", k=2)
            raw_down = staged(2 * NE * DH).rearrange("p (k n) -> p k n", k=2)
            raw_up = staged(HT * D).rearrange("p (k n) -> p k n", k=HT)
            txt = staged(4 * D).rearrange("p (g n) -> p g n", g=4)
            pos5 = staged(D)
            assert at[0] <= BATCH * NCH * D

            tok_bank, t_bank, proj_bank = banks[0:2], banks[2], banks[3:5]
            core_bank, num_bank, out_bank = banks[5], banks[6], banks[7]

            tok_loaded, proj_loaded, moe_loaded = sema("tok_loaded"), sema("proj_loaded"), sema("moe_loaded")
            small_loaded, pos_loaded, ids_loaded = sema("small_loaded"), sema("pos_loaded"), sema("ids_loaded")
            txt_gathered, txt_placed = sema("txt_gathered"), sema("txt_placed")
            ident_set, consts_set, base_set, ids_set = sema("ident_set"), sema("consts_set"), sema("base_set"), sema("ids_set")
            txt_masked, pads_set, cols_set = sema("txt_masked"), sema("pads_set"), sema("cols_set")
            tok_split, proj_split, moe_split = sema("tok_split"), sema("proj_split"), sema("moe_split")
            beta_mm, beta_set = sema("beta_mm"), sema("beta_set")
            pix_loaded, pix_hi, pix_lo = sema("pix_loaded"), sema("pix_hi"), sema("pix_lo")
            patch_done, patch_added = sema("patch_done"), sema("patch_added")
            ln1_stat, ln1_mv, ln1_rstd, xn_done = sema("ln1_stat"), sema("ln1_mv"), sema("ln1_rstd"), sema("xn_done")
            ln1_var = sema("ln1_var")
            h_biased = sema("h_biased")
            xt_done, xt_hi, xt_lo = sema("xt_done"), sema("xt_hi"), sema("xt_lo")
            proj_done, proj_out = sema("proj_done"), sema("proj_out")
            f_clamped, f_logged, f_summed, f_clipped, gate_done = (
                sema("f_clamped"), sema("f_logged"), sema("f_summed"), sema("f_clipped"), sema("gate_done"))
            qk_min, qk_exp, qk_elu, q_done, k_done = (
                sema("qk_min"), sema("qk_exp"), sema("qk_elu"), sema("q_done"), sema("k_done"))
            core_done, pk_done, state_done = sema("core_done"), sema("pk_done"), sema("state_done")
            num_done, num_out = sema("num_done"), sema("num_out")
            ln2_stat, ln2_mv, den_added, den_inv = sema("ln2_stat"), sema("ln2_mv"), sema("den_added"), sema("den_inv")
            ln2_chain, ln2_scale, y_done = sema("ln2_chain"), sema("ln2_scale"), sema("y_done")
            yt_done, yt_hi, yt_lo = sema("yt_done"), sema("yt_hi"), sema("yt_lo")
            out_done, h_done = sema("out_done"), sema("h_done")

            block = ctxa.enter_context(nc.Block())

            @block.sync
            def _(sp):
                def load_image(n):
                    need(sp, pix_lo, 3 * n)
                    sp.dma_start(xa[:, :], xblk[n, 0:KA, :]).then_inc(pix_loaded, 16)
                    sp.dma_start(xb[0:KB, :], xblk[n, KA:D, :]).then_inc(pix_loaded, 16)
                    sp.dma_start(xb[KB:128, 0:BLK * BLK - 1], xblk[n, KA:D, 1:BLK * BLK]).then_inc(pix_loaded, 16)

                load_image(0)
                sp.dma_start(raw_tok, wtok).then_inc(tok_loaded, 16)
                sp.dma_start(raw_proj, wproj).then_inc(proj_loaded, 16)
                sp.dma_start(raw_out, wout).then_inc(proj_loaded, 16)
                load_image(1)
                sp.dma_start(raw_r1, wr1).then_inc(moe_loaded, 16)
                sp.dma_start(raw_down, wdown).then_inc(moe_loaded, 16)
                sp.dma_start(raw_up, wup).then_inc(moe_loaded, 16)
                with sp.Fori(2, BATCH) as n:
                    load_image(n)

            @block.gpsimd
            def _(pool):
                pool.dma_start(idx[:, :], ids).then_inc(ids_loaded, 16)
                pool.memset(ident[:, :], 0.0).then_inc(ident_set, 1)
                pool.wait_ge(ident_set, 1)
                pool.affine_select(out=ident[:, :], in_=ident[:, :], compare_op=ALU.not_equal, fill=1.0,
                                   base=0, pattern=[[-1, 128]], channel_multiplier=1).then_inc(ident_set, 1)
                for i in range(2):
                    for buf in (pa_h[i], pa_l[i]):
                        pool.memset(buf[:, :, 0:1], 0.0).then_inc(pads_set, 1)
                        pool.memset(buf[:, :, 1 + BLK * GRID:XW], 0.0).then_inc(pads_set, 1)
                    for buf in (pb_h[i], pb_l[i]):
                        pool.memset(buf[:, 0:1], 0.0).then_inc(pads_set, 1)
                        pool.memset(buf[:, 1 + BLK * GRID:XW], 0.0).then_inc(pads_set, 1)
                    for buf in (y_h[i], y_l[i], y_s[i]):
                        pool.memset(buf[:, 2 * CH:256], 0.0).then_inc(pads_set, 1)
                    pool.memset(v[i][:, :, D:D + 1], 1.0).then_inc(pads_set, 1)
                for buf in (x_h, x_l, x_s):
                    pool.memset(buf[:, L:L + 2], 0.0).then_inc(pads_set, 1)
                pool.memset(patch_rows[:, :], 1.0 / WS).then_inc(consts_set, 1)
                pool.memset(causal[:, :], 1.0).then_inc(consts_set, 1)
                pool.memset(minus_half[:, :], -0.5).then_inc(consts_set, 1)
                pool.memset(epsilon[:, :], 1e-5).then_inc(consts_set, 1)
                pool.memset(gate_sign[:, :], 1.0).then_inc(consts_set, 1)
                pool.memset(beta_cols[:, :, :], 0.0).then_inc(consts_set, 1)
                pool.wait_ge(consts_set, 6)
                pool.affine_select(out=patch_rows[:, 0:1], in_=patch_rows[:, 0:1], compare_op=ALU.is_ge, fill=0.0,
                                   base=-1, pattern=[[0, 1]], channel_multiplier=1).then_inc(consts_set, 1)
                pool.affine_select(out=patch_rows[:, 5:6], in_=patch_rows[:, 5:6], compare_op=ALU.is_ge, fill=0.0,
                                   base=CH - TXT - 1, pattern=[[0, 1]], channel_multiplier=-1).then_inc(consts_set, 1)
                pool.affine_select(out=gate_sign[:, :], in_=gate_sign[:, :], compare_op=ALU.is_ge, fill=-1.0,
                                   base=-M_DIM, pattern=[[0, 1]], channel_multiplier=1).then_inc(consts_set, 1)
                pool.affine_select(out=causal[:, 0:CH], in_=causal[:, 0:CH], compare_op=ALU.is_ge, fill=0.0,
                                   base=0, pattern=[[1, CH]], channel_multiplier=-1).then_inc(consts_set, 1)

                def split_pixels_lo(n, p, k):
                    pool.wait_ge(pix_hi, 3 * n + k + 1)
                    if k < 2:
                        src = xa[:, :].rearrange("p (r c) -> p r c", c=BLK)[:, :, k:k + GRID]
                        hi, lo = pa_h[p][:, k, 1:1 + BLK * GRID], pa_l[p][:, k, 1:1 + BLK * GRID]
                    else:
                        src = xb[:, :].rearrange("p (r c) -> p r c", c=BLK)[:, :, 0:GRID]
                        hi, lo = pb_h[p][:, 1:1 + BLK * GRID], pb_l[p][:, 1:1 + BLK * GRID]
                    hi, lo = hi.rearrange("p (r c) -> p r c", c=GRID), lo.rearrange("p (r c) -> p r c", c=GRID)
                    pool.tensor_tensor(lo, src, hi, ALU.subtract).then_inc(pix_lo, 1)

                for k in range(3):
                    split_pixels_lo(0, 0, k)
                pool.wait_ge(pos_loaded, 64)
                pool.wait_ge(small_loaded, 32)
                pool.tensor_tensor(base[0:CH, 0, :], base[0:CH, 0, :], badd0[:, :], ALU.add).then_inc(base_set, 1)
                pool.tensor_tensor(base[0:CH, 1:5, :], base[0:CH, 1:5, :],
                                   tok_b.unsqueeze(1).broadcast_to([CH, 4, D]), ALU.add).then_inc(base_set, 1)
                pool.tensor_tensor(pos5[0:95, :], pos5[0:95, :], tok_b[0:95, :], ALU.add).then_inc(base_set, 1)
                pool.wait_ge(base_set, 3)
                pool.tensor_copy(base[0:95, 5:5 + BATCH, :],
                                 pos5[0:95, :].unsqueeze(1).broadcast_to([95, BATCH, D])).then_inc(base_set, 1)
                pool.wait_ge(ids_set, 5)
                for g in range(4):
                    pool.indirect_dma_start(out=txt[:, g, :], out_offset=None, in_=table,
                                            in_offset=bass.IndirectOffsetOnAxis(ap=idx_c[:, g:g + 1], axis=0),
                                            bounds_check=VOCAB - 1, oob_is_err=False).then_inc(txt_gathered, 16)
                pool.wait_ge(txt_masked, 4)
                for b in range(BATCH):
                    q = TXT * (b % 4)
                    pool.dma_start(base[CH - TXT:CH, 5 + b, :], txt[q:q + TXT, b // 4, :]).then_inc(txt_placed, 16)
                for k in range(3):
                    split_pixels_lo(1, 1, k)

                def rsqrt1(n, q):
                    pool.wait_ge(ln1_mv, 6 * n + 2 * q + 2)
                    need(pool, xn_done, 6 * n)
                    s = slice(2 * q, 2 * q + 2)
                    pool.tensor_tensor(var1[:, s], mv1[:, s, 1], epsilon[:, s], ALU.add).then_inc(ln1_var, 1)
                    pool.wait_ge(ln1_var, 3 * n + q + 1)
                    pool.tensor_tensor(rstd1[:, s], var1[:, s], minus_half[:, s], ALU.pow).then_inc(ln1_rstd, 1)

                def bias_h(n, q):
                    pool.wait_ge(xn_done, 6 * n + 2 * q + 2)
                    c = 6 * n + 2 * q
                    pool.tensor_tensor(H[0:CH, bass.ds(c, 2), :], H[0:CH, bass.ds(c, 2), :],
                                       beta_out[:, :].unsqueeze(1).broadcast_to([CH, 2, D]), ALU.add)\
                        .then_inc(h_biased, 1)

                def scale2(n, q):
                    s = slice(2 * q, 2 * q + 2)
                    m = 3 * n + q
                    pool.wait_ge(ln2_mv, 2 * m + 2)
                    need(pool, ln2_scale, 3 * n)
                    pool.wait_ge(den_inv, m + 1)
                    pool.tensor_tensor(vn[:, s], mv2[:, s, 1], rden[:, s], ALU.mult).then_inc(ln2_chain, 1)
                    pool.wait_ge(ln2_chain, 4 * m + 1)
                    pool.tensor_tensor(hs[:, s], vn[:, s], rden[:, s], ALU.mult).then_inc(ln2_chain, 1)
                    pool.wait_ge(ln2_chain, 4 * m + 2)
                    pool.tensor_tensor(vn[:, s], hs[:, s], epsilon[:, s], ALU.add).then_inc(ln2_chain, 1)
                    pool.wait_ge(ln2_chain, 4 * m + 3)
                    pool.tensor_tensor(hs[:, s], vn[:, s], minus_half[:, s], ALU.pow).then_inc(ln2_chain, 1)
                    pool.wait_ge(ln2_chain, 4 * m + 4)
                    need(pool, y_done, 6 * n)
                    pool.tensor_tensor(hscale[:, s], hs[:, s], rden[:, s], ALU.mult).then_inc(ln2_scale, 1)

                def mixed(n, p, front, back, pixels):
                    lo = (lambda k: split_pixels_lo(n + 2, p, k)) if pixels else (lambda k: None)
                    if front:
                        rsqrt1(n + 1, 0)
                    lo(0)
                    if front:
                        bias_h(n + 1, 0)
                        rsqrt1(n + 1, 1)
                    if back:
                        scale2(n, 0)
                    lo(1)
                    if front:
                        bias_h(n + 1, 1)
                        rsqrt1(n + 1, 2)
                    if back:
                        scale2(n, 1)
                    if front:
                        bias_h(n + 1, 2)
                    lo(2)
                    if back:
                        scale2(n, 2)

                pool.wait_ge(beta_set, 1)
                pool.wait_ge(consts_set, 10)
                mixed(-1, 1, True, False, False)
                mixed(0, 0, True, True, True)
                mixed(1, 1, True, True, True)
                with pool.Fori(1, BATCH // 2 - 1) as pair_of:
                    n = pair_of * 2
                    mixed(n, 0, True, True, True)
                    mixed(n + 1, 1, True, True, True)
                mixed(BATCH - 2, 0, True, True, False)
                mixed(BATCH - 1, 1, False, True, False)

            @block.scalar
            def _(act):
                act.dma_start(rowv[:, :], rows.partition_broadcast(CH)).then_inc(small_loaded, 16)
                act.dma_start(colv[:, :], cols).then_inc(small_loaded, 16)
                act.dma_start(badd0[0:1, :], cls).then_inc(pos_loaded, 16)
                act.dma_start(badd0[1:CH, :], rows[0:D].partition_broadcast(CH - 1)).then_inc(pos_loaded, 16)
                act.dma_start(base[0:CH, 0:5, :], pos[0:5 * CH, :].rearrange("(c p) d -> p c d", p=CH)).then_inc(pos_loaded, 16)
                act.dma_start(pos5[0:95, :], pos[5 * CH:TOK_IMG, :]).then_inc(pos_loaded, 16)
                act.dma_start(r2[:, :], wr2).then_inc(moe_loaded, 16)

                def split_pixels_hi(n, p, k):
                    pix_src = (xa if k < 2 else xb)[:, :]
                    dx = k if k < 2 else 0
                    dst = pa_h[p][:, k, 1:1 + BLK * GRID] if k < 2 else pb_h[p][:, 1:1 + BLK * GRID]
                    if k == 0:
                        act.wait_ge(pix_loaded, 48 * n + 48)
                        need(act, patch_done, 6 * (n - 1))
                    act.activation(dst.rearrange("p (r c) -> p r c", c=GRID),
                                   pix_src.rearrange("p (r c) -> p r c", c=BLK)[:, :, dx:dx + GRID],
                                   ACT.Copy).then_inc(pix_hi, 1)

                for k in range(3):
                    split_pixels_hi(0, 0, k)
                act.wait_ge(tok_loaded, 16)
                act.activation(wt_h[:, :, :], raw_tok, ACT.Copy, scale=WS).then_inc(tok_split, 1)
                act.wait_ge(proj_loaded, 32)
                act.activation(wp_h[:, :, :], raw_proj, ACT.Copy, scale=WS).then_inc(proj_split, 1)
                act.wait_ge(cols_set, 1)
                for k in range(2):
                    act.activation(wo_h[:, k, :], raw_out[:, k, :], ACT.Copy, scale=colv[:, 1 + k:2 + k])\
                        .then_inc(proj_split, 1)
                for k in range(3):
                    split_pixels_hi(1, 1, k)
                def x_high(n, q):
                    act.wait_ge(xt_done, 3 * n + q + 1)
                    need(act, proj_done, 7 * n)
                    c = 2 * CH * q
                    act.activation(x_h[:, c:c + 2 * CH], t_bank[:, 0:2 * CH], ACT.Copy).then_inc(xt_hi, 1)
                    act.activation(x_s[0:KB, c:c + 2 * CH], t_bank[0:KB, 2 * CH:4 * CH], ACT.Copy).then_inc(xt_hi, 1)

                def y_high(n, p, q):
                    m = 3 * n + q
                    i = (3 * p + q) % 2
                    act.wait_ge(yt_done, m + 1)
                    need(act, out_done, m - 1)
                    act.activation(y_h[i][:, 0:2 * CH], t_bank[:, 0:2 * CH], ACT.Copy).then_inc(yt_hi, 1)
                    act.activation(y_s[i][0:KB, 0:2 * CH], t_bank[0:KB, 2 * CH:4 * CH], ACT.Copy).then_inc(yt_hi, 1)

                def num_copy(n, q):
                    act.wait_ge(num_done, 6 * n + 2 * q + 2)
                    need(act, y_done, 2 * (3 * n + q))
                    act.activation(num[:, :, :], num_bank[0:CH, 0:2 * (D + 1)].rearrange("p (c d) -> p c d", c=2),
                                   ACT.Copy).then_inc(num_out, 1)

                def proj_wait(n, j):
                    act.wait_ge(proj_done, 7 * n + j + 1)

                def take_qk_f(n, p):
                    for half in range(2):
                        s = slice(HALF * half, HALF * half + HALF)
                        proj_wait(n, 2 * half)
                        if half == 0:
                            need(act, qk_elu, n)
                        act.activation(qk[:, s], proj_bank[(7 * p + 2 * half) % 2][:, 0:HALF], ACT.Copy,
                                       scale=1.0 / WS).then_inc(proj_out, 1)
                        proj_wait(n, 2 * half + 1)
                        if half == 0:
                            need(act, q_done, n)
                            need(act, k_done, n)
                        act.activation(gate[:, s], proj_bank[(7 * p + 2 * half + 1) % 2][:, 0:HALF], ACT.Exp,
                                       bias=forget_bias, scale=-1.0 / WS).then_inc(proj_out, 1)

                def take_v(n, p, q):
                    proj_wait(n, 4 + q)
                    if q == 0:
                        need(act, num_done, 6 * (n - 1))
                    act.activation(v[p][:, 2 * q:2 * q + 2, 0:D],
                                   proj_bank[(7 * p + 4 + q) % 2][0:CH, 0:2 * D].rearrange("p (c d) -> p c d", c=2),
                                   ACT.Copy, scale=1.0 / WS).then_inc(proj_out, 1)

                def log_forget(n):
                    act.wait_ge(f_clamped, n + 1)
                    act.activation(gate[:, :], gate[:, :], ACT.Ln, bias=1.0).then_inc(f_logged, 1)

                def exp_qk(n):
                    act.wait_ge(qk_min, n + 1)
                    act.activation(qk_e[:, :], qk_e[:, :], ACT.Exp).then_inc(qk_exp, 1)

                def gates(n):
                    act.wait_ge(f_clipped, n + 1)
                    act.activation(gate[:, :], cum[:, :], ACT.Exp, scale=gate_sign[:, 0:1]).then_inc(gate_done, 1)

                def mixed(n, p, front, back, pixels):
                    m, r = n + 1, 1 - p
                    if pixels:
                        split_pixels_hi(n + 2, p, 0)
                    if front:
                        x_high(m, 0)
                    if back:
                        num_copy(n, 0)
                    if pixels:
                        split_pixels_hi(n + 2, p, 1)
                    if back:
                        y_high(n, p, 0)
                    if front:
                        x_high(m, 1)
                    if back:
                        num_copy(n, 1)
                    if pixels:
                        split_pixels_hi(n + 2, p, 2)
                    if back:
                        y_high(n, p, 1)
                    if front:
                        x_high(m, 2)
                    if back:
                        num_copy(n, 2)
                    if front:
                        take_qk_f(m, r)
                        take_v(m, r, 0)
                        log_forget(m)
                        take_v(m, r, 1)
                        exp_qk(m)
                        take_v(m, r, 2)
                    if back:
                        y_high(n, p, 2)
                    if front:
                        gates(m)

                act.wait_ge(consts_set, 10)
                act.wait_ge(cols_set, 2)
                mixed(-1, 1, True, False, False)
                act.wait_ge(moe_loaded, 64)
                act.activation(r1_h[:, :, :], raw_r1, ACT.Copy, scale=WS).then_inc(moe_split, 1)
                act.activation(down_h[:, :, :], raw_down, ACT.Copy, scale=WS).then_inc(moe_split, 1)
                act.activation(up_h[:, :, :], raw_up, ACT.Copy, scale=WS).then_inc(moe_split, 1)
                mixed(0, 0, True, True, True)
                mixed(1, 1, True, True, True)
                with act.Fori(1, BATCH // 2 - 1) as pair_of:
                    n = pair_of * 2
                    mixed(n, 0, True, True, True)
                    mixed(n + 1, 1, True, True, True)
                mixed(BATCH - 2, 0, True, True, False)
                mixed(BATCH - 1, 1, False, True, False)

            @block.tensor
            def _(pe):
                def patch(n, p, c):
                    if c % 2 == 0:
                        pe.wait_ge(pix_lo, 3 * n + 3)
                    need(pe, patch_added, 6 * n + c - 1)
                    dst = tok_bank[c % 2][:, 0:D]
                    k = 0
                    for t in range(6):
                        dy = t // 2 if t < 4 else t - 4
                        a = CH * c + GRID * dy
                        if t < 4:
                            hi, lo = pa_h[p][:, t % 2, a:a + 128], pa_l[p][:, t % 2, a:a + 128]
                        else:
                            hi, lo = pb_h[p][:, a:a + 128], pb_l[p][:, a:a + 128]
                        for x, w in ((hi, wt_h), (hi, wt_l), (lo, wt_h)):
                            mm = pe.matmul(dst, x, w[:, t, :], start=(k == 0), stop=(k == 17))
                            k += 1
                    mm.then_inc(patch_done, 1)

                def turn_pair(src, dst_sem):
                    for c in range(2):
                        pe.transpose(t_bank[:, CH * c:CH * c + CH], src[:, c, 0:KA], ident[0:CH, 0:CH])
                    for c in range(2):
                        mm = pe.transpose(t_bank[0:KB, CH * (2 + c):CH * (3 + c)], src[:, c, KA:D], ident[0:CH, 0:CH])
                    mm.then_inc(dst_sem, 1)

                def turn_x(n, p, q):
                    pe.wait_ge(xn_done, 6 * n + 2 * q + 2)
                    need(pe, yt_lo, 2 * (3 * (n - 1) + q))
                    need(pe, xt_lo, 2 * (3 * n + q))
                    turn_pair(xn[(3 * p + q) % 2], xt_done)

                def turn_y(n, q):
                    pe.wait_ge(y_done, 6 * n + 2 * q + 2)
                    if not isinstance(n, int) or n < BATCH - 1:
                        pe.wait_ge(xt_lo, 2 * (3 * (n + 1) + q + 1))
                    need(pe, yt_lo, 2 * (3 * n + q))
                    turn_pair(y, yt_done)

                def proj_qk_f(n, p):
                    pe.wait_ge(xt_lo, 6 * n + 6)
                    for j in range(4):
                        need(pe, proj_out, 7 * n + j - 1)
                        mm_features(pe, proj_bank[(7 * p + j) % 2][:, 0:HALF], wp_h, wp_l, 128 * (j % 2),
                                    128 * (j % 2) + 128, x_h, x_l, x_s, HALF * (j // 2), HALF * (j // 2) + HALF)\
                            .then_inc(proj_done, 1)

                def proj_v(n, p):
                    for q in range(3):
                        pe.wait_ge(proj_out, 7 * n + 4 + q - 1)
                        for c in range(2):
                            mm = mm_tokens(pe, proj_bank[(7 * p + 4 + q) % 2][:, D * c:D * c + D], wp_h, wp_l,
                                           4 * M_DIM, NPROJ, x_h, x_l, x_s, CH * (2 * q + c))
                        mm.then_inc(proj_done, 1)

                def core(n, p, c):
                    if c == 0:
                        pe.wait_ge(q_done, n + 1)
                        pe.wait_ge(k_done, n + 1)
                    need(pe, pk_done, 6 * n + c)
                    need(pe, state_done, 5 * n + max(c - 1, 0))
                    if c > 0:
                        if c == 1:
                            pe.wait_ge(proj_out, 7 * n + 7)
                        pe.matmul(core_bank[0:M_DIM, 256:256 + D + 1], pk[(c - 1) % 2][:, CH:CH + M_DIM],
                                  v[p][:, c - 1, :], start=True, stop=True)
                    s = slice(CH * c, CH * c + CH)
                    pe.matmul(core_bank[0:CH, 0:CH], kT[p][:, s], qT[p][:, s], start=True, stop=True)
                    pe.transpose(core_bank[0:CH, CH:CH + M_DIM], kT[p][:, s], ident[0:M_DIM, 0:M_DIM])\
                        .then_inc(core_done, 1)

                def numer(n, p, c):
                    pe.wait_ge(pk_done, 6 * n + c + 1)
                    if c == 0:
                        pe.wait_ge(proj_out, 7 * n + 7)
                    if c % 2 == 0:
                        need(pe, num_out, 3 * n + c // 2)
                    dst = num_bank[0:CH, (D + 1) * (c % 2):(D + 1) * (c % 2 + 1)]
                    mm = pe.matmul(dst, pk[c % 2][:, 0:CH], v[p][:, c, :], start=True, stop=(c == 0))
                    if c > 0:
                        pe.wait_ge(state_done, 5 * n + c)
                        mm = pe.matmul(dst, qT[p][:, CH * c:CH * c + CH], state[c % 2][:, :], start=False, stop=True)
                    mm.then_inc(num_done, 1)

                def project_out(n, p, q):
                    m = 3 * n + q
                    i = (3 * p + q) % 2
                    pe.wait_ge(yt_lo, 2 * m + 2)
                    need(pe, h_done, m)
                    for c in range(2):
                        mm = mm_tokens(pe, out_bank[:, D * c:D * c + D], wo_h, wo_l, 0, D,
                                       y_h[i], y_l[i], y_s[i], CH * c)
                    mm.then_inc(out_done, 1)

                def mixed(n, p, front, back):
                    m, r = n + 1, 1 - p
                    if front:
                        patch(m, r, 0)
                        patch(m, r, 1)
                    if back:
                        core(n, p, 0)
                    if front:
                        patch(m, r, 2)
                    if back:
                        core(n, p, 1)
                        numer(n, p, 0)
                    if front:
                        turn_x(m, r, 0)
                        patch(m, r, 3)
                    if back:
                        core(n, p, 2)
                        numer(n, p, 1)
                    if front:
                        patch(m, r, 4)
                    if back:
                        core(n, p, 3)
                        turn_y(n, 0)
                        numer(n, p, 2)
                    if front:
                        turn_x(m, r, 1)
                        patch(m, r, 5)
                    if back:
                        core(n, p, 4)
                        numer(n, p, 3)
                        project_out(n, p, 0)
                        core(n, p, 5)
                        turn_y(n, 1)
                        numer(n, p, 4)
                    if front:
                        turn_x(m, r, 2)
                    if back:
                        numer(n, p, 5)
                        project_out(n, p, 1)
                    if front:
                        proj_qk_f(m, r)
                        proj_v(m, r)
                    if back:
                        turn_y(n, 2)
                        project_out(n, p, 2)

                pe.wait_ge(ident_set, 2)
                pe.wait_ge(cols_set, 4)
                pe.wait_ge(proj_loaded, 32)
                pe.matmul(out_bank[0:CH, 0:D], beta_cols[:, 0, :], raw_out[:, 0, :], start=True, stop=False)
                pe.matmul(out_bank[0:CH, 0:D], beta_cols[0:KB, 1, :], raw_out[0:KB, 1, :], start=False, stop=True)\
                    .then_inc(beta_mm, 1)
                pe.wait_ge(tok_split, 2)
                pe.wait_ge(proj_split, 6)
                pe.wait_ge(pads_set, 27)
                pe.wait_ge(beta_set, 1)
                mixed(-1, 1, True, False)
                mixed(0, 0, True, True)
                mixed(1, 1, True, True)
                with pe.Fori(1, BATCH // 2 - 1) as pair_of:
                    n = pair_of * 2
                    mixed(n, 0, True, True)
                    mixed(n + 1, 1, True, True)
                mixed(BATCH - 2, 0, True, True)
                mixed(BATCH - 1, 1, False, True)

            @block.vector
            def _(dve):
                dve.wait_ge(ids_loaded, 16)
                dve.tensor_scalar(idx_ok[:, :], idx[:, :], 0.0, None, ALU.is_ge).then_inc(ids_set, 1)
                dve.tensor_scalar(idx_hi[:, :], idx[:, :], float(VOCAB - 1), None, ALU.is_le).then_inc(ids_set, 1)
                dve.tensor_scalar(idx_c[:, :], idx[:, :], 0.0, float(VOCAB - 1), ALU.max, ALU.min).then_inc(ids_set, 1)
                dve.wait_ge(ids_set, 3)
                dve.tensor_tensor(idx_ok[:, :], idx_ok[:, :], idx_hi[:, :], ALU.mult).then_inc(ids_set, 2)
                dve.wait_ge(small_loaded, 32)
                dve.wait_ge(consts_set, 6)
                dve.tensor_scalar(colv[:, 1:3], colv[:, 1:3], WS, None, ALU.mult).then_inc(cols_set, 1)
                dve.tensor_scalar(colv[:, 0:1], colv[:, 0:1], -1.0, None, ALU.mult).then_inc(cols_set, 1)
                for k in range(2):
                    dve.tensor_scalar(beta_cols[:, k, :], beta_cols[:, k, :], colv[:, 3 + k:4 + k], None, ALU.add)\
                        .then_inc(cols_set, 1)
                dve.wait_ge(tok_split, 1)
                dve.scalar_tensor_tensor(out=wt_l[:, :, :].rearrange("p k n -> p (k n)"), in0=raw_tok.rearrange("p k n -> p (k n)"), scalar=WS, in1=wt_h[:, :, :].rearrange("p k n -> p (k n)"), op0=ALU.mult,
                                         op1=ALU.subtract).then_inc(tok_split, 1)
                dve.wait_ge(proj_split, 3)
                dve.scalar_tensor_tensor(out=wp_l[:, :, :], in0=raw_proj, scalar=WS, in1=wp_h[:, :, :], op0=ALU.mult,
                                         op1=ALU.subtract).then_inc(proj_split, 1)
                dve.wait_ge(cols_set, 1)
                for k in range(2):
                    dve.scalar_tensor_tensor(out=wo_l[:, k, :], in0=raw_out[:, k, :], scalar=colv[:, 1 + k:2 + k],
                                             in1=wo_h[:, k, :], op0=ALU.mult, op1=ALU.subtract)\
                        .then_inc(proj_split, 1)
                dve.wait_ge(beta_mm, 1)
                dve.tensor_copy(beta_out[:, :], out_bank[0:CH, 0:D]).then_inc(beta_set, 1)
                dve.wait_ge(txt_gathered, 64)
                dve.wait_ge(ids_set, 5)
                for g in range(4):
                    dve.tensor_scalar(txt[:, g, :], txt[:, g, :], idx_ok[:, g:g + 1], None, ALU.mult)\
                        .then_inc(txt_masked, 1)

                def patch_add(n, c):
                    dve.wait_ge(patch_done, 6 * n + c + 1)
                    dst = H[0:CH, bass.ds(6 * n + c, 1), :].rearrange("p c d -> p (c d)")
                    add = base[0:CH, c, :] if c < 5 else \
                        base[0:CH, bass.ds(n + 5, 1), :].rearrange("p c d -> p (c d)")
                    dve.scalar_tensor_tensor(out=dst, in0=tok_bank[c % 2][0:CH, 0:D], scalar=patch_rows[:, c:c + 1],
                                             in1=add, op0=ALU.mult, op1=ALU.add).then_inc(patch_added, 1)
                    dve.wait_ge(patch_added, 6 * n + c + 1)
                    need(dve, ln1_mv, 6 * n)
                    dve.nop(nofuse=True)
                    dve.bn_stats(stat1[:, c, :], dst).then_inc(ln1_stat, 1)
                    dve.wait_ge(ln1_stat, 6 * n + c + 1)
                    need(dve, ln1_rstd, 3 * n)
                    need(dve, xn_done, 6 * n)
                    dve.nop(nofuse=True)
                    dve.bn_aggr(mv1[:, c, :], stat1[:, c, :]).then_inc(ln1_mv, 1)

                def norm_x(n, p, q):
                    dve.wait_ge(ln1_rstd, 3 * n + q + 1)
                    need(dve, xt_done, 3 * n + q - 1)
                    for c in range(2 * q, 2 * q + 2):
                        src = H[0:CH, bass.ds(6 * n + c, 1), :].rearrange("p c d -> p (c d)")
                        dve.tensor_scalar(xn[(3 * p + q) % 2][:, c % 2, :], src, mv1[:, c, 0:1], rstd1[:, c:c + 1],
                                          ALU.subtract, ALU.mult).then_inc(xn_done, 1)

                def x_low(n, q):
                    dve.wait_ge(xt_hi, 2 * (3 * n + q) + 2)
                    c = 2 * CH * q
                    dve.tensor_tensor(x_l[:, c:c + 2 * CH], t_bank[:, 0:2 * CH], x_h[:, c:c + 2 * CH],
                                      ALU.subtract).then_inc(xt_lo, 1)
                    dve.tensor_tensor(x_s[KB:128, c:c + 2 * CH], t_bank[0:KB, 2 * CH:4 * CH],
                                      x_s[0:KB, c:c + 2 * CH], ALU.subtract).then_inc(xt_lo, 1)

                def y_low(n, p, q):
                    i = (3 * p + q) % 2
                    dve.wait_ge(yt_hi, 2 * (3 * n + q) + 2)
                    dve.tensor_tensor(y_l[i][:, 0:2 * CH], t_bank[:, 0:2 * CH], y_h[i][:, 0:2 * CH],
                                      ALU.subtract).then_inc(yt_lo, 1)
                    dve.tensor_tensor(y_s[i][KB:128, 0:2 * CH], t_bank[0:KB, 2 * CH:4 * CH],
                                      y_s[i][0:KB, 0:2 * CH], ALU.subtract).then_inc(yt_lo, 1)

                def take_core(n, c):
                    dve.wait_ge(core_done, 6 * n + c + 1)
                    need(dve, num_done, 6 * n + c - 1)
                    dve.tensor_tensor(pk[c % 2][:, :], core_bank[0:CH, 0:CH + M_DIM], causal[:, :],
                                      ALU.mult).then_inc(pk_done, 1)
                    if c == 1:
                        dve.tensor_copy(state[1][:, :], core_bank[0:M_DIM, 256:256 + D + 1]).then_inc(state_done, 1)
                    if c > 1:
                        dve.wait_ge(state_done, 5 * n + c - 1)
                        dve.tensor_tensor(state[c % 2][:, :], core_bank[0:M_DIM, 256:256 + D + 1],
                                          state[(c - 1) % 2][:, :], ALU.add).then_inc(state_done, 1)

                def num_stats(n, q):
                    m = 3 * n + q
                    s = slice(2 * q, 2 * q + 2)
                    dve.wait_ge(num_out, m + 1)
                    need(dve, ln2_scale, 3 * n)
                    need(dve, y_done, 6 * n)
                    dve.tensor_scalar(den[:, s], num[:, :, D], 1e-6, None, ALU.add).then_inc(den_added, 1)
                    dve.nop(nofuse=True)
                    for c in range(2):
                        dve.bn_stats(stat2[:, 2 * q + c, :], num[:, c, 0:D]).then_inc(ln2_stat, 1)
                    dve.wait_ge(den_added, m + 1)
                    dve.reciprocal(rden[:, s], den[:, s]).then_inc(den_inv, 1)
                    for c in range(2):
                        dve.wait_ge(ln2_stat, 2 * m + c + 1)
                        dve.nop(nofuse=True)
                        dve.bn_aggr(mv2[:, 2 * q + c, :], stat2[:, 2 * q + c, :]).then_inc(ln2_mv, 1)

                def norm_y(n, q):
                    m = 3 * n + q
                    dve.wait_ge(ln2_scale, m + 1)
                    need(dve, yt_done, m)
                    for c in range(2):
                        dve.tensor_scalar(y[:, c, :], num[:, c, 0:D], mv2[:, 2 * q + c, 0:1],
                                          hscale[:, 2 * q + c:2 * q + c + 1], ALU.subtract, ALU.mult)\
                            .then_inc(y_done, 1)

                def add_out(n, q):
                    dve.wait_ge(out_done, 3 * n + q + 1)
                    dve.wait_ge(h_biased, 3 * n + q + 1)
                    dst = H[0:CH, bass.ds(6 * n + 2 * q, 2), :].rearrange("p c d -> p (c d)")
                    dve.scalar_tensor_tensor(out=dst, in0=out_bank[0:CH, 0:2 * D], scalar=1.0 / WS, in1=dst,
                                             op0=ALU.mult, op1=ALU.add).then_inc(h_done, 1)

                def clamp_and_min(n):
                    dve.wait_ge(proj_out, 7 * n + 4)
                    dve.tensor_scalar(gate[:, :], gate[:, :], PROB_CLAMP, None, ALU.min).then_inc(f_clamped, 1)
                    need(dve, q_done, n)
                    need(dve, k_done, n)
                    dve.tensor_scalar(qk_e[:, :], qk[:, :], 0.0, None, ALU.min).then_inc(qk_min, 1)

                def scan(n):
                    dve.wait_ge(f_logged, n + 1)
                    need(dve, gate_done, n)
                    dve.tensor_tensor_scan(cum[:, :], gate[:, :], gate[:, :], 0.0, ALU.add, ALU.max)\
                        .then_inc(f_summed, 1)
                    dve.wait_ge(f_summed, n + 1)
                    dve.tensor_scalar(cum[:, :], cum[:, :], 20.0, -20.0, ALU.min, ALU.max).then_inc(f_clipped, 1)

                def elu(n):
                    dve.wait_ge(qk_exp, n + 1)
                    dve.scalar_tensor_tensor(out=qk_e[:, :], in0=qk[:, :], scalar=0.0, in1=qk_e[:, :], op0=ALU.max,
                                             op1=ALU.add).then_inc(qk_elu, 1)

                def gate_qk(n, p):
                    dve.wait_ge(gate_done, n + 1)
                    dve.wait_ge(qk_elu, n + 1)
                    need(dve, num_done, 6 * (n - 1))
                    dve.scalar_tensor_tensor(out=qT[p][:, :], in0=qk_e[0:64, :], scalar=M_DIM ** -0.5,
                                             in1=gate[0:64, :], op0=ALU.mult, op1=ALU.mult).then_inc(q_done, 1)
                    dve.tensor_tensor(kT[p][:, :], qk_e[64:128, :], gate[64:128, :], ALU.mult).then_inc(k_done, 1)

                def mixed(n, p, front, back):
                    m, r = n + 1, 1 - p
                    if front:
                        patch_add(m, 0)
                        patch_add(m, 1)
                    if back:
                        take_core(n, 0)
                    if front:
                        norm_x(m, r, 0)
                        patch_add(m, 2)
                    if back:
                        take_core(n, 1)
                    if front:
                        x_low(m, 0)
                        patch_add(m, 3)
                        norm_x(m, r, 1)
                    if back:
                        take_core(n, 2)
                        num_stats(n, 0)
                    if front:
                        patch_add(m, 4)
                    if back:
                        norm_y(n, 0)
                        take_core(n, 3)
                        y_low(n, p, 0)
                    if front:
                        x_low(m, 1)
                        patch_add(m, 5)
                    if back:
                        take_core(n, 4)
                        num_stats(n, 1)
                    if front:
                        norm_x(m, r, 2)
                    if back:
                        add_out(n, 0)
                        take_core(n, 5)
                        norm_y(n, 1)
                    if back:
                        y_low(n, p, 1)
                    if front:
                        x_low(m, 2)
                    if back:
                        num_stats(n, 2)
                        add_out(n, 1)
                    if front:
                        clamp_and_min(m)
                    if back:
                        norm_y(n, 2)
                    if front:
                        scan(m)
                    if back:
                        y_low(n, p, 2)
                    if front:
                        elu(m)
                        gate_qk(m, r)
                    if back:
                        add_out(n, 2)

                dve.wait_ge(base_set, 4)
                dve.wait_ge(txt_placed, 16 * BATCH)
                dve.wait_ge(consts_set, 10)
                mixed(-1, 1, True, False)
                dve.wait_ge(moe_split, 3)
                dve.scalar_tensor_tensor(out=r1_l[:, :, :], in0=raw_r1, scalar=WS, in1=r1_h[:, :, :],
                                         op0=ALU.mult, op1=ALU.subtract).then_inc(moe_split, 1)
                dve.scalar_tensor_tensor(out=down_l[:, :, :], in0=raw_down, scalar=WS, in1=down_h[:, :, :],
                                         op0=ALU.mult, op1=ALU.subtract).then_inc(moe_split, 1)
                dve.scalar_tensor_tensor(out=up_l[:, :, :].rearrange("p k n -> p (k n)"), in0=raw_up.rearrange("p k n -> p (k n)"), scalar=WS, in1=up_h[:, :, :].rearrange("p k n -> p (k n)"),
                                         op0=ALU.mult, op1=ALU.subtract).then_inc(moe_split, 1)
                mixed(0, 0, True, True)
                mixed(1, 1, True, True)
                with dve.Fori(1, BATCH // 2 - 1) as pair_of:
                    n = pair_of * 2
                    mixed(n, 0, True, True)
                    mixed(n + 1, 1, True, True)
                mixed(BATCH - 2, 0, True, True)
                mixed(BATCH - 1, 1, False, True)
                dve.wait_ge(moe_split, 6)
                dve.wait_ge(h_done, 3 * BATCH)

        ctxb = ExitStack()
        with ctxb:
            def sa(name, shape, dt=fp32):
                return sb(name, shape, dt, ctxb)

            def sema(name):
                return sem(name, ctxb)

            gx_h = [sa(f"gx_h{i}", [128, GT], fp16) for i in range(2)]
            gx_l = [sa(f"gx_l{i}", [128, GT], fp16) for i in range(2)]
            gx_s = [sa(f"gx_s{i}", [128, GT], fp16) for i in range(2)]
            z32 = [sa(f"z32_{i}", [128, GT]) for i in range(Z_BANKS)]
            z_h = [sa(f"z_h{i}", [128, 2, 512], fp16) for i in range(Z_RING)]
            z_l = [sa(f"z_l{i}", [128, 2, 512], fp16) for i in range(Z_RING)]
            x2 = [sa(f"x2_{i}", [CH, GCH, D]) for i in range(2)]
            acc = [sa(f"acc{i}", [CH, GCH, D]) for i in range(2)]
            hb = sa("hb", [CH, GCH, D])
            res = [sa(f"res{i}", [CH, GCH, D]) for i in range(2)]
            bstat = sa("bstat", [CH, GCH, 6])
            bmv = sa("bmv", [CH, GCH, 2])
            brstd = sa("brstd", [CH, GCH])
            bvar = sa("bvar", [CH, GCH])
            cstat = sa("cstat", [CH, GCH, 6])
            cmv = sa("cmv", [CH, GCH, 2])
            crstd = sa("crstd", [CH, GCH])
            cvar = sa("cvar", [CH, GCH])
            rg = sa("rg", [H1, GT])
            logit = sa("logit", [CH, GCH, NE])
            lmax = sa("lmax", [CH, GCH])
            shifted = sa("shifted", [CH, GCH, NE])
            euler = sa("euler", [CH, GCH, NE])
            expo = sa("expo", [CH, GCH, NE])
            esum = sa("esum", [CH, GCH])
            einv = sa("einv", [CH, GCH])
            prob = sa("prob", [CH, GCH, NE])
            top = sa("top", [CH, GCH, 8])
            above = sa("above", [CH, GCH, NE])
            equal = sa("equal", [CH, GCH, NE])
            resets = sa("resets", [CH, GCH, NE])
            rank = sa("rank", [CH, GCH, NE])
            first_above = sa("first_above", [CH, GCH])
            rank2 = sa("rank2", [CH, GCH, NE])
            taken = sa("taken", [CH, GCH, NE])
            picked = sa("picked", [CH, GCH, NE])
            weighted = sa("weighted", [CH, GCH, NE])
            tsum = sa("tsum", [CH, GCH])
            tscaled = sa("tscaled", [CH, GCH])
            tinv = sa("tinv", [CH, GCH])
            share = [sa(f"share{i}", [CH, GCH, NE]) for i in range(2)]

            z_bank, up_bank, turn_bank, route_bank = banks[0:4], banks[4:6], banks[6], banks[7]

            b_var, c_var = sema("b_var"), sema("c_var")
            b_consts = sema("b_consts")
            b_stat, b_mv, b_rstd, x2_done = sema("b_stat"), sema("b_mv"), sema("b_rstd"), sema("x2_done")
            gx_done, gx_hi, gx_lo = sema("gx_done"), sema("gx_hi"), sema("gx_lo")
            route1_done, route_gelu, route2_done = sema("route1_done"), sema("route_gelu"), sema("route2_done")
            logit_done, lmax_done, shift_done, expo_done = (
                sema("logit_done"), sema("lmax_done"), sema("shift_done"), sema("expo_done"))
            esum_done, einv_done, prob_done, top_done = (
                sema("esum_done"), sema("einv_done"), sema("prob_done"), sema("top_done"))
            tsum_done, weighted_done = sema("tsum_done"), sema("weighted_done")
            above_done, equal_done, rank2_done = sema("above_done"), sema("equal_done"), sema("rank2_done")
            taken_done, picked_done, tscaled_done = sema("taken_done"), sema("picked_done"), sema("tscaled_done")
            rank_done, tinv_done, share_done = sema("rank_done"), sema("tinv_done"), sema("share_done")
            z_done, z32_done, zh_done, zl_done = sema("z_done"), sema("z32_done"), sema("zh_done"), sema("zl_done")
            up_done, acc_done = sema("up_done"), sema("acc_done")
            c_stat, c_mv, c_rstd, normed = sema("c_stat"), sema("c_mv"), sema("c_rstd"), sema("normed")
            hb_done, scaled, res_done, stored = sema("hb_done"), sema("scaled"), sema("res_done"), [sema("stored_even"), sema("stored_odd")]
            block = ctxb.enter_context(nc.Block())

            @block.sync
            def _(sp):
                def store(g, p):
                    sp.wait_ge(res_done, g + 1)
                    dst = out[bass.ds(g * GT, GT), :].rearrange("(c p) d -> p c d", p=CH)
                    sp.dma_start(dst[0:112], res[p][0:112]).then_inc(stored[p], 16)
                    sp.dma_start(dst[112:CH], res[p][112:CH]).then_inc(stored[p], 16)

                with sp.Fori(0, NG // 2) as pair_of:
                    g = pair_of * 2
                    store(g, 0)
                    store(g + 1, 1)
                for p in range(2):
                    sp.wait_ge(stored[p], 16 * NG)

            @block.gpsimd
            def _(pool):
                for i in range(Z_RING):
                    for buf in (z_h[i], z_l[i]):
                        pool.memset(buf[:, :, GT:512], 0.0).then_inc(b_consts, 1)
                pool.memset(euler[:, :, :], 2.718281828459045).then_inc(b_consts, 1)
                pool.memset(resets[:, :, :], 1.0).then_inc(b_consts, 1)
                pool.wait_ge(b_consts, 10)
                pool.memset(resets[:, :, 0:1], 0.0).then_inc(b_consts, 1)

                def rsqrt_b(g):
                    pool.wait_ge(b_mv, 4 * g + 4)
                    need(pool, x2_done, 4 * g)
                    pool.tensor_tensor(bvar[:, :], bmv[:, :, 1], epsilon[:, 0:GCH], ALU.add).then_inc(b_var, 1)
                    pool.wait_ge(b_var, g + 1)
                    pool.tensor_tensor(brstd[:, :], bvar[:, :], minus_half[:, 0:GCH], ALU.pow).then_inc(b_rstd, 1)

                def rsqrt_c(g):
                    pool.wait_ge(c_mv, 4 * g + 4)
                    need(pool, normed, 4 * g)
                    pool.tensor_tensor(cvar[:, :], cmv[:, :, 1], epsilon[:, 0:GCH], ALU.add).then_inc(c_var, 1)
                    pool.wait_ge(c_var, g + 1)
                    pool.tensor_tensor(crstd[:, :], cvar[:, :], minus_half[:, 0:GCH], ALU.pow).then_inc(c_rstd, 1)

                def wide(a):
                    return a.unsqueeze(2).broadcast_to([CH, GCH, NE])

                def softmax_exp(g):
                    pool.wait_ge(lmax_done, g + 1)
                    need(pool, expo_done, g)
                    pool.tensor_tensor(shifted[:, :, :], logit[:, :, :], wide(lmax[:, :]), ALU.subtract)\
                        .then_inc(shift_done, 1)
                    pool.wait_ge(shift_done, g + 1)
                    need(pool, prob_done, g)
                    pool.tensor_tensor(expo[:, :, :], euler[:, :, :], shifted[:, :, :], ALU.pow).then_inc(expo_done, 1)

                def probabilities(g):
                    pool.wait_ge(einv_done, g + 1)
                    need(pool, share_done, g)
                    pool.tensor_tensor(prob[:, :, :], expo[:, :, :], wide(einv[:, :]), ALU.mult).then_inc(prob_done, 1)

                def choose(g, p):
                    pool.wait_ge(picked_done, g + 1)
                    need(pool, share_done, g)
                    pool.tensor_tensor(weighted[:, :, :], picked[:, :, :], prob[:, :, :], ALU.mult)\
                        .then_inc(weighted_done, 1)
                    pool.wait_ge(weighted_done, g + 1)
                    pool.wait_ge(tinv_done, g + 1)
                    need(pool, acc_done, 32 * (g - 1))
                    pool.tensor_tensor(share[p][:, :, :], weighted[:, :, :], wide(tinv[:, :]), ALU.mult)\
                        .then_inc(share_done, 1)

                def add_beta(g):
                    need(pool, res_done, g)
                    pool.tensor_tensor(hb[:, :, :], H[0:CH, bass.ds(GCH * g, GCH), :],
                                       ffn_beta.unsqueeze(1).broadcast_to([CH, GCH, D]), ALU.add).then_inc(hb_done, 1)

                def finish(g, p):
                    pool.wait_ge(normed, 4 * g + 4)
                    pool.tensor_tensor(acc[p][:, :, :], acc[p][:, :, :],
                                       ffn_gamma.unsqueeze(1).broadcast_to([CH, GCH, D]), ALU.mult).then_inc(scaled, 1)
                    pool.wait_ge(scaled, g + 1)
                    pool.wait_ge(hb_done, g + 1)
                    need(pool, stored[p], 16 * (g - p))
                    pool.tensor_tensor(res[p][:, :, :], acc[p][:, :, :], hb[:, :, :], ALU.add).then_inc(res_done, 1)

                def group(g, p, prep, fin):
                    if prep:
                        rsqrt_b(g + 1)
                    if fin:
                        add_beta(g - 1)
                        rsqrt_c(g - 1)
                        finish(g - 1, 1 - p)
                    if prep:
                        softmax_exp(g + 1)
                        probabilities(g + 1)
                        choose(g + 1, 1 - p)

                group(-1, 1, True, False)
                group(0, 0, True, False)
                group(1, 1, True, True)
                group(2, 0, True, True)
                group(3, 1, True, True)
                with pool.Fori(2, NG // 2 - 1) as pair_of:
                    g = pair_of * 2
                    group(g, 0, True, True)
                    group(g + 1, 1, True, True)
                group(NG - 2, 0, True, True)
                group(NG - 1, 1, False, True)
                group(NG, 0, False, True)

            @block.scalar
            def _(act):
                def gx_high(g, p, part):
                    act.wait_ge(gx_done, 2 * g + part + 1)
                    need(act, z_done, 16 * (g - 1))
                    need(act, route1_done, g - 1)
                    dst, src = (gx_h[p][:, :], turn_bank[:, 0:GT]) if part == 0 else \
                        (gx_s[p][0:KB, :], turn_bank[0:KB, 0:GT])
                    act.activation(dst, src, ACT.Copy).then_inc(gx_hi, 1)

                def gelu_router(g):
                    act.wait_ge(route1_done, g + 1)
                    need(act, route2_done, g)
                    act.activation(rg[:, :], route_bank[0:H1, 0:GT], ACT.Gelu, bias=router_b1,
                                   scale=1.0 / WS).then_inc(route_gelu, 1)

                def gelu_hidden(g, e):
                    for t in range(2):
                        n = 16 * g + 2 * e + t
                        i = (2 * e + t) % Z_BANKS
                        act.wait_ge(z_done, n + 1)
                        need(act, zl_done, n + 1 - Z_BANKS)
                        bias = down_b[:, 2 * e + t:2 * e + t + 1]
                        act.activation(z32[i][:, :], z_bank[i][:, 0:GT], ACT.Gelu, bias=bias, scale=1.0 / WS)\
                            .then_inc(z32_done, 1)
                        if t == 0:
                            need(act, up_done, 2 * (8 * g + e + 1 - Z_RING))
                        act.activation(z_h[e % Z_RING][:, t, 0:GT], z_bank[i][:, 0:GT], ACT.Gelu, bias=bias,
                                       scale=1.0 / WS).then_inc(zh_done, 1)

                def group(g, p, own, prep):
                    for e in range(NE):
                        if e < 6:
                            if own:
                                gelu_hidden(g, e + 2)
                        elif prep:
                            gelu_hidden(g + 1, e - 6)
                        if prep:
                            if e == 1:
                                gx_high(g + 1, 1 - p, 0)
                            if e == 2:
                                gx_high(g + 1, 1 - p, 1)
                            if e == 3:
                                gelu_router(g + 1)

                group(-1, 1, False, True)
                group(0, 0, True, True)
                group(1, 1, True, True)
                with act.Fori(1, NG // 2 - 1) as pair_of:
                    g = pair_of * 2
                    group(g, 0, True, True)
                    group(g + 1, 1, True, True)
                group(NG - 2, 0, True, True)
                group(NG - 1, 1, True, False)

            @block.tensor
            def _(pe):
                def turn(g, p, part):
                    if part == 0:
                        pe.wait_ge(x2_done, 4 * g + 4)
                    need(pe, gx_lo, 2 * g + part)
                    pe.nop(nofuse=True)
                    rows_of = 128 if part == 0 else KB
                    for c in range(GCH):
                        src = x2[p][:, c, 0:KA] if part == 0 else x2[p][:, c, KA:D]
                        mm = pe.transpose(turn_bank[0:rows_of, CH * c:CH * c + CH], src, ident[0:CH, 0:CH])
                    mm.then_inc(gx_done, 1)

                def route1(g, p):
                    pe.wait_ge(gx_lo, 2 * g + 2)
                    need(pe, logit_done, g)
                    mm_features(pe, route_bank[0:H1, 0:GT], r1_h, r1_l, 0, H1, gx_h[p], gx_l[p], gx_s[p], 0, GT)\
                        .then_inc(route1_done, 1)

                def route2(g):
                    pe.wait_ge(route_gelu, g + 1)
                    for c in range(GCH):
                        mm = pe.matmul(route_bank[0:CH, NE * c:NE * c + NE], rg[:, CH * c:CH * c + CH], r2[:, :],
                                       start=True, stop=True)
                    mm.then_inc(route2_done, 1)

                def down(g, p, e):
                    if e == 0:
                        pe.wait_ge(gx_lo, 2 * g + 2)
                    for t in range(2):
                        n = 16 * g + 2 * e + t
                        need(pe, zh_done, n + 1 - Z_BANKS)
                        lo = 128 * (2 * e + t)
                        mm_features(pe, z_bank[(2 * e + t) % Z_BANKS][:, 0:GT], down_h, down_l, lo, lo + 128,
                                    gx_h[p], gx_l[p], gx_s[p], 0, GT).then_inc(z_done, 1)

                def up(g, e):
                    s = 8 * g + e
                    i = e % Z_RING
                    pe.wait_ge(zh_done, 2 * s + 2)
                    pe.wait_ge(zl_done, 2 * s + 2)
                    for half in range(2):
                        need(pe, acc_done, 4 * s - 2 + 2 * half)
                        for c in range(2):
                            a = CH * (2 * half + c)
                            k = 0
                            for t in range(2):
                                z1, z0 = z_h[i][:, t, a:a + 128], z_l[i][:, t, a:a + 128]
                                for z, w in ((z1, up_h), (z1, up_l), (z0, up_h)):
                                    mm = pe.matmul(up_bank[half][:, D * c:D * c + D], z, w[:, 2 * e + t, :],
                                                   start=(k == 0), stop=(k == 5))
                                    k += 1
                        mm.then_inc(up_done, 1)

                def group(g, p, own, prep):
                    q = 1 - p
                    for e in range(NE):
                        if e < 6:
                            if own:
                                down(g, p, e + 2)
                        elif prep:
                            down(g + 1, q, e - 6)
                        if prep:
                            if e == 1:
                                turn(g + 1, q, 0)
                            if e == 2:
                                turn(g + 1, q, 1)
                            if e == 3:
                                route1(g + 1, q)
                            if e == 4:
                                route2(g + 1)
                        if own:
                            up(g, e)

                pe.wait_ge(b_consts, 8)
                group(-1, 1, False, True)
                group(0, 0, True, True)
                group(1, 1, True, True)
                with pe.Fori(1, NG // 2 - 1) as pair_of:
                    g = pair_of * 2
                    group(g, 0, True, True)
                    group(g + 1, 1, True, True)
                group(NG - 2, 0, True, True)
                group(NG - 1, 1, True, False)

            @block.vector
            def _(dve):
                def h_chunk(g, c):
                    return H[0:CH, bass.ds(GCH * g + c, 1), :].rearrange("p c d -> p (c d)")

                def stats_b(g):
                    need(dve, b_rstd, g)
                    need(dve, x2_done, 4 * g)
                    need(dve, b_mv, 4 * g)
                    dve.nop(nofuse=True)
                    for c in range(GCH):
                        dve.bn_stats(bstat[:, c, :], h_chunk(g, c)).then_inc(b_stat, 1)
                    for c in range(GCH):
                        dve.wait_ge(b_stat, 4 * g + c + 1)
                        dve.nop(nofuse=True)
                        dve.bn_aggr(bmv[:, c, :], bstat[:, c, :]).then_inc(b_mv, 1)

                def norm_b(g, p):
                    dve.wait_ge(b_rstd, g + 1)
                    need(dve, gx_done, 2 * (g - 1))
                    need(dve, acc_done, 32 * (g - 2) + 4)
                    for c in range(GCH):
                        dve.tensor_scalar(x2[p][:, c, :], h_chunk(g, c), bmv[:, c, 0:1], brstd[:, c:c + 1],
                                          ALU.subtract, ALU.mult).then_inc(x2_done, 1)

                def gx_low(g, p, part):
                    dve.wait_ge(gx_hi, 2 * g + part + 1)
                    if part == 0:
                        dve.tensor_tensor(gx_l[p][:, :], turn_bank[:, 0:GT], gx_h[p][:, :], ALU.subtract)\
                            .then_inc(gx_lo, 1)
                    else:
                        dve.tensor_tensor(gx_s[p][KB:128, :], turn_bank[0:KB, 0:GT], gx_s[p][0:KB, :],
                                          ALU.subtract).then_inc(gx_lo, 1)

                def logits(g):
                    dve.wait_ge(route2_done, g + 1)
                    need(dve, shift_done, g)
                    dve.tensor_tensor(logit[:, :, :], route_bank[0:CH, 0:GCH * NE].rearrange("p (c e) -> p c e", e=NE),
                                      router_b2.unsqueeze(1).broadcast_to([CH, GCH, NE]), ALU.add).then_inc(logit_done, 1)
                    dve.wait_ge(logit_done, g + 1)
                    dve.tensor_reduce(lmax[:, :], logit[:, :, :], AX, ALU.max).then_inc(lmax_done, 1)

                def expo_sums(g):
                    dve.wait_ge(expo_done, g + 1)
                    need(dve, einv_done, g)
                    dve.tensor_reduce(esum[:, :], expo[:, :, :], AX, ALU.add).then_inc(esum_done, 1)
                    dve.wait_ge(esum_done, g + 1)
                    need(dve, prob_done, g)
                    dve.reciprocal(einv[:, :], esum[:, :]).then_inc(einv_done, 1)

                def tops(g):
                    dve.wait_ge(prob_done, g + 1)
                    need(dve, share_done, g)
                    dve.nop(nofuse=True)
                    for c in range(GCH):
                        dve.max(top[:, c, :], prob[:, c, :]).then_inc(top_done, 1)

                def compare(g):
                    dve.wait_ge(top_done, 4 * g + 4)
                    second = top[:, :, 1:2].broadcast_to([CH, GCH, NE])
                    dve.tensor_tensor(above[:, :, :], prob[:, :, :], second, ALU.is_gt).then_inc(above_done, 1)
                    dve.tensor_tensor(equal[:, :, :], prob[:, :, :], second, ALU.is_equal).then_inc(equal_done, 1)
                    dve.tensor_tensor(first_above[:, :], top[:, :, 0], top[:, :, 1], ALU.is_gt).then_inc(above_done, 1)
                    dve.tensor_tensor(tsum[:, :], top[:, :, 0], top[:, :, 1], ALU.add).then_inc(tsum_done, 1)

                def pick_two(g):
                    dve.wait_ge(equal_done, g + 1)
                    dve.tensor_tensor_scan(rank[:, :, :].rearrange("p c e -> p (c e)"),
                                           resets[:, :, :].rearrange("p c e -> p (c e)"),
                                           equal[:, :, :].rearrange("p c e -> p (c e)"),
                                           0.0, ALU.mult, ALU.add).then_inc(rank_done, 1)
                    dve.wait_ge(tsum_done, g + 1)
                    dve.tensor_scalar(tscaled[:, :], tsum[:, :], 1e-8, WS, ALU.add, ALU.mult).then_inc(tscaled_done, 1)
                    dve.wait_ge(rank_done, g + 1)
                    dve.wait_ge(above_done, 2 * g + 2)
                    dve.tensor_tensor(rank2[:, :, :], rank[:, :, :],
                                      first_above[:, :].unsqueeze(2).broadcast_to([CH, GCH, NE]), ALU.add)\
                        .then_inc(rank2_done, 1)
                    dve.wait_ge(tscaled_done, g + 1)
                    dve.reciprocal(tinv[:, :], tscaled[:, :]).then_inc(tinv_done, 1)
                    dve.wait_ge(rank2_done, g + 1)
                    dve.scalar_tensor_tensor(out=taken[:, :, :], in0=rank2[:, :, :], scalar=2.0, in1=equal[:, :, :],
                                             op0=ALU.is_le, op1=ALU.mult).then_inc(taken_done, 1)
                    dve.wait_ge(taken_done, g + 1)
                    dve.tensor_tensor(picked[:, :, :], taken[:, :, :], above[:, :, :], ALU.add).then_inc(picked_done, 1)

                def split_hidden(g, e):
                    for t in range(2):
                        n = 16 * g + 2 * e + t
                        dve.wait_ge(zh_done, n + 1)
                        if t == 0:
                            need(dve, up_done, 2 * (8 * g + e + 1 - Z_RING))
                        i = (2 * e + t) % Z_BANKS
                        dve.tensor_tensor(z_l[e % Z_RING][:, t, 0:GT], z32[i][:, :], z_h[e % Z_RING][:, t, 0:GT],
                                          ALU.subtract).then_inc(zl_done, 1)

                def accumulate(g, p, e):
                    s = 8 * g + e
                    if e == 0:
                        dve.wait_ge(share_done, g + 1)
                        need(dve, scaled, g - 1)
                        need(dve, res_done, g - 1)
                    for half in range(2):
                        dve.wait_ge(up_done, 2 * s + half + 1)
                        for c in range(2):
                            k = 2 * half + c
                            if e > 0:
                                dve.wait_ge(acc_done, 4 * s + k - 3)
                            dve.scalar_tensor_tensor(
                                out=acc[p][:, k, :], in0=up_bank[half][0:CH, D * c:D * c + D],
                                scalar=share[p][:, k, e:e + 1], in1=(x2 if e == 0 else acc)[p][:, k, :],
                                op0=ALU.mult, op1=ALU.add).then_inc(acc_done, 1)

                def stats_c(g, p):
                    need(dve, normed, 4 * g)
                    need(dve, c_mv, 4 * g)
                    dve.wait_ge(acc_done, 32 * g + 32)
                    dve.nop(nofuse=True)
                    for c in range(GCH):
                        dve.bn_stats(cstat[:, c, :], acc[p][:, c, :]).then_inc(c_stat, 1)
                    for c in range(GCH):
                        dve.wait_ge(c_stat, 4 * g + c + 1)
                        dve.nop(nofuse=True)
                        dve.bn_aggr(cmv[:, c, :], cstat[:, c, :]).then_inc(c_mv, 1)

                def norm_c(g, p):
                    dve.wait_ge(c_rstd, g + 1)
                    for c in range(GCH):
                        dve.tensor_scalar(acc[p][:, c, :], acc[p][:, c, :], cmv[:, c, 0:1], crstd[:, c:c + 1],
                                          ALU.subtract, ALU.mult).then_inc(normed, 1)

                def group(g, p, own, prep, fin):
                    q = 1 - p
                    for e in range(NE):
                        if prep and e == 0:
                            stats_b(g + 1)
                        if prep and e == 6:
                            expo_sums(g + 1)
                        if e < 6:
                            if own:
                                split_hidden(g, e + 2)
                        elif prep:
                            split_hidden(g + 1, e - 6)
                        if prep:
                            if e == 0:
                                norm_b(g + 1, q)
                            if e == 1:
                                gx_low(g + 1, q, 0)
                            if e == 2:
                                gx_low(g + 1, q, 1)
                            if e == 6:
                                tops(g + 1)
                            if e == 7:
                                compare(g + 1)
                                pick_two(g + 1)
                        if own:
                            accumulate(g, p, e)
                        if fin and e == 0:
                            stats_c(g - 1, q)
                        if fin and e == 1:
                            norm_c(g - 1, q)
                        if prep and e == 4:
                            logits(g + 1)

                group(-1, 1, False, True, False)
                group(0, 0, True, True, False)
                group(1, 1, True, True, True)
                with dve.Fori(1, NG // 2 - 1) as pair_of:
                    g = pair_of * 2
                    group(g, 0, True, True, True)
                    group(g + 1, 1, True, True, True)
                group(NG - 2, 0, True, True, True)
                group(NG - 1, 1, True, False, True)
                stats_c(NG - 1, 1)
                norm_c(NG - 1, 1)


def kernel(x, x_txt, L0_tok_w, L0_tok_b, L0_tok_cls_token, L0_tok_pos_embedding, L0_txt_W, L0_attn_Wq, L0_attn_Wk,
           L0_attn_Wv, L0_attn_Wf, L0_attn_bf, L0_attn_Wo, L0_attn_gamma, L0_attn_beta, L0_ffn_w1, L0_ffn_b1,
           L0_ffn_w2, L0_ffn_b2, L0_ffn_down_w, L0_ffn_down_b, L0_ffn_up_w, L0_ffn_gamma, L0_ffn_beta):
    import numpy as np
    import concourse.bacc as bacc
    from concourse.bass_utils import run_bass_kernel_spmd

    def arr(a):
        return np.asarray(a)

    def two_tiles(w):
        return np.stack([w[:KA], np.concatenate([w[KA:], w[KA:]], axis=0)], axis=1)

    def column(a):
        return np.concatenate([a[:KA, None], np.concatenate([a[KA:], a[KA:]])[:, None]], axis=1)

    img = arr(x).reshape(BATCH, 3, BLK, 8, BLK, 8).transpose(0, 1, 3, 5, 2, 4).reshape(BATCH, D, BLK * BLK)
    w = arr(L0_tok_w).reshape(D, 3, 2, 8, 2, 8).transpose(2, 4, 1, 3, 5, 0).reshape(2, 2, D, D)
    w_a = w[:, :, :KA].reshape(4, KA, D).transpose(1, 0, 2)
    w_b = w[:, :, KA:].reshape(2, 2 * KB, D).transpose(1, 0, 2)
    wf = arr(L0_attn_Wf)
    b1 = arr(L0_ffn_b1)
    ins = {
        "xblk": img,
        "ids": arr(x_txt).reshape(4, 128).T,
        "wtok": np.concatenate([w_a, w_b], axis=1),
        "pos": arr(L0_tok_pos_embedding)[0],
        "cls": arr(L0_tok_cls_token)[0],
        "rows": np.concatenate([arr(L0_tok_b), arr(L0_ffn_gamma), arr(L0_ffn_beta), arr(L0_ffn_b2)]),
        "cols": np.concatenate([np.concatenate([arr(L0_attn_bf)] * 2)[:, None], column(arr(L0_attn_gamma)),
                                column(arr(L0_attn_beta)), arr(L0_ffn_down_b).reshape(HT, 128).T,
                                np.concatenate([b1, b1])[:128, None]], axis=1),
        "table": arr(L0_txt_W),
        "wproj": two_tiles(np.concatenate([arr(L0_attn_Wq), arr(L0_attn_Wk), wf, wf, arr(L0_attn_Wv)], axis=1)),
        "wout": two_tiles(arr(L0_attn_Wo)),
        "wr1": two_tiles(arr(L0_ffn_w1)),
        "wr2": arr(L0_ffn_w2),
        "wdown": two_tiles(arr(L0_ffn_down_w).transpose(1, 0, 2).reshape(D, NE * DH)),
        "wup": arr(L0_ffn_up_w).reshape(HT, 128, D).transpose(1, 0, 2),
    }
    nc = bacc.Bacc("TRN2", target_bir_lowering=False, num_devices=1)
    arrays, args = {}, {}
    for name, a in ins.items():
        a = np.ascontiguousarray(a)
        arrays[f"in_{name}"] = a
        args[name] = nc.dram_tensor(f"in_{name}", a.shape, mybir.dt.from_np(a.dtype), kind="ExternalInput").ap()
    res = nc.dram_tensor("tokens_out", (BATCH * L, D), mybir.dt.float32, kind="ExternalOutput").ap()
    embed_fuse_moe(nc, out=res, **args)
    r = run_bass_kernel_spmd(nc, [arrays], core_ids=[0])
    return r.results[0]["tokens_out"].reshape(BATCH, L, D)
```

```python
import concourse.bass as bass
from concourse import mybir
from contextlib import ExitStack

BATCH, D = 16, 192
GRID, BLK = 27, 28
TOK_IMG = GRID * GRID + 1
TXT = 32
L = TOK_IMG + TXT
CH = 127
NCH = L // CH
NPAIR = NCH // 2
HALF = L // 2
KA, KB = 128, D - 128
M_DIM = 64
VOCAB = 8000
NPROJ = 4 * M_DIM + D
NE, DH = 8, 256
HT = NE * DH // 128
H1 = D // 2
GCH = 4
GT = GCH * CH
NG = BATCH * NCH // GCH
XW = 790
WS = 1024.0
PROB_CLAMP = 1e6 - 1.0
Z_BANKS = 4
Z_RING = 4


def embed_fuse_moe(nc, xblk, ids, wtok, pos, cls, rows, cols, table, wproj, wout, wr1, wr2, wdown, wup, out):
    fp32, fp16, i32 = mybir.dt.float32, mybir.dt.float16, mybir.dt.int32
    ALU = mybir.AluOpType
    ACT = mybir.ActivationFunctionType
    AX = mybir.AxisListType.X

    ctx = ExitStack()
    with ctx:
        def sem(name, scope=ctx):
            return scope.enter_context(nc.semaphore(name))

        def sb(name, shape, dt=fp32, scope=ctx):
            return scope.enter_context(nc.sbuf_tensor(name, shape, dt))

        def need(eng, s, value):
            if not isinstance(value, int) or value > 0:
                eng.wait_ge(s, value)

        banks = [ctx.enter_context(nc.psum_tensor(f"bank{i}", [128, 512], fp32)) for i in range(8)]

        H = sb("H", [128, BATCH * NCH, D])
        ident = sb("ident", [128, 128])
        minus_half = sb("minus_half", [CH, NCH])
        epsilon = sb("epsilon", [CH, NCH])
        colv = sb("colv", [128, 22])
        rowv = sb("rowv", [CH, 3 * D + NE])
        down_h = sb("down_h", [128, 2, NE * DH], fp16)
        down_l = sb("down_l", [128, 2, NE * DH], fp16)
        up_h = sb("up_h", [128, HT, D], fp16)
        up_l = sb("up_l", [128, HT, D], fp16)
        r1_h = sb("r1_h", [128, 2, H1], fp16)
        r1_l = sb("r1_l", [128, 2, H1], fp16)
        r2 = sb("r2", [H1, NE])
        forget_bias, down_b, router_b1 = colv[:, 0:1], colv[:, 5:21], colv[0:H1, 21:22]
        tok_b, ffn_gamma, ffn_beta, router_b2 = (
            rowv[:, 0:D], rowv[:, D:2 * D], rowv[:, 2 * D:3 * D], rowv[:, 3 * D:3 * D + NE])

        def mm_features(pe, dst, w_h, w_l, lo, hi, x_h, x_l, x_s, c0, c1):
            pe.matmul(dst, w_h[:, 0, lo:hi], x_h[:, c0:c1], start=True, stop=False)
            pe.matmul(dst, w_h[:, 0, lo:hi], x_l[:, c0:c1], start=False, stop=False)
            pe.matmul(dst, w_l[:, 0, lo:hi], x_h[:, c0:c1], start=False, stop=False)
            pe.matmul(dst, w_h[:, 1, lo:hi], x_s[:, c0:c1], start=False, stop=False)
            return pe.matmul(dst, w_l[:, 1, lo:hi], x_s[:, c0:c1], start=False, stop=True)

        def mm_tokens(pe, dst, w_h, w_l, lo, hi, x_h, x_l, x_s, c0):
            c1 = c0 + 128
            pe.matmul(dst, x_h[:, c0:c1], w_h[:, 0, lo:hi], start=True, stop=False)
            pe.matmul(dst, x_h[:, c0:c1], w_l[:, 0, lo:hi], start=False, stop=False)
            pe.matmul(dst, x_l[:, c0:c1], w_h[:, 0, lo:hi], start=False, stop=False)
            pe.matmul(dst, x_s[:, c0:c1], w_h[:, 1, lo:hi], start=False, stop=False)
            return pe.matmul(dst, x_s[:, c0:c1], w_l[:, 1, lo:hi], start=False, stop=True)

        ctxa = ExitStack()
        with ctxa:
            def sa(name, shape, dt=fp32):
                return sb(name, shape, dt, ctxa)

            def sema(name):
                return sem(name, ctxa)

            xa = sa("xa", [128, BLK * BLK])
            xb = sa("xb", [128, BLK * BLK])
            pa_h = [sa(f"pa_h{i}", [128, 2, XW], fp16) for i in range(2)]
            pa_l = [sa(f"pa_l{i}", [128, 2, XW], fp16) for i in range(2)]
            pb_h = [sa(f"pb_h{i}", [128, XW], fp16) for i in range(2)]
            pb_l = [sa(f"pb_l{i}", [128, XW], fp16) for i in range(2)]
            wt_h = sa("wt_h", [128, 6, D], fp16)
            wt_l = sa("wt_l", [128, 6, D], fp16)
            wp_h = sa("wp_h", [128, 2, NPROJ], fp16)
            wp_l = sa("wp_l", [128, 2, NPROJ], fp16)
            wo_h = sa("wo_h", [128, 2, D], fp16)
            wo_l = sa("wo_l", [128, 2, D], fp16)
            base = sa("base", [128, NCH - 1 + BATCH, D])
            patch_rows = sa("patch_rows", [CH, NCH])
            causal = sa("causal", [CH, CH + M_DIM])
            gate_sign = sa("gate_sign", [128, 1])
            beta_cols = sa("beta_cols", [128, 2, CH])
            beta_out = sa("beta_out", [CH, D])
            badd0 = sa("badd0", [CH, D])
            idx = sa("idx", [128, 4], i32)
            idx_ok = sa("idx_ok", [128, 4])
            idx_hi = sa("idx_hi", [128, 4])
            idx_c = sa("idx_c", [128, 4], i32)
            xn = [sa(f"xn{i}", [CH, 2, D]) for i in range(2)]
            x_h = sa("x_h", [128, L + 2], fp16)
            x_l = sa("x_l", [128, L + 2], fp16)
            x_s = sa("x_s", [128, L + 2], fp16)
            stat1 = sa("stat1", [CH, NCH, 6])
            mv1 = sa("mv1", [CH, NCH, 2])
            rstd1 = sa("rstd1", [CH, NCH])
            var1 = sa("var1", [CH, NCH])
            qk = sa("qk", [128, L])
            qk_e = sa("qk_e", [128, L])
            gate = sa("gate", [128, L])
            cum = sa("cum", [128, L])
            qT = [sa(f"qT{i}", [M_DIM, L]) for i in range(2)]
            kT = [sa(f"kT{i}", [M_DIM, L]) for i in range(2)]
            v = [sa(f"v{i}", [CH, NCH, D + 1]) for i in range(2)]
            pk = [sa(f"pk{i}", [CH, CH + M_DIM]) for i in range(2)]
            state = [sa(f"state{i}", [M_DIM, D + 1]) for i in range(2)]
            num = sa("num", [CH, 2, D + 1])
            stat2 = sa("stat2", [CH, NCH, 6])
            mv2 = sa("mv2", [CH, NCH, 2])
            den = sa("den", [CH, NCH])
            den_sq = sa("den_sq", [CH, NCH])
            vn = sa("vn", [CH, NCH])
            hscale = sa("hscale", [CH, NCH])
            y = sa("y", [CH, 2, D])
            y_h = [sa(f"y_h{i}", [128, 256], fp16) for i in range(2)]
            y_l = [sa(f"y_l{i}", [128, 256], fp16) for i in range(2)]
            y_s = [sa(f"y_s{i}", [128, 256], fp16) for i in range(2)]

            Hflat = H[:, :, :].rearrange("p c d -> p (c d)")
            at = [40 * D]

            def staged(n):
                at[0] += n
                return Hflat[:, at[0] - n:at[0]]
            raw_tok = staged(6 * D).rearrange("p (k n) -> p k n", k=6)
            raw_proj = staged(2 * NPROJ).rearrange("p (k n) -> p k n", k=2)
            raw_out = staged(2 * D).rearrange("p (k n) -> p k n", k=2)
            raw_r1 = staged(2 * H1).rearrange("p (k n) -> p k n", k=2)
            raw_down = staged(2 * NE * DH).rearrange("p (k n) -> p k n", k=2)
            raw_up = staged(HT * D).rearrange("p (k n) -> p k n", k=HT)
            txt = staged(4 * D).rearrange("p (g n) -> p g n", g=4)
            pos5 = staged(D)
            assert at[0] <= BATCH * NCH * D

            tok_bank, x_bank, proj_bank = banks[0:2], banks[2], banks[3:5]
            core_bank, num_bank, y_bank = banks[5], banks[6], banks[7]

            tok_loaded, proj_loaded, moe_loaded = sema("tok_loaded"), sema("proj_loaded"), sema("moe_loaded")
            small_loaded, pos_loaded, ids_loaded = sema("small_loaded"), sema("pos_loaded"), sema("ids_loaded")
            txt_gathered, txt_placed = sema("txt_gathered"), sema("txt_placed")
            ident_set, consts_set, base_set, ids_set = sema("ident_set"), sema("consts_set"), sema("base_set"), sema("ids_set")
            txt_masked, pads_set, cols_set = sema("txt_masked"), sema("pads_set"), sema("cols_set")
            tok_split, proj_split = sema("tok_split"), sema("proj_split")
            moe_scaled, moe_hi, moe_lo = sema("moe_scaled"), sema("moe_hi"), sema("moe_lo")
            beta_mm, beta_set = sema("beta_mm"), sema("beta_set")
            pix_loaded, pix_hi, pix_lo = sema("pix_loaded"), sema("pix_hi"), sema("pix_lo")
            patch_done, patch_added = sema("patch_done"), sema("patch_added")
            ln1_stat, ln1_mv, ln1_rstd, xn_done = sema("ln1_stat"), sema("ln1_mv"), sema("ln1_rstd"), sema("xn_done")
            ln1_var = sema("ln1_var")
            h_biased = sema("h_biased")
            xt_done, xt_hi, xt_lo = sema("xt_done"), sema("xt_hi"), sema("xt_lo")
            proj_done, proj_out = sema("proj_done"), sema("proj_out")
            f_clamped, f_logged, f_summed, f_clipped, gate_done = (
                sema("f_clamped"), sema("f_logged"), sema("f_summed"), sema("f_clipped"), sema("gate_done"))
            qk_min, qk_exp, qk_elu, q_done, k_done = (
                sema("qk_min"), sema("qk_exp"), sema("qk_elu"), sema("q_done"), sema("k_done"))
            core_done, pk_done, state_done = sema("core_done"), sema("pk_done"), sema("state_done")
            num_done, num_out = sema("num_done"), sema("num_out")
            ln2_stat, ln2_mv, den_scaled, den_squared = (
                sema("ln2_stat"), sema("ln2_mv"), sema("den_scaled"), sema("den_squared"))
            ln2_var, ln2_scale, y_done = sema("ln2_var"), sema("ln2_scale"), sema("y_done")
            yt_done, yt_hi, yt_lo = sema("yt_done"), sema("yt_hi"), sema("yt_lo")
            out_done, h_done = sema("out_done"), sema("h_done")

            block = ctxa.enter_context(nc.Block())

            @block.sync
            def _(sp):
                def load_image(n):
                    need(sp, pix_lo, 3 * n)
                    sp.dma_start(xa[:, :], xblk[n, 0:KA, :]).then_inc(pix_loaded, 16)
                    sp.dma_start(xb[0:KB, :], xblk[n, KA:D, :]).then_inc(pix_loaded, 16)
                    sp.dma_start(xb[KB:128, 0:BLK * BLK - 1], xblk[n, KA:D, 1:BLK * BLK]).then_inc(pix_loaded, 16)

                sp.dma_start(idx[:, :], ids).then_inc(ids_loaded, 16)
                load_image(0)
                sp.dma_start(raw_tok, wtok).then_inc(tok_loaded, 16)
                sp.dma_start(raw_proj, wproj).then_inc(proj_loaded, 16)
                sp.dma_start(raw_out, wout).then_inc(proj_loaded, 16)
                load_image(1)
                sp.dma_start(raw_r1, wr1).then_inc(moe_loaded, 16)
                sp.dma_start(raw_down, wdown).then_inc(moe_loaded, 16)
                sp.dma_start(raw_up, wup).then_inc(moe_loaded, 16)
                sp.wait_ge(txt_masked, 4)
                for b in range(BATCH):
                    q = TXT * (b % 4)
                    sp.dma_start(base[CH - TXT:CH, 5 + b, :], txt[q:q + TXT, b // 4, :]).then_inc(txt_placed, 16)
                with sp.Fori(2, BATCH) as n:
                    load_image(n)

            @block.gpsimd
            def _(pool):
                pool.memset(ident[:, :], 0.0).then_inc(ident_set, 1)
                pool.wait_ge(ident_set, 1)
                pool.affine_select(out=ident[:, :], in_=ident[:, :], compare_op=ALU.not_equal, fill=1.0,
                                   base=0, pattern=[[-1, 128]], channel_multiplier=1).then_inc(ident_set, 1)
                pool.wait_ge(ids_set, 5)
                for g in range(4):
                    pool.indirect_dma_start(out=txt[:, g, :], out_offset=None, in_=table,
                                            in_offset=bass.IndirectOffsetOnAxis(ap=idx_c[:, g:g + 1], axis=0),
                                            bounds_check=VOCAB - 1, oob_is_err=False).then_inc(txt_gathered, 16)
                for i in range(2):
                    for buf in (pa_h[i], pa_l[i]):
                        pool.memset(buf[:, :, 0:1], 0.0).then_inc(pads_set, 1)
                        pool.memset(buf[:, :, 1 + BLK * GRID:XW], 0.0).then_inc(pads_set, 1)
                    for buf in (pb_h[i], pb_l[i]):
                        pool.memset(buf[:, 0:1], 0.0).then_inc(pads_set, 1)
                        pool.memset(buf[:, 1 + BLK * GRID:XW], 0.0).then_inc(pads_set, 1)
                    for buf in (y_h[i], y_l[i], y_s[i]):
                        pool.memset(buf[:, 2 * CH:256], 0.0).then_inc(pads_set, 1)
                    pool.memset(v[i][:, :, D:D + 1], 1.0).then_inc(pads_set, 1)
                for buf in (x_h, x_l, x_s):
                    pool.memset(buf[:, L:L + 2], 0.0).then_inc(pads_set, 1)
                pool.memset(patch_rows[:, :], 1.0 / WS).then_inc(consts_set, 1)
                pool.memset(causal[:, :], 1.0).then_inc(consts_set, 1)
                pool.memset(minus_half[:, :], -0.5).then_inc(consts_set, 1)
                pool.memset(epsilon[:, :], 1e-5).then_inc(consts_set, 1)
                pool.memset(gate_sign[:, :], 1.0).then_inc(consts_set, 1)
                pool.memset(beta_cols[:, :, :], 0.0).then_inc(consts_set, 1)
                pool.wait_ge(consts_set, 6)
                pool.affine_select(out=patch_rows[:, 0:1], in_=patch_rows[:, 0:1], compare_op=ALU.is_ge, fill=0.0,
                                   base=-1, pattern=[[0, 1]], channel_multiplier=1).then_inc(consts_set, 1)
                pool.affine_select(out=patch_rows[:, 5:6], in_=patch_rows[:, 5:6], compare_op=ALU.is_ge, fill=0.0,
                                   base=CH - TXT - 1, pattern=[[0, 1]], channel_multiplier=-1).then_inc(consts_set, 1)
                pool.affine_select(out=gate_sign[:, :], in_=gate_sign[:, :], compare_op=ALU.is_ge, fill=-1.0,
                                   base=-M_DIM, pattern=[[0, 1]], channel_multiplier=1).then_inc(consts_set, 1)
                pool.affine_select(out=causal[:, 0:CH], in_=causal[:, 0:CH], compare_op=ALU.is_ge, fill=0.0,
                                   base=0, pattern=[[1, CH]], channel_multiplier=-1).then_inc(consts_set, 1)

                def split_pixels_lo(n, p, k):
                    pool.wait_ge(pix_hi, 3 * n + k + 1)
                    if k < 2:
                        src = xa[:, :].rearrange("p (r c) -> p r c", c=BLK)[:, :, k:k + GRID]
                        hi, lo = pa_h[p][:, k, 1:1 + BLK * GRID], pa_l[p][:, k, 1:1 + BLK * GRID]
                    else:
                        src = xb[:, :].rearrange("p (r c) -> p r c", c=BLK)[:, :, 0:GRID]
                        hi, lo = pb_h[p][:, 1:1 + BLK * GRID], pb_l[p][:, 1:1 + BLK * GRID]
                    hi, lo = hi.rearrange("p (r c) -> p r c", c=GRID), lo.rearrange("p (r c) -> p r c", c=GRID)
                    pool.tensor_tensor(lo, src, hi, ALU.subtract).then_inc(pix_lo, 1)

                for k in range(3):
                    split_pixels_lo(0, 0, k)
                pool.wait_ge(pos_loaded, 64)
                pool.wait_ge(small_loaded, 32)
                pool.tensor_tensor(base[0:CH, 0, :], base[0:CH, 0, :], badd0[:, :], ALU.add).then_inc(base_set, 1)
                pool.tensor_tensor(base[0:CH, 1:5, :], base[0:CH, 1:5, :],
                                   tok_b.unsqueeze(1).broadcast_to([CH, 4, D]), ALU.add).then_inc(base_set, 1)
                pool.tensor_tensor(pos5[0:95, :], pos5[0:95, :], tok_b[0:95, :], ALU.add).then_inc(base_set, 1)
                pool.wait_ge(base_set, 3)
                pool.tensor_copy(base[0:95, 5, :], pos5[0:95, :]).then_inc(base_set, 1)

                def rsqrt1(n, q):
                    pool.wait_ge(ln1_mv, 6 * n + 2 * q + 2)
                    need(pool, xn_done, 6 * n)
                    s = slice(2 * q, 2 * q + 2)
                    pool.tensor_tensor(var1[:, s], mv1[:, s, 1], epsilon[:, s], ALU.add).then_inc(ln1_var, 1)
                    pool.wait_ge(ln1_var, 3 * n + q + 1)
                    pool.tensor_tensor(rstd1[:, s], var1[:, s], minus_half[:, s], ALU.pow).then_inc(ln1_rstd, 1)

                def bias_h(n, q):
                    pool.wait_ge(xn_done, 6 * n + 2 * q + 2)
                    c = 6 * n + 2 * q
                    pool.tensor_tensor(H[0:CH, bass.ds(c, 2), :], H[0:CH, bass.ds(c, 2), :],
                                       beta_out[:, :].unsqueeze(1).broadcast_to([CH, 2, D]), ALU.add)\
                        .then_inc(h_biased, 1)

                def scale2(n, q):
                    s = slice(2 * q, 2 * q + 2)
                    m = 3 * n + q
                    pool.wait_ge(den_scaled, m + 1)
                    need(pool, ln2_var, 3 * n)
                    pool.tensor_tensor(den_sq[:, s], den[:, s], den[:, s], ALU.mult).then_inc(den_squared, 1)
                    pool.wait_ge(ln2_mv, 2 * m + 2)
                    need(pool, ln2_scale, 3 * n)
                    pool.wait_ge(den_squared, m + 1)
                    pool.tensor_tensor(vn[:, s], mv2[:, s, 1], den_sq[:, s], ALU.add).then_inc(ln2_var, 1)
                    pool.wait_ge(ln2_var, m + 1)
                    need(pool, y_done, 6 * n)
                    pool.tensor_tensor(hscale[:, s], vn[:, s], minus_half[:, s], ALU.pow).then_inc(ln2_scale, 1)

                def mixed(n, p, front, back, pixels):
                    lo = (lambda k: split_pixels_lo(n + 2, p, k)) if pixels else (lambda k: None)
                    if front:
                        rsqrt1(n + 1, 0)
                    lo(0)
                    if front:
                        bias_h(n + 1, 0)
                        rsqrt1(n + 1, 1)
                    if back:
                        scale2(n, 0)
                    lo(1)
                    if front:
                        bias_h(n + 1, 1)
                        rsqrt1(n + 1, 2)
                    if back:
                        scale2(n, 1)
                    if front:
                        bias_h(n + 1, 2)
                    lo(2)
                    if back:
                        scale2(n, 2)

                def moe_low(k, src, hi, lo):
                    pool.wait_ge(moe_hi, k + 1)
                    pool.tensor_tensor(lo, src, hi, ALU.subtract).then_inc(moe_lo, 1)

                pool.wait_ge(beta_set, 1)
                pool.wait_ge(consts_set, 10)
                mixed(-1, 1, True, False, False)
                pool.tensor_copy(base[0:95, 6:5 + BATCH, :],
                                 pos5[0:95, :].unsqueeze(1).broadcast_to([95, BATCH - 1, D])).then_inc(base_set, 1)
                for k in range(3):
                    split_pixels_lo(1, 1, k)
                mixed(0, 0, True, True, True)
                moe_low(0, raw_r1, r1_h[:, :, :], r1_l[:, :, :])
                moe_low(1, raw_down, down_h[:, :, :], down_l[:, :, :])
                mixed(1, 1, True, True, True)
                moe_low(2, raw_up, up_h[:, :, :], up_l[:, :, :])
                with pool.Fori(1, BATCH // 2 - 1) as pair_of:
                    n = pair_of * 2
                    mixed(n, 0, True, True, True)
                    mixed(n + 1, 1, True, True, True)
                mixed(BATCH - 2, 0, True, True, False)
                mixed(BATCH - 1, 1, False, True, False)

            @block.scalar
            def _(act):
                act.preload_act_table_set("natural_log_exp_and_others")
                act.dma_start(rowv[:, :], rows.partition_broadcast(CH)).then_inc(small_loaded, 16)
                act.dma_start(colv[:, :], cols).then_inc(small_loaded, 16)
                act.dma_start(badd0[0:1, :], cls).then_inc(pos_loaded, 16)
                act.dma_start(badd0[1:CH, :], rows[0:D].partition_broadcast(CH - 1)).then_inc(pos_loaded, 16)
                act.dma_start(base[0:CH, 0:5, :], pos[0:5 * CH, :].rearrange("(c p) d -> p c d", p=CH)).then_inc(pos_loaded, 16)
                act.dma_start(pos5[0:95, :], pos[5 * CH:TOK_IMG, :]).then_inc(pos_loaded, 16)
                act.dma_start(r2[:, :], wr2).then_inc(moe_loaded, 16)

                def split_pixels_hi(n, p, k):
                    pix_src = (xa if k < 2 else xb)[:, :]
                    dx = k if k < 2 else 0
                    dst = pa_h[p][:, k, 1:1 + BLK * GRID] if k < 2 else pb_h[p][:, 1:1 + BLK * GRID]
                    if k == 0:
                        act.wait_ge(pix_loaded, 48 * n + 48)
                        need(act, patch_done, 6 * (n - 1))
                    act.activation(dst.rearrange("p (r c) -> p r c", c=GRID),
                                   pix_src.rearrange("p (r c) -> p r c", c=BLK)[:, :, dx:dx + GRID],
                                   ACT.Copy).then_inc(pix_hi, 1)

                for k in range(3):
                    split_pixels_hi(0, 0, k)
                act.wait_ge(tok_loaded, 16)
                act.activation(wt_h[:, :, :], raw_tok, ACT.Copy, scale=WS).then_inc(tok_split, 1)
                act.wait_ge(proj_loaded, 32)
                act.activation(wp_h[:, :, :], raw_proj, ACT.Copy, scale=WS).then_inc(proj_split, 1)
                act.wait_ge(cols_set, 1)
                for k in range(2):
                    act.activation(wo_h[:, k, :], raw_out[:, k, :], ACT.Copy, scale=colv[:, 1 + k:2 + k])\
                        .then_inc(proj_split, 1)

                def x_high(n, q):
                    act.wait_ge(xt_done, 3 * n + q + 1)
                    need(act, proj_done, 7 * n)
                    c = 2 * CH * q
                    act.activation(x_h[:, c:c + 2 * CH], x_bank[:, 0:2 * CH], ACT.Copy).then_inc(xt_hi, 1)
                    act.activation(x_s[0:KB, c:c + 2 * CH], x_bank[0:KB, 2 * CH:4 * CH], ACT.Copy).then_inc(xt_hi, 1)

                def y_high(n, p, q):
                    m = 3 * n + q
                    i = (3 * p + q) % 2
                    act.wait_ge(yt_done, m + 1)
                    need(act, out_done, m - 1)
                    act.activation(y_h[i][:, 0:2 * CH], y_bank[:, 0:2 * CH], ACT.Copy).then_inc(yt_hi, 1)
                    act.activation(y_s[i][0:KB, 0:2 * CH], y_bank[0:KB, 2 * CH:4 * CH], ACT.Copy).then_inc(yt_hi, 1)

                def num_copy(n, q):
                    act.wait_ge(num_done, 6 * n + 2 * q + 2)
                    need(act, y_done, 2 * (3 * n + q))
                    act.activation(num[:, :, :], num_bank[0:CH, 0:2 * (D + 1)].rearrange("p (c d) -> p c d", c=2),
                                   ACT.Copy).then_inc(num_out, 1)

                def take_qk(n, half):
                    s = slice(HALF * half, HALF * half + HALF)
                    act.wait_ge(proj_done, 7 * n + 2 * half + 1)
                    if half == 0:
                        need(act, qk_elu, n)
                    act.activation(qk[:, s], proj_bank[0][:, 0:HALF], ACT.Copy, scale=1.0 / WS).then_inc(proj_out, 1)

                def take_f(n, half):
                    s = slice(HALF * half, HALF * half + HALF)
                    act.wait_ge(proj_done, 7 * n + 2 * half + 2)
                    if half == 0:
                        need(act, q_done, n)
                        need(act, k_done, n)
                    act.activation(gate[:, s], proj_bank[1][:, 0:HALF], ACT.Exp, bias=forget_bias, scale=-1.0 / WS)\
                        .then_inc(proj_out, 1)

                def take_v(n, p, q):
                    act.wait_ge(proj_done, 7 * n + 5 + q)
                    if q == 0:
                        need(act, num_done, 6 * (n - 1))
                    act.activation(v[p][:, 2 * q:2 * q + 2, 0:D],
                                   proj_bank[(q + 1) % 2][0:CH, 0:2 * D].rearrange("p (c d) -> p c d", c=2),
                                   ACT.Copy, scale=1.0 / WS).then_inc(proj_out, 1)

                def relu_qk(n):
                    act.wait_ge(proj_out, 7 * n + 4)
                    need(act, q_done, n)
                    need(act, k_done, n)
                    act.activation(qk_e[:, :], qk[:, :], ACT.Relu, scale=-1.0).then_inc(qk_min, 1)

                def log_forget(n):
                    act.wait_ge(f_clamped, n + 1)
                    act.activation(gate[:, :], gate[:, :], ACT.Ln, bias=1.0).then_inc(f_logged, 1)

                def exp_qk(n):
                    act.wait_ge(qk_min, n + 1)
                    act.activation(qk_e[:, :], qk_e[:, :], ACT.Exp, scale=-1.0).then_inc(qk_exp, 1)

                def gates(n):
                    act.wait_ge(f_clipped, n + 1)
                    act.activation(gate[:, :], cum[:, :], ACT.Exp, scale=gate_sign[:, 0:1]).then_inc(gate_done, 1)

                def mixed(n, p, front, back, pixels, before):
                    m, r = n + 1, 1 - p
                    if back:
                        gates(n)
                    if pixels:
                        split_pixels_hi(n + 2, p, 0)
                    if before:
                        y_high(n - 1, r, 2)
                    if front:
                        x_high(m, 0)
                    if back:
                        num_copy(n, 0)
                    if pixels:
                        split_pixels_hi(n + 2, p, 1)
                    if front:
                        x_high(m, 1)
                    if back:
                        y_high(n, p, 0)
                        num_copy(n, 1)
                    if pixels:
                        split_pixels_hi(n + 2, p, 2)
                    if front:
                        x_high(m, 2)
                        take_qk(m, 0)
                        take_f(m, 0)
                    if back:
                        num_copy(n, 2)
                        y_high(n, p, 1)
                    if front:
                        take_qk(m, 1)
                        take_f(m, 1)
                        relu_qk(m)
                        log_forget(m)
                        take_v(m, r, 0)
                        exp_qk(m)
                        take_v(m, r, 1)
                        take_v(m, r, 2)

                def moe_high(k, src, hi):
                    act.activation(src, src, ACT.Copy, scale=WS).then_inc(moe_scaled, 1)
                    act.wait_ge(moe_scaled, k + 1)
                    act.activation(hi, src, ACT.Copy).then_inc(moe_hi, 1)

                act.wait_ge(consts_set, 10)
                act.wait_ge(cols_set, 2)
                mixed(-1, 1, True, False, False, False)
                for k in range(3):
                    split_pixels_hi(1, 1, k)
                mixed(0, 0, True, True, True, False)
                act.wait_ge(moe_loaded, 64)
                moe_high(0, raw_r1, r1_h[:, :, :])
                moe_high(1, raw_down, down_h[:, :, :])
                mixed(1, 1, True, True, True, True)
                moe_high(2, raw_up, up_h[:, :, :])
                with act.Fori(1, BATCH // 2 - 1) as pair_of:
                    n = pair_of * 2
                    mixed(n, 0, True, True, True, True)
                    mixed(n + 1, 1, True, True, True, True)
                mixed(BATCH - 2, 0, True, True, False, True)
                mixed(BATCH - 1, 1, False, True, False, True)
                y_high(BATCH - 1, 1, 2)

            @block.tensor
            def _(pe):
                def patch(n, p, c):
                    if c % 2 == 0:
                        pe.wait_ge(pix_lo, 3 * n + 3)
                    need(pe, patch_added, 6 * n + c - 1)
                    dst = tok_bank[c % 2][:, 0:D]
                    k = 0
                    for t in range(6):
                        dy = t // 2 if t < 4 else t - 4
                        a = CH * c + GRID * dy
                        if t < 4:
                            hi, lo = pa_h[p][:, t % 2, a:a + 128], pa_l[p][:, t % 2, a:a + 128]
                        else:
                            hi, lo = pb_h[p][:, a:a + 128], pb_l[p][:, a:a + 128]
                        for x, w in ((hi, wt_h), (hi, wt_l), (lo, wt_h)):
                            mm = pe.matmul(dst, x, w[:, t, :], start=(k == 0), stop=(k == 17))
                            k += 1
                    mm.then_inc(patch_done, 1)

                def turn_pair(bank, src, dst_sem):
                    for c in range(2):
                        pe.transpose(bank[:, CH * c:CH * c + CH], src[:, c, 0:KA], ident[0:CH, 0:CH])
                    for c in range(2):
                        mm = pe.transpose(bank[0:KB, CH * (2 + c):CH * (3 + c)], src[:, c, KA:D], ident[0:CH, 0:CH])
                    mm.then_inc(dst_sem, 1)

                def turn_x(n, p, q):
                    pe.wait_ge(xn_done, 6 * n + 2 * q + 2)
                    need(pe, xt_lo, 2 * (3 * n + q))
                    turn_pair(x_bank, xn[(3 * p + q) % 2], xt_done)

                def turn_y(n, q):
                    pe.wait_ge(y_done, 6 * n + 2 * q + 2)
                    need(pe, yt_lo, 2 * (3 * n + q))
                    turn_pair(y_bank, y, yt_done)

                def proj_qk_f(n, half):
                    pe.wait_ge(xt_lo, 6 * n + 4 + 2 * half)
                    for j in range(2):
                        if half == 0:
                            need(pe, h_done, 3 * (n - 1) + j)
                        else:
                            pe.wait_ge(proj_out, 7 * n + j + 1)
                        mm_features(pe, proj_bank[j][:, 0:HALF], wp_h, wp_l, 128 * j, 128 * j + 128,
                                    x_h, x_l, x_s, HALF * half, HALF * half + HALF).then_inc(proj_done, 1)

                def proj_v(n):
                    for q in range(3):
                        if q == 1:
                            need(pe, h_done, 3 * (n - 1) + 2)
                            if isinstance(n, int) and n == 0:
                                pe.wait_ge(proj_out, 3)
                        else:
                            pe.wait_ge(proj_out, 7 * n + 4 + q // 2)
                        for c in range(2):
                            mm = mm_tokens(pe, proj_bank[(q + 1) % 2][:, D * c:D * c + D], wp_h, wp_l,
                                           4 * M_DIM, NPROJ, x_h, x_l, x_s, CH * (2 * q + c))
                        mm.then_inc(proj_done, 1)

                def core(n, p, c):
                    if c == 0:
                        pe.wait_ge(q_done, n + 1)
                        pe.wait_ge(k_done, n + 1)
                    need(pe, pk_done, 6 * n + c)
                    need(pe, state_done, 5 * n + max(c - 1, 0))
                    if c > 0:
                        if c == 1:
                            pe.wait_ge(proj_out, 7 * n + 7)
                        pe.matmul(core_bank[0:M_DIM, 256:256 + D + 1], pk[(c - 1) % 2][:, CH:CH + M_DIM],
                                  v[p][:, c - 1, :], start=True, stop=True)
                    s = slice(CH * c, CH * c + CH)
                    pe.matmul(core_bank[0:CH, 0:CH], kT[p][:, s], qT[p][:, s], start=True, stop=True)
                    pe.transpose(core_bank[0:CH, CH:CH + M_DIM], kT[p][:, s], ident[0:M_DIM, 0:M_DIM])\
                        .then_inc(core_done, 1)

                def numer(n, p, c):
                    pe.wait_ge(pk_done, 6 * n + c + 1)
                    if c == 0:
                        pe.wait_ge(proj_out, 7 * n + 7)
                    if c % 2 == 0:
                        need(pe, num_out, 3 * n + c // 2)
                    dst = num_bank[0:CH, (D + 1) * (c % 2):(D + 1) * (c % 2 + 1)]
                    mm = pe.matmul(dst, pk[c % 2][:, 0:CH], v[p][:, c, :], start=True, stop=(c == 0))
                    if c > 0:
                        pe.wait_ge(state_done, 5 * n + c)
                        mm = pe.matmul(dst, qT[p][:, CH * c:CH * c + CH], state[c % 2][:, :], start=False, stop=True)
                    mm.then_inc(num_done, 1)

                def project_out(n, p, q, bank):
                    i = (3 * p + q) % 2
                    pe.wait_ge(yt_lo, 2 * (3 * n + q) + 2)
                    for c in range(2):
                        mm = mm_tokens(pe, bank[:, D * c:D * c + D], wo_h, wo_l, 0, D,
                                       y_h[i], y_l[i], y_s[i], CH * c)
                    mm.then_inc(out_done, 1)

                def mixed(n, p, front, back, before):
                    m, r = n + 1, 1 - p
                    if front:
                        patch(m, r, 0)
                        patch(m, r, 1)
                    if before:
                        turn_y(n - 1, 2)
                    if back:
                        core(n, p, 0)
                    if before:
                        pe.wait_ge(proj_out, 7 * n + 6)
                        project_out(n - 1, r, 2, proj_bank[0])
                    if front:
                        patch(m, r, 2)
                    if back:
                        core(n, p, 1)
                        numer(n, p, 0)
                    if front:
                        turn_x(m, r, 0)
                        patch(m, r, 3)
                    if back:
                        core(n, p, 2)
                        numer(n, p, 1)
                    if front:
                        patch(m, r, 4)
                    if back:
                        core(n, p, 3)
                        numer(n, p, 2)
                    if front:
                        turn_x(m, r, 1)
                        patch(m, r, 5)
                    if back:
                        turn_y(n, 0)
                        core(n, p, 4)
                        numer(n, p, 3)
                        pe.wait_ge(proj_out, 7 * n + 7)
                        project_out(n, p, 0, proj_bank[1])
                        core(n, p, 5)
                        numer(n, p, 4)
                    if front:
                        turn_x(m, r, 2)
                    if back:
                        numer(n, p, 5)
                    if front:
                        proj_qk_f(m, 0)
                    if back:
                        turn_y(n, 1)
                    if front:
                        proj_qk_f(m, 1)
                        if back:
                            pe.wait_ge(proj_out, 7 * m + 3)
                            project_out(n, p, 1, proj_bank[0])
                        proj_v(m)
                    else:
                        pe.wait_ge(h_done, 3 * n)
                        project_out(n, p, 1, proj_bank[0])

                pe.wait_ge(ident_set, 2)
                pe.wait_ge(cols_set, 4)
                pe.wait_ge(proj_loaded, 32)
                pe.matmul(y_bank[0:CH, 0:D], beta_cols[:, 0, :], raw_out[:, 0, :], start=True, stop=False)
                pe.matmul(y_bank[0:CH, 0:D], beta_cols[0:KB, 1, :], raw_out[0:KB, 1, :], start=False, stop=True)\
                    .then_inc(beta_mm, 1)
                pe.wait_ge(tok_split, 2)
                pe.wait_ge(proj_split, 6)
                pe.wait_ge(pads_set, 27)
                pe.wait_ge(beta_set, 1)
                mixed(-1, 1, True, False, False)
                mixed(0, 0, True, True, False)
                mixed(1, 1, True, True, True)
                with pe.Fori(1, BATCH // 2 - 1) as pair_of:
                    n = pair_of * 2
                    mixed(n, 0, True, True, True)
                    mixed(n + 1, 1, True, True, True)
                mixed(BATCH - 2, 0, True, True, True)
                mixed(BATCH - 1, 1, False, True, True)
                turn_y(BATCH - 1, 2)
                pe.wait_ge(h_done, 3 * BATCH - 1)
                project_out(BATCH - 1, 1, 2, proj_bank[0])

            @block.vector
            def _(dve):
                dve.wait_ge(ids_loaded, 16)
                dve.tensor_scalar(idx_ok[:, :], idx[:, :], 0.0, None, ALU.is_ge).then_inc(ids_set, 1)
                dve.tensor_scalar(idx_hi[:, :], idx[:, :], float(VOCAB - 1), None, ALU.is_le).then_inc(ids_set, 1)
                dve.tensor_scalar(idx_c[:, :], idx[:, :], 0.0, float(VOCAB - 1), ALU.max, ALU.min).then_inc(ids_set, 1)
                dve.wait_ge(ids_set, 3)
                dve.tensor_tensor(idx_ok[:, :], idx_ok[:, :], idx_hi[:, :], ALU.mult).then_inc(ids_set, 2)
                dve.wait_ge(small_loaded, 32)
                dve.wait_ge(consts_set, 6)
                dve.tensor_scalar(colv[:, 1:3], colv[:, 1:3], WS, None, ALU.mult).then_inc(cols_set, 1)
                dve.tensor_scalar(colv[:, 0:1], colv[:, 0:1], -1.0, None, ALU.mult).then_inc(cols_set, 1)
                for k in range(2):
                    dve.tensor_scalar(beta_cols[:, k, :], beta_cols[:, k, :], colv[:, 3 + k:4 + k], None, ALU.add)\
                        .then_inc(cols_set, 1)
                dve.wait_ge(tok_split, 1)
                dve.scalar_tensor_tensor(out=wt_l[:, :, :].rearrange("p k n -> p (k n)"), in0=raw_tok.rearrange("p k n -> p (k n)"), scalar=WS, in1=wt_h[:, :, :].rearrange("p k n -> p (k n)"), op0=ALU.mult,
                                         op1=ALU.subtract).then_inc(tok_split, 1)
                dve.wait_ge(proj_split, 3)
                dve.scalar_tensor_tensor(out=wp_l[:, :, :], in0=raw_proj, scalar=WS, in1=wp_h[:, :, :], op0=ALU.mult,
                                         op1=ALU.subtract).then_inc(proj_split, 1)
                dve.wait_ge(cols_set, 1)
                for k in range(2):
                    dve.scalar_tensor_tensor(out=wo_l[:, k, :], in0=raw_out[:, k, :], scalar=colv[:, 1 + k:2 + k],
                                             in1=wo_h[:, k, :], op0=ALU.mult, op1=ALU.subtract)\
                        .then_inc(proj_split, 1)
                dve.wait_ge(beta_mm, 1)
                dve.tensor_copy(beta_out[:, :], y_bank[0:CH, 0:D]).then_inc(beta_set, 1)
                dve.wait_ge(txt_gathered, 64)
                dve.wait_ge(ids_set, 5)
                for g in range(4):
                    dve.tensor_scalar(txt[:, g, :], txt[:, g, :], idx_ok[:, g:g + 1], None, ALU.mult)\
                        .then_inc(txt_masked, 1)

                def patch_add(n, c):
                    dve.wait_ge(patch_done, 6 * n + c + 1)
                    if c == 5 and isinstance(n, int) and n < 2:
                        dve.wait_ge(base_set, 4 + n)
                        dve.wait_ge(txt_placed, 16 * BATCH)
                    dst = H[0:CH, bass.ds(6 * n + c, 1), :].rearrange("p c d -> p (c d)")
                    add = base[0:CH, c, :] if c < 5 else \
                        base[0:CH, bass.ds(n + 5, 1), :].rearrange("p c d -> p (c d)")
                    dve.scalar_tensor_tensor(out=dst, in0=tok_bank[c % 2][0:CH, 0:D], scalar=patch_rows[:, c:c + 1],
                                             in1=add, op0=ALU.mult, op1=ALU.add).then_inc(patch_added, 1)
                    dve.wait_ge(patch_added, 6 * n + c + 1)
                    need(dve, ln1_mv, 6 * n)
                    dve.nop(nofuse=True)
                    dve.bn_stats(stat1[:, c, :], dst).then_inc(ln1_stat, 1)
                    dve.wait_ge(ln1_stat, 6 * n + c + 1)
                    need(dve, ln1_rstd, 3 * n)
                    need(dve, xn_done, 6 * n)
                    dve.nop(nofuse=True)
                    dve.bn_aggr(mv1[:, c, :], stat1[:, c, :]).then_inc(ln1_mv, 1)

                def norm_x(n, p, q):
                    dve.wait_ge(ln1_rstd, 3 * n + q + 1)
                    need(dve, xt_done, 3 * n + q - 1)
                    for c in range(2 * q, 2 * q + 2):
                        src = H[0:CH, bass.ds(6 * n + c, 1), :].rearrange("p c d -> p (c d)")
                        dve.tensor_scalar(xn[(3 * p + q) % 2][:, c % 2, :], src, mv1[:, c, 0:1], rstd1[:, c:c + 1],
                                          ALU.subtract, ALU.mult).then_inc(xn_done, 1)

                def x_low(n, q):
                    dve.wait_ge(xt_hi, 2 * (3 * n + q) + 2)
                    c = 2 * CH * q
                    dve.tensor_tensor(x_l[:, c:c + 2 * CH], x_bank[:, 0:2 * CH], x_h[:, c:c + 2 * CH],
                                      ALU.subtract).then_inc(xt_lo, 1)
                    dve.tensor_tensor(x_s[KB:128, c:c + 2 * CH], x_bank[0:KB, 2 * CH:4 * CH],
                                      x_s[0:KB, c:c + 2 * CH], ALU.subtract).then_inc(xt_lo, 1)

                def y_low(n, p, q):
                    i = (3 * p + q) % 2
                    dve.wait_ge(yt_hi, 2 * (3 * n + q) + 2)
                    dve.tensor_tensor(y_l[i][:, 0:2 * CH], y_bank[:, 0:2 * CH], y_h[i][:, 0:2 * CH],
                                      ALU.subtract).then_inc(yt_lo, 1)
                    dve.tensor_tensor(y_s[i][KB:128, 0:2 * CH], y_bank[0:KB, 2 * CH:4 * CH],
                                      y_s[i][0:KB, 0:2 * CH], ALU.subtract).then_inc(yt_lo, 1)

                def take_core(n, c):
                    dve.wait_ge(core_done, 6 * n + c + 1)
                    need(dve, num_done, 6 * n + c - 1)
                    dve.tensor_tensor(pk[c % 2][:, :], core_bank[0:CH, 0:CH + M_DIM], causal[:, :],
                                      ALU.mult).then_inc(pk_done, 1)
                    if c == 1:
                        dve.tensor_copy(state[1][:, :], core_bank[0:M_DIM, 256:256 + D + 1]).then_inc(state_done, 1)
                    if c > 1:
                        dve.wait_ge(state_done, 5 * n + c - 1)
                        dve.tensor_tensor(state[c % 2][:, :], core_bank[0:M_DIM, 256:256 + D + 1],
                                          state[(c - 1) % 2][:, :], ALU.add).then_inc(state_done, 1)

                def num_stats(n, q):
                    m = 3 * n + q
                    s = slice(2 * q, 2 * q + 2)
                    dve.wait_ge(num_out, m + 1)
                    need(dve, ln2_scale, 3 * n)
                    need(dve, y_done, 6 * n)
                    dve.tensor_scalar(den[:, s], num[:, :, D], 1e-6, 1e-5 ** 0.5, ALU.add, ALU.mult)\
                        .then_inc(den_scaled, 1)
                    dve.nop(nofuse=True)
                    for c in range(2):
                        dve.bn_stats(stat2[:, 2 * q + c, :], num[:, c, 0:D]).then_inc(ln2_stat, 1)
                    for c in range(2):
                        dve.wait_ge(ln2_stat, 2 * m + c + 1)
                        dve.nop(nofuse=True)
                        dve.bn_aggr(mv2[:, 2 * q + c, :], stat2[:, 2 * q + c, :]).then_inc(ln2_mv, 1)

                def norm_y(n, q):
                    m = 3 * n + q
                    dve.wait_ge(ln2_scale, m + 1)
                    need(dve, yt_done, m)
                    for c in range(2):
                        dve.tensor_scalar(y[:, c, :], num[:, c, 0:D], mv2[:, 2 * q + c, 0:1],
                                          hscale[:, 2 * q + c:2 * q + c + 1], ALU.subtract, ALU.mult)\
                            .then_inc(y_done, 1)

                def add_out(n, q):
                    dve.wait_ge(out_done, 3 * n + q + 1)
                    dve.wait_ge(h_biased, 3 * n + q + 1)
                    dst = H[0:CH, bass.ds(6 * n + 2 * q, 2), :].rearrange("p c d -> p (c d)")
                    dve.scalar_tensor_tensor(out=dst, in0=proj_bank[1 if q == 0 else 0][0:CH, 0:2 * D], scalar=1.0 / WS, in1=dst,
                                             op0=ALU.mult, op1=ALU.add).then_inc(h_done, 1)

                def clamp(n):
                    dve.wait_ge(proj_out, 7 * n + 4)
                    dve.tensor_scalar(gate[:, :], gate[:, :], PROB_CLAMP, None, ALU.min).then_inc(f_clamped, 1)

                def scan(n):
                    dve.wait_ge(f_logged, n + 1)
                    need(dve, gate_done, n)
                    dve.tensor_tensor_scan(cum[:, :], gate[:, :], gate[:, :], 0.0, ALU.add, ALU.max)\
                        .then_inc(f_summed, 1)
                    dve.wait_ge(f_summed, n + 1)
                    dve.tensor_scalar(cum[:, :], cum[:, :], 20.0, -20.0, ALU.min, ALU.max).then_inc(f_clipped, 1)

                def elu(n):
                    dve.wait_ge(qk_exp, n + 1)
                    dve.scalar_tensor_tensor(out=qk_e[:, :], in0=qk[:, :], scalar=0.0, in1=qk_e[:, :], op0=ALU.max,
                                             op1=ALU.add).then_inc(qk_elu, 1)

                def gate_qk(n, p):
                    dve.wait_ge(gate_done, n + 1)
                    dve.wait_ge(qk_elu, n + 1)
                    need(dve, num_done, 6 * (n - 1))
                    dve.scalar_tensor_tensor(out=qT[p][:, :], in0=qk_e[0:64, :], scalar=M_DIM ** -0.5,
                                             in1=gate[0:64, :], op0=ALU.mult, op1=ALU.mult).then_inc(q_done, 1)
                    dve.tensor_tensor(kT[p][:, :], qk_e[64:128, :], gate[64:128, :], ALU.mult).then_inc(k_done, 1)

                def mixed(n, p, front, back, before):
                    m, r = n + 1, 1 - p
                    if back:
                        gate_qk(n, p)
                    if before:
                        y_low(n - 1, r, 2)
                    if front:
                        patch_add(m, 0)
                        patch_add(m, 1)
                    if back:
                        take_core(n, 0)
                    if front:
                        norm_x(m, r, 0)
                    if before:
                        add_out(n - 1, 2)
                    if front:
                        patch_add(m, 2)
                    if back:
                        take_core(n, 1)
                    if front:
                        x_low(m, 0)
                        patch_add(m, 3)
                    if back:
                        take_core(n, 2)
                    if front:
                        norm_x(m, r, 1)
                    if back:
                        num_stats(n, 0)
                    if front:
                        patch_add(m, 4)
                    if back:
                        take_core(n, 3)
                        norm_y(n, 0)
                    if front:
                        x_low(m, 1)
                        patch_add(m, 5)
                    if back:
                        take_core(n, 4)
                        y_low(n, p, 0)
                    if front:
                        norm_x(m, r, 2)
                    if back:
                        num_stats(n, 1)
                        take_core(n, 5)
                        add_out(n, 0)
                    if front:
                        x_low(m, 2)
                    if back:
                        norm_y(n, 1)
                        num_stats(n, 2)
                        y_low(n, p, 1)
                    if front:
                        clamp(m)
                    if back:
                        add_out(n, 1)
                    if front:
                        scan(m)
                    if back:
                        norm_y(n, 2)
                    if front:
                        elu(m)

                dve.wait_ge(base_set, 2)
                dve.wait_ge(consts_set, 10)
                mixed(-1, 1, True, False, False)
                mixed(0, 0, True, True, False)
                mixed(1, 1, True, True, True)
                with dve.Fori(1, BATCH // 2 - 1) as pair_of:
                    n = pair_of * 2
                    mixed(n, 0, True, True, True)
                    mixed(n + 1, 1, True, True, True)
                mixed(BATCH - 2, 0, True, True, True)
                mixed(BATCH - 1, 1, False, True, True)
                y_low(BATCH - 1, 1, 2)
                add_out(BATCH - 1, 2)
                dve.wait_ge(moe_lo, 3)
                dve.wait_ge(h_done, 3 * BATCH)

        ctxb = ExitStack()
        with ctxb:
            def sa(name, shape, dt=fp32):
                return sb(name, shape, dt, ctxb)

            def sema(name):
                return sem(name, ctxb)

            gx_h = [sa(f"gx_h{i}", [128, GT], fp16) for i in range(2)]
            gx_l = [sa(f"gx_l{i}", [128, GT], fp16) for i in range(2)]
            gx_s = [sa(f"gx_s{i}", [128, GT], fp16) for i in range(2)]
            z32 = [sa(f"z32_{i}", [128, GT]) for i in range(Z_BANKS)]
            z_h = [sa(f"z_h{i}", [128, 2, 512], fp16) for i in range(Z_RING)]
            z_l = [sa(f"z_l{i}", [128, 2, 512], fp16) for i in range(Z_RING)]
            x2 = [sa(f"x2_{i}", [CH, GCH, D]) for i in range(2)]
            acc = [sa(f"acc{i}", [CH, GCH, D]) for i in range(2)]
            hb = sa("hb", [CH, GCH, D])
            res = [sa(f"res{i}", [CH, GCH, D]) for i in range(2)]
            bstat = sa("bstat", [CH, GCH, 6])
            bmv = sa("bmv", [CH, GCH, 2])
            brstd = sa("brstd", [CH, GCH])
            bvar = sa("bvar", [CH, GCH])
            cstat = sa("cstat", [CH, GCH, 6])
            cmv = sa("cmv", [CH, GCH, 2])
            crstd = sa("crstd", [CH, GCH])
            cvar = sa("cvar", [CH, GCH])
            rg = sa("rg", [H1, GT])
            logit = sa("logit", [CH, GCH, NE])
            lmax = sa("lmax", [CH, GCH])
            shifted = sa("shifted", [CH, GCH, NE])
            euler = sa("euler", [CH, GCH, NE])
            expo = sa("expo", [CH, GCH, NE])
            esum = sa("esum", [CH, GCH])
            einv = sa("einv", [CH, GCH])
            prob = sa("prob", [CH, GCH, NE])
            top = sa("top", [CH, GCH, 8])
            above = sa("above", [CH, GCH, NE])
            equal = sa("equal", [CH, GCH, NE])
            resets = sa("resets", [CH, GCH, NE])
            rank = sa("rank", [CH, GCH, NE])
            first_above = sa("first_above", [CH, GCH])
            rank2 = sa("rank2", [CH, GCH, NE])
            taken = sa("taken", [CH, GCH, NE])
            picked = sa("picked", [CH, GCH, NE])
            weighted = sa("weighted", [CH, GCH, NE])
            tsum = sa("tsum", [CH, GCH])
            tscaled = sa("tscaled", [CH, GCH])
            tinv = sa("tinv", [CH, GCH])
            share = [sa(f"share{i}", [CH, GCH, NE]) for i in range(2)]

            z_bank, up_bank, turn_bank, route_bank = banks[0:4], banks[4:6], banks[6], banks[7]

            b_var, c_var = sema("b_var"), sema("c_var")
            b_consts = sema("b_consts")
            b_stat, b_mv, b_rstd, x2_done = sema("b_stat"), sema("b_mv"), sema("b_rstd"), sema("x2_done")
            gx_done, gx_hi, gx_lo = sema("gx_done"), sema("gx_hi"), sema("gx_lo")
            route1_done, route_gelu, route2_done = sema("route1_done"), sema("route_gelu"), sema("route2_done")
            logit_done, lmax_done, shift_done, expo_done = (
                sema("logit_done"), sema("lmax_done"), sema("shift_done"), sema("expo_done"))
            esum_done, einv_done, prob_done, top_done = (
                sema("esum_done"), sema("einv_done"), sema("prob_done"), sema("top_done"))
            tsum_done, weighted_done = sema("tsum_done"), sema("weighted_done")
            above_done, equal_done, rank2_done = sema("above_done"), sema("equal_done"), sema("rank2_done")
            taken_done, picked_done, tscaled_done = sema("taken_done"), sema("picked_done"), sema("tscaled_done")
            rank_done, tinv_done, share_done = sema("rank_done"), sema("tinv_done"), sema("share_done")
            z_done, z32_done, zh_done, zl_done = sema("z_done"), sema("z32_done"), sema("zh_done"), sema("zl_done")
            up_done, acc_done = sema("up_done"), sema("acc_done")
            c_stat, c_mv, c_rstd, normed = sema("c_stat"), sema("c_mv"), sema("c_rstd"), sema("normed")
            hb_done, scaled, res_done, stored = sema("hb_done"), sema("scaled"), sema("res_done"), [sema("stored_even"), sema("stored_odd")]
            block = ctxb.enter_context(nc.Block())

            @block.sync
            def _(sp):
                def store(g, p):
                    sp.wait_ge(res_done, g + 1)
                    dst = out[bass.ds(g * GT, GT), :].rearrange("(c p) d -> p c d", p=CH)
                    sp.dma_start(dst[0:112], res[p][0:112]).then_inc(stored[p], 16)
                    sp.dma_start(dst[112:CH], res[p][112:CH]).then_inc(stored[p], 16)

                with sp.Fori(0, NG // 2) as pair_of:
                    g = pair_of * 2
                    store(g, 0)
                    store(g + 1, 1)
                for p in range(2):
                    sp.wait_ge(stored[p], 16 * NG)

            @block.gpsimd
            def _(pool):
                for i in range(Z_RING):
                    for buf in (z_h[i], z_l[i]):
                        pool.memset(buf[:, :, GT:512], 0.0).then_inc(b_consts, 1)
                pool.memset(euler[:, :, :], 2.718281828459045).then_inc(b_consts, 1)
                pool.memset(resets[:, :, :], 1.0).then_inc(b_consts, 1)
                pool.wait_ge(b_consts, 10)
                pool.memset(resets[:, :, 0:1], 0.0).then_inc(b_consts, 1)

                def rsqrt_b(g):
                    pool.wait_ge(b_mv, 4 * g + 4)
                    need(pool, x2_done, 4 * g)
                    pool.tensor_tensor(bvar[:, :], bmv[:, :, 1], epsilon[:, 0:GCH], ALU.add).then_inc(b_var, 1)
                    pool.wait_ge(b_var, g + 1)
                    pool.tensor_tensor(brstd[:, :], bvar[:, :], minus_half[:, 0:GCH], ALU.pow).then_inc(b_rstd, 1)

                def rsqrt_c(g):
                    pool.wait_ge(c_mv, 4 * g + 4)
                    need(pool, normed, 4 * g)
                    pool.tensor_tensor(cvar[:, :], cmv[:, :, 1], epsilon[:, 0:GCH], ALU.add).then_inc(c_var, 1)
                    pool.wait_ge(c_var, g + 1)
                    pool.tensor_tensor(crstd[:, :], cvar[:, :], minus_half[:, 0:GCH], ALU.pow).then_inc(c_rstd, 1)

                def wide(a):
                    return a.unsqueeze(2).broadcast_to([CH, GCH, NE])

                def softmax_exp(g):
                    pool.wait_ge(lmax_done, g + 1)
                    need(pool, expo_done, g)
                    pool.tensor_tensor(shifted[:, :, :], logit[:, :, :], wide(lmax[:, :]), ALU.subtract)\
                        .then_inc(shift_done, 1)
                    pool.wait_ge(shift_done, g + 1)
                    need(pool, prob_done, g)
                    pool.tensor_tensor(expo[:, :, :], euler[:, :, :], shifted[:, :, :], ALU.pow).then_inc(expo_done, 1)

                def probabilities(g):
                    pool.wait_ge(einv_done, g + 1)
                    need(pool, share_done, g)
                    pool.tensor_tensor(prob[:, :, :], expo[:, :, :], wide(einv[:, :]), ALU.mult).then_inc(prob_done, 1)

                def choose(g, p):
                    pool.wait_ge(picked_done, g + 1)
                    need(pool, share_done, g)
                    pool.tensor_tensor(weighted[:, :, :], picked[:, :, :], prob[:, :, :], ALU.mult)\
                        .then_inc(weighted_done, 1)
                    pool.wait_ge(weighted_done, g + 1)
                    pool.wait_ge(tinv_done, g + 1)
                    need(pool, acc_done, 32 * (g - 1))
                    pool.tensor_tensor(share[p][:, :, :], weighted[:, :, :], wide(tinv[:, :]), ALU.mult)\
                        .then_inc(share_done, 1)

                def add_beta(g):
                    need(pool, res_done, g)
                    pool.tensor_tensor(hb[:, :, :], H[0:CH, bass.ds(GCH * g, GCH), :],
                                       ffn_beta.unsqueeze(1).broadcast_to([CH, GCH, D]), ALU.add).then_inc(hb_done, 1)

                def finish(g, p):
                    pool.wait_ge(normed, 4 * g + 4)
                    pool.tensor_tensor(acc[p][:, :, :], acc[p][:, :, :],
                                       ffn_gamma.unsqueeze(1).broadcast_to([CH, GCH, D]), ALU.mult).then_inc(scaled, 1)
                    pool.wait_ge(scaled, g + 1)
                    pool.wait_ge(hb_done, g + 1)
                    need(pool, stored[p], 16 * (g - p))
                    pool.tensor_tensor(res[p][:, :, :], acc[p][:, :, :], hb[:, :, :], ALU.add).then_inc(res_done, 1)

                def group(g, p, prep, fin):
                    if prep:
                        rsqrt_b(g + 1)
                    if fin:
                        add_beta(g - 1)
                        rsqrt_c(g - 1)
                        finish(g - 1, 1 - p)
                    if prep:
                        softmax_exp(g + 1)
                        probabilities(g + 1)
                        choose(g + 1, 1 - p)

                group(-1, 1, True, False)
                group(0, 0, True, False)
                group(1, 1, True, True)
                group(2, 0, True, True)
                group(3, 1, True, True)
                with pool.Fori(2, NG // 2 - 1) as pair_of:
                    g = pair_of * 2
                    group(g, 0, True, True)
                    group(g + 1, 1, True, True)
                group(NG - 2, 0, True, True)
                group(NG - 1, 1, False, True)
                group(NG, 0, False, True)

            @block.scalar
            def _(act):
                def gx_high(g, p, part):
                    act.wait_ge(gx_done, 2 * g + part + 1)
                    need(act, z_done, 16 * (g - 1))
                    need(act, route1_done, g - 1)
                    dst, src = (gx_h[p][:, :], turn_bank[:, 0:GT]) if part == 0 else \
                        (gx_s[p][0:KB, :], turn_bank[0:KB, 0:GT])
                    act.activation(dst, src, ACT.Copy).then_inc(gx_hi, 1)

                def gelu_router(g):
                    act.wait_ge(route1_done, g + 1)
                    need(act, route2_done, g)
                    act.activation(rg[:, :], route_bank[0:H1, 0:GT], ACT.Gelu, bias=router_b1,
                                   scale=1.0 / WS).then_inc(route_gelu, 1)

                def gelu_hidden(g, e):
                    for t in range(2):
                        n = 16 * g + 2 * e + t
                        i = (2 * e + t) % Z_BANKS
                        act.wait_ge(z_done, n + 1)
                        need(act, zl_done, n + 1 - Z_BANKS)
                        bias = down_b[:, 2 * e + t:2 * e + t + 1]
                        act.activation(z32[i][:, :], z_bank[i][:, 0:GT], ACT.Gelu, bias=bias, scale=1.0 / WS)\
                            .then_inc(z32_done, 1)
                        if t == 0:
                            need(act, up_done, 2 * (8 * g + e + 1 - Z_RING))
                        act.activation(z_h[e % Z_RING][:, t, 0:GT], z_bank[i][:, 0:GT], ACT.Gelu, bias=bias,
                                       scale=1.0 / WS).then_inc(zh_done, 1)

                def group(g, p, own, prep):
                    for e in range(NE):
                        if e < 6:
                            if own:
                                gelu_hidden(g, e + 2)
                        elif prep:
                            gelu_hidden(g + 1, e - 6)
                        if prep:
                            if e == 1:
                                gx_high(g + 1, 1 - p, 0)
                            if e == 2:
                                gx_high(g + 1, 1 - p, 1)
                            if e == 3:
                                gelu_router(g + 1)

                group(-1, 1, False, True)
                group(0, 0, True, True)
                group(1, 1, True, True)
                with act.Fori(1, NG // 2 - 1) as pair_of:
                    g = pair_of * 2
                    group(g, 0, True, True)
                    group(g + 1, 1, True, True)
                group(NG - 2, 0, True, True)
                group(NG - 1, 1, True, False)

            @block.tensor
            def _(pe):
                def turn(g, p, part):
                    if part == 0:
                        pe.wait_ge(x2_done, 4 * g + 4)
                    need(pe, gx_lo, 2 * g + part)
                    pe.nop(nofuse=True)
                    rows_of = 128 if part == 0 else KB
                    for c in range(GCH):
                        src = x2[p][:, c, 0:KA] if part == 0 else x2[p][:, c, KA:D]
                        mm = pe.transpose(turn_bank[0:rows_of, CH * c:CH * c + CH], src, ident[0:CH, 0:CH])
                    mm.then_inc(gx_done, 1)

                def route1(g, p):
                    pe.wait_ge(gx_lo, 2 * g + 2)
                    need(pe, logit_done, g)
                    mm_features(pe, route_bank[0:H1, 0:GT], r1_h, r1_l, 0, H1, gx_h[p], gx_l[p], gx_s[p], 0, GT)\
                        .then_inc(route1_done, 1)

                def route2(g):
                    pe.wait_ge(route_gelu, g + 1)
                    for c in range(GCH):
                        mm = pe.matmul(route_bank[0:CH, NE * c:NE * c + NE], rg[:, CH * c:CH * c + CH], r2[:, :],
                                       start=True, stop=True)
                    mm.then_inc(route2_done, 1)

                def down(g, p, e):
                    if e == 0:
                        pe.wait_ge(gx_lo, 2 * g + 2)
                    for t in range(2):
                        n = 16 * g + 2 * e + t
                        need(pe, zh_done, n + 1 - Z_BANKS)
                        lo = 128 * (2 * e + t)
                        mm_features(pe, z_bank[(2 * e + t) % Z_BANKS][:, 0:GT], down_h, down_l, lo, lo + 128,
                                    gx_h[p], gx_l[p], gx_s[p], 0, GT).then_inc(z_done, 1)

                def up(g, e):
                    s = 8 * g + e
                    i = e % Z_RING
                    pe.wait_ge(zh_done, 2 * s + 2)
                    pe.wait_ge(zl_done, 2 * s + 2)
                    for half in range(2):
                        need(pe, acc_done, 4 * s - 2 + 2 * half)
                        for c in range(2):
                            a = CH * (2 * half + c)
                            k = 0
                            for t in range(2):
                                z1, z0 = z_h[i][:, t, a:a + 128], z_l[i][:, t, a:a + 128]
                                for z, w in ((z1, up_h), (z1, up_l), (z0, up_h)):
                                    mm = pe.matmul(up_bank[half][:, D * c:D * c + D], z, w[:, 2 * e + t, :],
                                                   start=(k == 0), stop=(k == 5))
                                    k += 1
                        mm.then_inc(up_done, 1)

                def group(g, p, own, prep):
                    q = 1 - p
                    for e in range(NE):
                        if e < 6:
                            if own:
                                down(g, p, e + 2)
                        elif prep:
                            down(g + 1, q, e - 6)
                        if prep:
                            if e == 1:
                                turn(g + 1, q, 0)
                            if e == 2:
                                turn(g + 1, q, 1)
                            if e == 3:
                                route1(g + 1, q)
                            if e == 4:
                                route2(g + 1)
                        if own:
                            up(g, e)

                pe.wait_ge(b_consts, 8)
                group(-1, 1, False, True)
                group(0, 0, True, True)
                group(1, 1, True, True)
                with pe.Fori(1, NG // 2 - 1) as pair_of:
                    g = pair_of * 2
                    group(g, 0, True, True)
                    group(g + 1, 1, True, True)
                group(NG - 2, 0, True, True)
                group(NG - 1, 1, True, False)

            @block.vector
            def _(dve):
                def h_chunk(g, c):
                    return H[0:CH, bass.ds(GCH * g + c, 1), :].rearrange("p c d -> p (c d)")

                def stats_b(g):
                    need(dve, b_rstd, g)
                    need(dve, x2_done, 4 * g)
                    need(dve, b_mv, 4 * g)
                    dve.nop(nofuse=True)
                    for c in range(GCH):
                        dve.bn_stats(bstat[:, c, :], h_chunk(g, c)).then_inc(b_stat, 1)
                    for c in range(GCH):
                        dve.wait_ge(b_stat, 4 * g + c + 1)
                        dve.nop(nofuse=True)
                        dve.bn_aggr(bmv[:, c, :], bstat[:, c, :]).then_inc(b_mv, 1)

                def norm_b(g, p):
                    dve.wait_ge(b_rstd, g + 1)
                    need(dve, gx_done, 2 * (g - 1))
                    need(dve, acc_done, 32 * (g - 2) + 4)
                    for c in range(GCH):
                        dve.tensor_scalar(x2[p][:, c, :], h_chunk(g, c), bmv[:, c, 0:1], brstd[:, c:c + 1],
                                          ALU.subtract, ALU.mult).then_inc(x2_done, 1)

                def gx_low(g, p, part):
                    dve.wait_ge(gx_hi, 2 * g + part + 1)
                    if part == 0:
                        dve.tensor_tensor(gx_l[p][:, :], turn_bank[:, 0:GT], gx_h[p][:, :], ALU.subtract)\
                            .then_inc(gx_lo, 1)
                    else:
                        dve.tensor_tensor(gx_s[p][KB:128, :], turn_bank[0:KB, 0:GT], gx_s[p][0:KB, :],
                                          ALU.subtract).then_inc(gx_lo, 1)

                def logits(g):
                    dve.wait_ge(route2_done, g + 1)
                    need(dve, shift_done, g)
                    dve.tensor_tensor(logit[:, :, :], route_bank[0:CH, 0:GCH * NE].rearrange("p (c e) -> p c e", e=NE),
                                      router_b2.unsqueeze(1).broadcast_to([CH, GCH, NE]), ALU.add).then_inc(logit_done, 1)
                    dve.wait_ge(logit_done, g + 1)
                    dve.tensor_reduce(lmax[:, :], logit[:, :, :], AX, ALU.max).then_inc(lmax_done, 1)

                def expo_sums(g):
                    dve.wait_ge(expo_done, g + 1)
                    need(dve, einv_done, g)
                    dve.tensor_reduce(esum[:, :], expo[:, :, :], AX, ALU.add).then_inc(esum_done, 1)
                    dve.wait_ge(esum_done, g + 1)
                    need(dve, prob_done, g)
                    dve.reciprocal(einv[:, :], esum[:, :]).then_inc(einv_done, 1)

                def tops(g):
                    dve.wait_ge(prob_done, g + 1)
                    need(dve, share_done, g)
                    dve.nop(nofuse=True)
                    for c in range(GCH):
                        dve.max(top[:, c, :], prob[:, c, :]).then_inc(top_done, 1)

                def compare(g):
                    dve.wait_ge(top_done, 4 * g + 4)
                    second = top[:, :, 1:2].broadcast_to([CH, GCH, NE])
                    dve.tensor_tensor(above[:, :, :], prob[:, :, :], second, ALU.is_gt).then_inc(above_done, 1)
                    dve.tensor_tensor(equal[:, :, :], prob[:, :, :], second, ALU.is_equal).then_inc(equal_done, 1)
                    dve.tensor_tensor(first_above[:, :], top[:, :, 0], top[:, :, 1], ALU.is_gt).then_inc(above_done, 1)
                    dve.tensor_tensor(tsum[:, :], top[:, :, 0], top[:, :, 1], ALU.add).then_inc(tsum_done, 1)

                def pick_two(g):
                    dve.wait_ge(equal_done, g + 1)
                    dve.tensor_tensor_scan(rank[:, :, :].rearrange("p c e -> p (c e)"),
                                           resets[:, :, :].rearrange("p c e -> p (c e)"),
                                           equal[:, :, :].rearrange("p c e -> p (c e)"),
                                           0.0, ALU.mult, ALU.add).then_inc(rank_done, 1)
                    dve.wait_ge(tsum_done, g + 1)
                    dve.tensor_scalar(tscaled[:, :], tsum[:, :], 1e-8, WS, ALU.add, ALU.mult).then_inc(tscaled_done, 1)
                    dve.wait_ge(rank_done, g + 1)
                    dve.wait_ge(above_done, 2 * g + 2)
                    dve.tensor_tensor(rank2[:, :, :], rank[:, :, :],
                                      first_above[:, :].unsqueeze(2).broadcast_to([CH, GCH, NE]), ALU.add)\
                        .then_inc(rank2_done, 1)
                    dve.wait_ge(tscaled_done, g + 1)
                    dve.reciprocal(tinv[:, :], tscaled[:, :]).then_inc(tinv_done, 1)
                    dve.wait_ge(rank2_done, g + 1)
                    dve.scalar_tensor_tensor(out=taken[:, :, :], in0=rank2[:, :, :], scalar=2.0, in1=equal[:, :, :],
                                             op0=ALU.is_le, op1=ALU.mult).then_inc(taken_done, 1)
                    dve.wait_ge(taken_done, g + 1)
                    dve.tensor_tensor(picked[:, :, :], taken[:, :, :], above[:, :, :], ALU.add).then_inc(picked_done, 1)

                def split_hidden(g, e):
                    for t in range(2):
                        n = 16 * g + 2 * e + t
                        dve.wait_ge(zh_done, n + 1)
                        if t == 0:
                            need(dve, up_done, 2 * (8 * g + e + 1 - Z_RING))
                        i = (2 * e + t) % Z_BANKS
                        dve.tensor_tensor(z_l[e % Z_RING][:, t, 0:GT], z32[i][:, :], z_h[e % Z_RING][:, t, 0:GT],
                                          ALU.subtract).then_inc(zl_done, 1)

                def accumulate(g, p, e):
                    s = 8 * g + e
                    if e == 0:
                        dve.wait_ge(share_done, g + 1)
                        need(dve, scaled, g - 1)
                        need(dve, res_done, g - 1)
                    for half in range(2):
                        dve.wait_ge(up_done, 2 * s + half + 1)
                        for c in range(2):
                            k = 2 * half + c
                            if e > 0:
                                dve.wait_ge(acc_done, 4 * s + k - 3)
                            dve.scalar_tensor_tensor(
                                out=acc[p][:, k, :], in0=up_bank[half][0:CH, D * c:D * c + D],
                                scalar=share[p][:, k, e:e + 1], in1=(x2 if e == 0 else acc)[p][:, k, :],
                                op0=ALU.mult, op1=ALU.add).then_inc(acc_done, 1)

                def stats_c(g, p):
                    need(dve, normed, 4 * g)
                    need(dve, c_mv, 4 * g)
                    dve.wait_ge(acc_done, 32 * g + 32)
                    dve.nop(nofuse=True)
                    for c in range(GCH):
                        dve.bn_stats(cstat[:, c, :], acc[p][:, c, :]).then_inc(c_stat, 1)
                    for c in range(GCH):
                        dve.wait_ge(c_stat, 4 * g + c + 1)
                        dve.nop(nofuse=True)
                        dve.bn_aggr(cmv[:, c, :], cstat[:, c, :]).then_inc(c_mv, 1)

                def norm_c(g, p):
                    dve.wait_ge(c_rstd, g + 1)
                    for c in range(GCH):
                        dve.tensor_scalar(acc[p][:, c, :], acc[p][:, c, :], cmv[:, c, 0:1], crstd[:, c:c + 1],
                                          ALU.subtract, ALU.mult).then_inc(normed, 1)

                def group(g, p, own, prep, fin):
                    q = 1 - p
                    for e in range(NE):
                        if prep and e == 0:
                            stats_b(g + 1)
                        if prep and e == 6:
                            expo_sums(g + 1)
                        if e < 6:
                            if own:
                                split_hidden(g, e + 2)
                        elif prep:
                            split_hidden(g + 1, e - 6)
                        if prep:
                            if e == 0:
                                norm_b(g + 1, q)
                            if e == 1:
                                gx_low(g + 1, q, 0)
                            if e == 2:
                                gx_low(g + 1, q, 1)
                            if e == 6:
                                tops(g + 1)
                            if e == 7:
                                compare(g + 1)
                                pick_two(g + 1)
                        if own:
                            accumulate(g, p, e)
                        if fin and e == 0:
                            stats_c(g - 1, q)
                        if fin and e == 1:
                            norm_c(g - 1, q)
                        if prep and e == 4:
                            logits(g + 1)

                group(-1, 1, False, True, False)
                group(0, 0, True, True, False)
                group(1, 1, True, True, True)
                with dve.Fori(1, NG // 2 - 1) as pair_of:
                    g = pair_of * 2
                    group(g, 0, True, True, True)
                    group(g + 1, 1, True, True, True)
                group(NG - 2, 0, True, True, True)
                group(NG - 1, 1, True, False, True)
                stats_c(NG - 1, 1)
                norm_c(NG - 1, 1)


def kernel(x, x_txt, L0_tok_w, L0_tok_b, L0_tok_cls_token, L0_tok_pos_embedding, L0_txt_W, L0_attn_Wq, L0_attn_Wk,
           L0_attn_Wv, L0_attn_Wf, L0_attn_bf, L0_attn_Wo, L0_attn_gamma, L0_attn_beta, L0_ffn_w1, L0_ffn_b1,
           L0_ffn_w2, L0_ffn_b2, L0_ffn_down_w, L0_ffn_down_b, L0_ffn_up_w, L0_ffn_gamma, L0_ffn_beta):
    import numpy as np
    import concourse.bacc as bacc
    from concourse.bass_utils import run_bass_kernel_spmd

    def arr(a):
        return np.asarray(a)

    def two_tiles(w):
        return np.stack([w[:KA], np.concatenate([w[KA:], w[KA:]], axis=0)], axis=1)

    def column(a):
        return np.concatenate([a[:KA, None], np.concatenate([a[KA:], a[KA:]])[:, None]], axis=1)

    img = arr(x).reshape(BATCH, 3, BLK, 8, BLK, 8).transpose(0, 1, 3, 5, 2, 4).reshape(BATCH, D, BLK * BLK)
    w = arr(L0_tok_w).reshape(D, 3, 2, 8, 2, 8).transpose(2, 4, 1, 3, 5, 0).reshape(2, 2, D, D)
    w_a = w[:, :, :KA].reshape(4, KA, D).transpose(1, 0, 2)
    w_b = w[:, :, KA:].reshape(2, 2 * KB, D).transpose(1, 0, 2)
    wf = arr(L0_attn_Wf)
    b1 = arr(L0_ffn_b1)
    ins = {
        "xblk": img,
        "ids": arr(x_txt).reshape(4, 128).T,
        "wtok": np.concatenate([w_a, w_b], axis=1),
        "pos": arr(L0_tok_pos_embedding)[0],
        "cls": arr(L0_tok_cls_token)[0],
        "rows": np.concatenate([arr(L0_tok_b), arr(L0_ffn_gamma), arr(L0_ffn_beta), arr(L0_ffn_b2)]),
        "cols": np.concatenate([np.concatenate([arr(L0_attn_bf)] * 2)[:, None], column(arr(L0_attn_gamma)),
                                column(arr(L0_attn_beta)), arr(L0_ffn_down_b).reshape(HT, 128).T,
                                np.concatenate([b1, b1])[:128, None]], axis=1),
        "table": arr(L0_txt_W),
        "wproj": two_tiles(np.concatenate([arr(L0_attn_Wq), arr(L0_attn_Wk), wf, wf, arr(L0_attn_Wv)], axis=1)),
        "wout": two_tiles(arr(L0_attn_Wo)),
        "wr1": two_tiles(arr(L0_ffn_w1)),
        "wr2": arr(L0_ffn_w2),
        "wdown": two_tiles(arr(L0_ffn_down_w).transpose(1, 0, 2).reshape(D, NE * DH)),
        "wup": arr(L0_ffn_up_w).reshape(HT, 128, D).transpose(1, 0, 2),
    }
    nc = bacc.Bacc("TRN2", target_bir_lowering=False, num_devices=1)
    arrays, args = {}, {}
    for name, a in ins.items():
        a = np.ascontiguousarray(a)
        arrays[f"in_{name}"] = a
        args[name] = nc.dram_tensor(f"in_{name}", a.shape, mybir.dt.from_np(a.dtype), kind="ExternalInput").ap()
    res = nc.dram_tensor("tokens_out", (BATCH * L, D), mybir.dt.float32, kind="ExternalOutput").ap()
    embed_fuse_moe(nc, out=res, **args)
    r = run_bass_kernel_spmd(nc, [arrays], core_ids=[0])
    return r.results[0]["tokens_out"].reshape(BATCH, L, D)
```

```python
import concourse.bass as bass
from concourse import mybir
from contextlib import ExitStack

BATCH, D = 16, 192
GRID, BLK = 27, 28
TOK_IMG = GRID * GRID + 1
TXT = 32
L = TOK_IMG + TXT
CH = 127
NCH = L // CH
HALF = L // 2
KA, KB = 128, D - 128
M_DIM = 64
VOCAB = 8000
NPROJ = 4 * M_DIM + D
NE, DH = 8, 256
HT = NE * DH // 128
H1 = D // 2
GCH = 4
GT = GCH * CH
NG = BATCH * NCH // GCH
XW = 790
WS = 1024.0
PROB_CLAMP = 1e6 - 1.0
Z_BANKS = 4
Z_RING = 4


def embed_fuse_moe(nc, xblk, ids, wtok, pos, cls, rows, cols, table, wproj, wout, wr1, wr2, wdown, wup, out):
    fp32, fp16, i32 = mybir.dt.float32, mybir.dt.float16, mybir.dt.int32
    ALU = mybir.AluOpType
    ACT = mybir.ActivationFunctionType
    AX = mybir.AxisListType.X

    ctx = ExitStack()
    with ctx:
        def sem(name, scope=ctx):
            return scope.enter_context(nc.semaphore(name))

        def sb(name, shape, dt=fp32, scope=ctx):
            return scope.enter_context(nc.sbuf_tensor(name, shape, dt))

        def need(eng, s, value):
            if not isinstance(value, int) or value > 0:
                eng.wait_ge(s, value)

        banks = [ctx.enter_context(nc.psum_tensor(f"bank{i}", [128, 512], fp32)) for i in range(6)]
        turn_bank = ctx.enter_context(nc.psum_tensor("turn_bank", [128, 4, 2, 128], fp16))

        H = sb("H", [128, BATCH * NCH, D])
        ident = sb("ident", [128, 128])
        ident16 = sb("ident16", [CH, CH], fp16)
        minus_half = sb("minus_half", [CH, NCH])
        epsilon = sb("epsilon", [CH, NCH])
        colv = sb("colv", [128, 22])
        rowv = sb("rowv", [CH, 3 * D + NE])
        down_h = sb("down_h", [128, 2, NE * DH], fp16)
        down_l = sb("down_l", [128, 2, NE * DH], fp16)
        up_h = sb("up_h", [128, HT, D], fp16)
        up_l = sb("up_l", [128, HT, D], fp16)
        r1_h = sb("r1_h", [128, 2, H1], fp16)
        r1_l = sb("r1_l", [128, 2, H1], fp16)
        r2 = sb("r2", [H1, NE])
        forget_bias, down_b, router_b1 = colv[:, 0:1], colv[:, 5:21], colv[0:H1, 21:22]
        tok_b, ffn_gamma, ffn_beta, router_b2 = (
            rowv[:, 0:D], rowv[:, D:2 * D], rowv[:, 2 * D:3 * D], rowv[:, 3 * D:3 * D + NE])

        def has_image(n):
            return not isinstance(n, int) or n < BATCH

        rest_columns = ((slice(D, D + KB), slice(KA, D)), (slice(D + KB, 2 * D), slice(0, KA)))

        def turn_tokens(pe, dst, src):
            for c in range(2):
                for k, a in enumerate((0, D + KB, KA)):
                    mm = pe.transpose(dst[:, k, c, 0:CH], src[:, c, a:a + 128], ident16[:, :])
            return mm

        def mm_features(pe, dst, w_h, w_l, lo, hi, x_hl, x_s, c0, c1):
            pe.matmul(dst, w_h[:, 0, lo:hi], x_hl[:, 0, c0:c1], start=True, stop=False)
            pe.matmul(dst, w_h[:, 0, lo:hi], x_hl[:, 1, c0:c1], start=False, stop=False)
            pe.matmul(dst, w_l[:, 0, lo:hi], x_hl[:, 0, c0:c1], start=False, stop=False)
            pe.matmul(dst, w_h[:, 1, lo:hi], x_s[:, c0:c1], start=False, stop=False)
            return pe.matmul(dst, w_l[:, 1, lo:hi], x_s[:, c0:c1], start=False, stop=True)

        def mm_tokens(pe, dst, w_h, w_l, lo, hi, x_hl, x_s, c0):
            c1 = c0 + 128
            pe.matmul(dst, x_hl[:, 0, c0:c1], w_h[:, 0, lo:hi], start=True, stop=False)
            pe.matmul(dst, x_hl[:, 0, c0:c1], w_l[:, 0, lo:hi], start=False, stop=False)
            pe.matmul(dst, x_hl[:, 1, c0:c1], w_h[:, 0, lo:hi], start=False, stop=False)
            pe.matmul(dst, x_s[:, c0:c1], w_h[:, 1, lo:hi], start=False, stop=False)
            return pe.matmul(dst, x_s[:, c0:c1], w_l[:, 1, lo:hi], start=False, stop=True)

        route_bank = banks[1]
        g16 = sb("g16", [CH, GCH, 2 * D], fp16)
        gx_hl = [sb("gx_hl_even", [128, 2, GT], fp16)]
        gx_s = [sb("gx_s_even", [128, GT], fp16)]
        x2 = [sb("x2_even", [CH, GCH, D])]
        bstat = sb("bstat", [CH, GCH, 6])
        bmv = sb("bmv", [CH, GCH, 2])
        brstd = sb("brstd", [CH, GCH])
        bvar = sb("bvar", [CH, GCH])
        rg = sb("rg", [H1, GT])
        logit = sb("logit", [CH, GCH, NE])
        lmax = sb("lmax", [CH, GCH])

        b_var, c_var = sem("b_var"), sem("c_var")
        b_consts = sem("b_consts")
        b_stat, b_mv, b_rstd, x2_done = sem("b_stat"), sem("b_mv"), sem("b_rstd"), sem("x2_done")
        g_round, g_rest = sem("g_round"), sem("g_rest")
        gx_done, gx_main, gx_side = sem("gx_done"), sem("gx_main"), sem("gx_side")
        route1_done, route_gelu, route2_done = sem("route1_done"), sem("route_gelu"), sem("route2_done")
        logit_done, lmax_done, shift_done, expo_done = (
            sem("logit_done"), sem("lmax_done"), sem("shift_done"), sem("expo_done"))
        esum_done, einv_done, prob_done, top_done = (
            sem("esum_done"), sem("einv_done"), sem("prob_done"), sem("top_done"))
        tsum_done, weighted_done = sem("tsum_done"), sem("weighted_done")
        above_done, equal_done, rank2_done = sem("above_done"), sem("equal_done"), sem("rank2_done")
        taken_done, picked_done, tscaled_done = sem("taken_done"), sem("picked_done"), sem("tscaled_done")
        rank_done, tinv_done, share_done = sem("rank_done"), sem("tinv_done"), sem("share_done")
        z_done, z32_done, zh_done, zl_done = sem("z_done"), sem("z32_done"), sem("zh_done"), sem("zl_done")
        up_done, acc_done = sem("up_done"), sem("acc_done")
        c_stat, c_mv, c_rstd, normed = sem("c_stat"), sem("c_mv"), sem("c_rstd"), sem("normed")
        hb_done, scaled, res_done, last_res = sem("hb_done"), sem("scaled"), sem("res_done"), sem("last_res")
        stored = [sem("stored_even"), sem("stored_odd")]

        def rsqrt_b(pool, g):
            pool.wait_ge(b_mv, 4 * g + 4)
            need(pool, x2_done, 4 * g)
            pool.tensor_tensor(bvar[:, :], bmv[:, :, 1], epsilon[:, 0:GCH], ALU.add).then_inc(b_var, 1)
            pool.wait_ge(b_var, g + 1)
            pool.tensor_tensor(brstd[:, :], bvar[:, :], minus_half[:, 0:GCH], ALU.pow).then_inc(b_rstd, 1)

        def rest_b(pool, g, p):
            for half in range(2):
                k = slice(2 * half, 2 * half + 2)
                pool.wait_ge(g_round, 2 * g + half + 1)
                for cols, features in rest_columns:
                    pool.tensor_tensor(g16[:, k, cols], x2[p][:, k, features],
                                       g16[:, k, 0:D][:, :, features], ALU.subtract).then_inc(g_rest, 1)

        def round_b(act, g, p):
            for half in range(2):
                k = slice(2 * half, 2 * half + 2)
                act.wait_ge(x2_done, 4 * g + 2 * half + 2)
                need(act, gx_done, 2 * g - 1 + half)
                act.activation(g16[:, k, 0:D], x2[p][:, k, :], ACT.Copy).then_inc(g_round, 1)

        def copy_gx_main(act, g, p, half):
            act.wait_ge(gx_done, 2 * g + half + 1)
            need(act, z_done, 16 * (g - 1))
            need(act, route1_done, g - 1)
            c = 2 * CH * half
            act.activation(gx_hl[p][:, :, c:c + 2 * CH].rearrange("p h (c t) -> p h c t", c=2),
                           turn_bank[:, 0:2, :, 0:CH], ACT.Copy).then_inc(gx_main, 1)

        def gelu_router(act, g):
            act.wait_ge(route1_done, g + 1)
            need(act, route2_done, g)
            act.activation(rg[:, :], route_bank[0:H1, 0:GT], ACT.Gelu, bias=router_b1,
                           scale=1.0 / WS).then_inc(route_gelu, 1)

        def turn(pe, g, p, half):
            pe.wait_ge(g_rest, 4 * g + 2 * half + 2)
            need(pe, gx_main, 2 * g + half)
            need(pe, gx_side, 2 * g + half)
            turn_tokens(pe, turn_bank, g16[:, 2 * half:2 * half + 2, :]).then_inc(gx_done, 1)

        def route1(pe, g, p):
            pe.wait_ge(gx_main, 2 * g + 2)
            pe.wait_ge(gx_side, 2 * g + 2)
            need(pe, logit_done, g)
            mm_features(pe, route_bank[0:H1, 0:GT], r1_h, r1_l, 0, H1, gx_hl[p], gx_s[p], 0, GT)\
                .then_inc(route1_done, 1)

        def route2(pe, g):
            pe.wait_ge(route_gelu, g + 1)
            for c in range(GCH):
                mm = pe.matmul(route_bank[0:CH, NE * c:NE * c + NE], rg[:, CH * c:CH * c + CH], r2[:, :],
                               start=True, stop=True)
            mm.then_inc(route2_done, 1)

        def h_chunk(g, c):
            return H[0:CH, bass.ds(GCH * g + c, 1), :].rearrange("p c d -> p (c d)")

        def stats_b(dve, g):
            need(dve, b_rstd, g)
            need(dve, x2_done, 4 * g)
            need(dve, b_mv, 4 * g)
            dve.nop(nofuse=True)
            for c in range(GCH):
                dve.bn_stats(bstat[:, c, :], h_chunk(g, c)).then_inc(b_stat, 1)
            for c in range(GCH):
                dve.wait_ge(b_stat, 4 * g + c + 1)
                dve.nop(nofuse=True)
                dve.bn_aggr(bmv[:, c, :], bstat[:, c, :]).then_inc(b_mv, 1)

        def norm_b(dve, g, p):
            dve.wait_ge(b_rstd, g + 1)
            need(dve, gx_done, 2 * (g - 1))
            need(dve, acc_done, 32 * (g - 2) + 4)
            for c in range(GCH):
                dve.tensor_scalar(x2[p][:, c, :], h_chunk(g, c), bmv[:, c, 0:1], brstd[:, c:c + 1],
                                  ALU.subtract, ALU.mult).then_inc(x2_done, 1)

        def copy_gx_side(dve, g, p, half):
            dve.wait_ge(gx_main, 2 * g + half + 1)
            c = 2 * CH * half
            dve.tensor_copy(gx_s[p][:, c:c + 2 * CH].rearrange("p (c t) -> p c t", c=2),
                            turn_bank[:, 2, :, 0:CH]).then_inc(gx_side, 1)

        def logits(dve, g):
            dve.wait_ge(route2_done, g + 1)
            need(dve, shift_done, g)
            dve.tensor_tensor(logit[:, :, :], route_bank[0:CH, 0:GCH * NE].rearrange("p (c e) -> p c e", e=NE),
                              router_b2.unsqueeze(1).broadcast_to([CH, GCH, NE]), ALU.add).then_inc(logit_done, 1)
            dve.wait_ge(logit_done, g + 1)
            dve.tensor_reduce(lmax[:, :], logit[:, :, :], AX, ALU.max).then_inc(lmax_done, 1)

        ctxa = ExitStack()
        with ctxa:
            def sa(name, shape, dt=fp32):
                return sb(name, shape, dt, ctxa)

            def sema(name):
                return sem(name, ctxa)

            xa = sa("xa", [128, BLK * BLK])
            xb = sa("xb", [128, BLK * BLK])
            pa_h = [sa(f"pa_h{i}", [128, 2, XW], fp16) for i in range(2)]
            pa_l = [sa(f"pa_l{i}", [128, 2, XW], fp16) for i in range(2)]
            pb_h = [sa(f"pb_h{i}", [128, XW], fp16) for i in range(2)]
            pb_l = [sa(f"pb_l{i}", [128, XW], fp16) for i in range(2)]
            wt_h = sa("wt_h", [128, 6, D], fp16)
            wt_l = sa("wt_l", [128, 6, D], fp16)
            wp_h = sa("wp_h", [128, 2, NPROJ], fp16)
            wp_l = sa("wp_l", [128, 2, NPROJ], fp16)
            wo_h = sa("wo_h", [128, 2, D], fp16)
            wo_l = sa("wo_l", [128, 2, D], fp16)
            base = sa("base", [128, NCH, D])
            patch_rows = sa("patch_rows", [CH, NCH])
            causal = sa("causal", [CH, CH + M_DIM])
            gate_sign = sa("gate_sign", [128, 1])
            beta_out = sa("beta_out", [CH, D])
            idx = sa("idx", [128, 4], i32)
            idx_ok = sa("idx_ok", [128, 4])
            idx_hi = sa("idx_hi", [128, 4])
            idx_c = sa("idx_c", [128, 4], i32)
            xn = [sa(f"xn{i}", [CH, 2, D]) for i in range(2)]
            x16 = [sa(f"x16_{i}", [CH, 2, 2 * D], fp16) for i in range(2)]
            x_hl = sa("x_hl", [128, 2, L + 2], fp16)
            x_s = sa("x_s", [128, L + 2], fp16)
            stat1 = sa("stat1", [CH, NCH, 6])
            mv1 = sa("mv1", [CH, NCH, 2])
            rstd1 = sa("rstd1", [CH, NCH])
            var1 = sa("var1", [CH, NCH])
            qk = sa("qk", [128, L])
            qk_e = sa("qk_e", [128, L])
            beta_cols = qk[:, 0:2 * CH].rearrange("p (k t) -> p k t", k=2)
            badd0 = qk_e[0:CH, 0:D]
            gate = sa("gate", [128, L])
            qT = [sa(f"qT{i}", [M_DIM, L]) for i in range(2)]
            kT = [sa(f"kT{i}", [M_DIM, L]) for i in range(2)]
            v = [sa(f"v{i}", [CH, NCH, D + 1]) for i in range(2)]
            pk = [sa(f"pk{i}", [CH, CH + M_DIM]) for i in range(2)]
            state = [sa(f"state{i}", [M_DIM, D + 1]) for i in range(2)]
            num = sa("num", [CH, 2, D + 1])
            stat2 = sa("stat2", [CH, NCH, 6])
            mv2 = sa("mv2", [CH, NCH, 2])
            den = sa("den", [CH, NCH])
            den_sq = sa("den_sq", [CH, NCH])
            vn = sa("vn", [CH, NCH])
            hscale = sa("hscale", [CH, NCH])
            y = sa("y", [CH, 2, D])
            y16 = sa("y16", [CH, 2, 2 * D], fp16)
            y_hl = [sa(f"y_hl{i}", [128, 2, 256], fp16) for i in range(2)]
            y_s = [sa(f"y_s{i}", [128, 256], fp16) for i in range(2)]

            Hflat = H[:, :, :].rearrange("p c d -> p (c d)")
            at = [40 * D]

            def staged(n):
                at[0] += n
                return Hflat[:, at[0] - n:at[0]]
            raw_tok = staged(6 * D).rearrange("p (k n) -> p k n", k=6)
            raw_proj = staged(2 * NPROJ).rearrange("p (k n) -> p k n", k=2)
            raw_out = staged(2 * D).rearrange("p (k n) -> p k n", k=2)
            raw_r1 = staged(2 * H1).rearrange("p (k n) -> p k n", k=2)
            raw_down = staged(2 * NE * DH).rearrange("p (k n) -> p k n", k=2)
            raw_up = staged(HT * D).rearrange("p (k n) -> p k n", k=HT)
            txt = staged(4 * D).rearrange("p (g n) -> p g n", g=4)
            assert at[0] <= BATCH * NCH * D

            moe_parts = [(raw_r1, r1_h[:, :, :], r1_l[:, :, :])]
            for k in range(2):
                for a in (0, NE * DH // 2):
                    b = a + NE * DH // 2
                    moe_parts.append((raw_down[:, k, a:b], down_h[:, k, a:b], down_l[:, k, a:b]))
            for a, b in ((0, 5), (5, 10), (10, HT)):
                moe_parts.append((raw_up[:, a:b, :], up_h[:, a:b, :], up_l[:, a:b, :]))

            tok_bank, proj_bank, core_bank, num_bank = banks[0:2], banks[2:4], banks[4], banks[5]
            y_bank = ctxa.enter_context(nc.psum_tensor("y_bank", [128, 4, 2, 128], fp16))
            T2 = 2 * CH

            tok_loaded, proj_loaded, moe_loaded = sema("tok_loaded"), sema("proj_loaded"), sema("moe_loaded")
            small_loaded, pos_loaded, ids_loaded = sema("small_loaded"), sema("pos_loaded"), sema("ids_loaded")
            txt_gathered, txt_first, txt_others = sema("txt_gathered"), sema("txt_first"), sema("txt_others")
            ident_set, consts_set = sema("ident_set"), sema("consts_set")
            base_set, ids_set = sema("base_set"), sema("ids_set")
            txt_masked, pads_set, cols_set = sema("txt_masked"), sema("pads_set"), sema("cols_set")
            tok_split, proj_split = sema("tok_split"), sema("proj_split")
            moe_scaled, moe_hi, moe_lo = sema("moe_scaled"), sema("moe_hi"), sema("moe_lo")
            beta_mm, beta_set = sema("beta_mm"), sema("beta_set")
            pix_loaded, pix_hi, pix_lo = sema("pix_loaded"), sema("pix_hi"), sema("pix_lo")
            patch_done, patch_added = sema("patch_done"), sema("patch_added")
            ln1_stat, ln1_mv, ln1_rstd, xn_done = sema("ln1_stat"), sema("ln1_mv"), sema("ln1_rstd"), sema("xn_done")
            ln1_var = sema("ln1_var")
            h_biased = sema("h_biased")
            x_round, x_rest, y_round, y_rest = sema("x_round"), sema("x_rest"), sema("y_round"), sema("y_rest")
            xt_done, xt_main, xt_side = sema("xt_done"), sema("xt_main"), sema("xt_side")
            proj_done, proj_out = sema("proj_done"), sema("proj_out")
            f_clamped, f_logged, f_summed, f_clipped, gate_done = (
                sema("f_clamped"), sema("f_logged"), sema("f_summed"), sema("f_clipped"), sema("gate_done"))
            qk_relu_done, qk_exp, qk_elu, q_done, k_done = (
                sema("qk_relu_done"), sema("qk_exp"), sema("qk_elu"), sema("q_done"), sema("k_done"))
            core_done, pk_done, state_done = sema("core_done"), sema("pk_done"), sema("state_done")
            num_done, num_out = sema("num_done"), sema("num_out")
            ln2_stat, ln2_mv, den_scaled, den_squared = (
                sema("ln2_stat"), sema("ln2_mv"), sema("den_scaled"), sema("den_squared"))
            ln2_var, ln2_scale, y_done = sema("ln2_var"), sema("ln2_scale"), sema("y_done")
            yt_done, yt_main, yt_side = sema("yt_done"), sema("yt_main"), sema("yt_side")
            out_done, h_done = sema("out_done"), sema("h_done")

            block = ctxa.enter_context(nc.Block())

            @block.sync
            def _(sp):
                def load_image(n):
                    need(sp, pix_lo, 3 * n)
                    sp.dma_start(xa[:, :], xblk[n, 0:KA, :]).then_inc(pix_loaded, 16)
                    sp.dma_start(xb[0:KB, :], xblk[n, KA:D, :]).then_inc(pix_loaded, 16)
                    sp.dma_start(xb[KB:128, 0:BLK * BLK - 1], xblk[n, KA:D, 1:BLK * BLK]).then_inc(pix_loaded, 16)

                def place_text(b, placed):
                    q = TXT * (b % 4)
                    sp.dma_start(H[CH - TXT:CH, NCH * b + NCH - 1, :], txt[q:q + TXT, b // 4, :]).then_inc(placed, 16)

                sp.dma_start(idx[:, :], ids).then_inc(ids_loaded, 16)
                load_image(0)
                sp.dma_start(raw_proj, wproj).then_inc(proj_loaded, 16)
                sp.dma_start(raw_out, wout).then_inc(proj_loaded, 16)
                load_image(1)
                sp.wait_ge(txt_masked, 4)
                for b in range(6):
                    place_text(b, txt_first)
                load_image(2)
                sp.dma_start(raw_r1, wr1).then_inc(moe_loaded, 16)
                sp.dma_start(raw_down, wdown).then_inc(moe_loaded, 16)
                sp.dma_start(raw_up, wup).then_inc(moe_loaded, 16)
                load_image(3)
                load_image(4)
                load_image(5)
                load_image(6)
                sp.wait_ge(tok_split, 2)
                sp.wait_ge(proj_split, 6)
                sp.wait_ge(moe_lo, 8)
                for b in range(6, BATCH):
                    place_text(b, txt_others)
                with sp.Fori(7, BATCH) as n:
                    load_image(n)

            @block.gpsimd
            def _(pool):
                pool.memset(ident[:, :], 0.0).then_inc(ident_set, 1)
                pool.wait_ge(ident_set, 1)
                pool.affine_select(out=ident[:, :], in_=ident[:, :], compare_op=ALU.not_equal, fill=1.0,
                                   base=0, pattern=[[-1, 128]], channel_multiplier=1).then_inc(ident_set, 1)
                pool.wait_ge(ident_set, 2)
                pool.tensor_copy(ident16[:, :], ident[0:CH, 0:CH]).then_inc(ident_set, 1)
                pool.wait_ge(ids_set, 5)
                for g in range(4):
                    pool.indirect_dma_start(out=txt[:, g, :], out_offset=None, in_=table,
                                            in_offset=bass.IndirectOffsetOnAxis(ap=idx_c[:, g:g + 1], axis=0),
                                            bounds_check=VOCAB - 1, oob_is_err=False).then_inc(txt_gathered, 16)
                for i in range(2):
                    for buf in (pa_h[i], pa_l[i]):
                        pool.memset(buf[:, :, 0:1], 0.0).then_inc(pads_set, 1)
                        pool.memset(buf[:, :, 1 + BLK * GRID:XW], 0.0).then_inc(pads_set, 1)
                    for buf in (pb_h[i], pb_l[i]):
                        pool.memset(buf[:, 0:1], 0.0).then_inc(pads_set, 1)
                        pool.memset(buf[:, 1 + BLK * GRID:XW], 0.0).then_inc(pads_set, 1)
                    pool.memset(y_hl[i][:, :, T2:256], 0.0).then_inc(pads_set, 1)
                    pool.memset(y_s[i][:, T2:256], 0.0).then_inc(pads_set, 1)
                    pool.memset(v[i][:, :, D:D + 1], 1.0).then_inc(pads_set, 1)
                pool.memset(x_hl[:, :, L:L + 2], 0.0).then_inc(pads_set, 1)
                pool.memset(x_s[:, L:L + 2], 0.0).then_inc(pads_set, 1)
                pool.memset(patch_rows[:, :], 1.0 / WS).then_inc(consts_set, 1)
                pool.memset(causal[:, :], 1.0).then_inc(consts_set, 1)
                pool.memset(minus_half[:, :], -0.5).then_inc(consts_set, 1)
                pool.memset(epsilon[:, :], 1e-5).then_inc(consts_set, 1)
                pool.memset(gate_sign[:, :], 1.0).then_inc(consts_set, 1)
                pool.memset(beta_cols[:, :, :], 0.0).then_inc(consts_set, 1)
                pool.wait_ge(consts_set, 6)
                pool.affine_select(out=patch_rows[:, 0:1], in_=patch_rows[:, 0:1], compare_op=ALU.is_ge, fill=0.0,
                                   base=-1, pattern=[[0, 1]], channel_multiplier=1).then_inc(consts_set, 1)
                pool.affine_select(out=gate_sign[:, :], in_=gate_sign[:, :], compare_op=ALU.is_ge, fill=-1.0,
                                   base=-M_DIM, pattern=[[0, 1]], channel_multiplier=1).then_inc(consts_set, 1)
                pool.affine_select(out=causal[:, 0:CH], in_=causal[:, 0:CH], compare_op=ALU.is_ge, fill=0.0,
                                   base=0, pattern=[[1, CH]], channel_multiplier=-1).then_inc(consts_set, 1)

                def split_pixels_lo(n, p, k):
                    pool.wait_ge(pix_hi, 3 * n + k + 1)
                    if k < 2:
                        src = xa[:, :].rearrange("p (r c) -> p r c", c=BLK)[:, :, k:k + GRID]
                        hi, lo = pa_h[p][:, k, 1:1 + BLK * GRID], pa_l[p][:, k, 1:1 + BLK * GRID]
                    else:
                        src = xb[:, :].rearrange("p (r c) -> p r c", c=BLK)[:, :, 0:GRID]
                        hi, lo = pb_h[p][:, 1:1 + BLK * GRID], pb_l[p][:, 1:1 + BLK * GRID]
                    hi, lo = hi.rearrange("p (r c) -> p r c", c=GRID), lo.rearrange("p (r c) -> p r c", c=GRID)
                    pool.tensor_tensor(lo, src, hi, ALU.subtract).then_inc(pix_lo, 1)

                split_pixels_lo(0, 0, 1)

                def rsqrt1(n, q):
                    pool.wait_ge(ln1_mv, 6 * n + 2 * q + 2)
                    need(pool, xn_done, 6 * n)
                    s = slice(2 * q, 2 * q + 2)
                    pool.tensor_tensor(var1[:, s], mv1[:, s, 1], epsilon[:, s], ALU.add).then_inc(ln1_var, 1)
                    pool.wait_ge(ln1_var, 3 * n + q + 1)
                    pool.tensor_tensor(rstd1[:, s], var1[:, s], minus_half[:, s], ALU.pow).then_inc(ln1_rstd, 1)

                def bias_h(n, q):
                    pool.wait_ge(xn_done, 6 * n + 2 * q + 2)
                    if isinstance(n, int) and n == 0:
                        pool.wait_ge(beta_set, 1)
                    c = 6 * n + 2 * q
                    pool.tensor_tensor(H[0:CH, bass.ds(c, 2), :], H[0:CH, bass.ds(c, 2), :],
                                       beta_out[:, :].unsqueeze(1).broadcast_to([CH, 2, D]), ALU.add)\
                        .then_inc(h_biased, 1)

                def scale2(n, q):
                    s = slice(2 * q, 2 * q + 2)
                    m = 3 * n + q
                    pool.wait_ge(den_scaled, m + 1)
                    need(pool, ln2_var, 3 * n)
                    pool.tensor_tensor(den_sq[:, s], den[:, s], den[:, s], ALU.mult).then_inc(den_squared, 1)
                    pool.wait_ge(ln2_mv, 2 * m + 2)
                    need(pool, ln2_scale, 3 * n)
                    pool.wait_ge(den_squared, m + 1)
                    pool.tensor_tensor(vn[:, s], mv2[:, s, 1], den_sq[:, s], ALU.add).then_inc(ln2_var, 1)
                    pool.wait_ge(ln2_var, m + 1)
                    need(pool, y_done, 6 * n)
                    pool.tensor_tensor(hscale[:, s], vn[:, s], minus_half[:, s], ALU.pow).then_inc(ln2_scale, 1)

                def rest(src, dst, wait, n, done):
                    pool.wait_ge(wait, n + 1)
                    for cols, features in rest_columns:
                        pool.tensor_tensor(dst[:, :, cols], src[:, :, features], dst[:, :, 0:D][:, :, features],
                                           ALU.subtract).then_inc(done, 1)

                def rest_x(n, p, q):
                    i = (3 * p + q) % 2
                    rest(xn[i], x16[i], x_round, 3 * n + q, x_rest)

                def rest_y(n, q):
                    rest(y, y16, y_round, 3 * n + q, y_rest)

                def mixed(n, p, front, back, extra={}):
                    m, r = n + 1, 1 - p

                    def other(place):
                        if place in extra:
                            extra[place]()

                    if front:
                        rsqrt1(m, 0)
                    other("rsqrt 0")
                    if back:
                        bias_h(n, 2)
                    if front:
                        rest_x(m, r, 0)
                    if back and has_image(n + 2):
                        split_pixels_lo(n + 2, p, 2)
                    if front:
                        bias_h(m, 0)
                        rsqrt1(m, 1)
                    other("rsqrt 1")
                    if back:
                        scale2(n, 0)
                    if front:
                        rest_x(m, r, 1)
                    if back:
                        rest_y(n, 0)
                    if front:
                        rsqrt1(m, 2)
                    other("rsqrt 2")
                    if back:
                        scale2(n, 1)
                    if front:
                        rest_x(m, r, 2)
                    if back:
                        rest_y(n, 1)
                    if front:
                        bias_h(m, 1)
                    if back:
                        scale2(n, 2)
                    if has_image(n + 3):
                        split_pixels_lo(n + 3, r, 0)
                    if back:
                        rest_y(n, 2)
                    other("rest 2")
                    if has_image(n + 3):
                        split_pixels_lo(n + 3, r, 1)
                    other("end")

                def moe_low(k):
                    src, hi, lo = moe_parts[k]
                    pool.wait_ge(moe_hi, k + 1)
                    pool.tensor_tensor(lo, src, hi, ALU.subtract).then_inc(moe_lo, 1)

                pool.wait_ge(consts_set, 9)
                mixed(-1, 1, True, False, {"rsqrt 0": lambda: split_pixels_lo(1, 1, 0),
                                           "rsqrt 1": lambda: split_pixels_lo(1, 1, 1),
                                           "rsqrt 2": lambda: split_pixels_lo(1, 1, 2)})
                for n in range(4):
                    mixed(n, n % 2, True, True, {"rest 2": lambda: moe_low(2 * n), "end": lambda: moe_low(2 * n + 1)})
                with pool.Fori(2, BATCH // 2 - 2) as pair_of:
                    n = pair_of * 2
                    mixed(n, 0, True, True)
                    mixed(n + 1, 1, True, True)
                for n in range(BATCH - 4, BATCH - 1):
                    mixed(n, n % 2, True, True)

                mixed(BATCH - 1, 1, False, True, {"rsqrt 0": lambda: rsqrt_b(pool, 0),
                                                  "rsqrt 1": lambda: rest_b(pool, 0, 0)})

            @block.scalar
            def _(act):
                act.preload_act_table_set("natural_log_exp_and_others")
                act.dma_start(raw_tok, wtok).then_inc(tok_loaded, 16)
                act.dma_start(rowv[:, :], rows.partition_broadcast(CH)).then_inc(small_loaded, 16)
                act.dma_start(colv[:, :], cols).then_inc(small_loaded, 16)
                act.dma_start(badd0[0:1, :], cls).then_inc(pos_loaded, 16)
                act.dma_start(badd0[1:CH, :], rows[0:D].partition_broadcast(CH - 1)).then_inc(pos_loaded, 16)
                act.dma_start(base[0:CH, 0:5, :], pos[0:5 * CH, :].rearrange("(c p) d -> p c d", p=CH))\
                    .then_inc(pos_loaded, 16)
                act.dma_start(base[0:CH - TXT, 5, :], pos[5 * CH:TOK_IMG, :]).then_inc(pos_loaded, 16)
                act.dma_start(r2[:, :], wr2).then_inc(moe_loaded, 16)

                def split_pixels_hi(n, p, k):
                    pix_src = (xa if k < 2 else xb)[:, :]
                    dx = k if k < 2 else 0
                    dst = pa_h[p][:, k, 1:1 + BLK * GRID] if k < 2 else pb_h[p][:, 1:1 + BLK * GRID]
                    if k == 0:
                        act.wait_ge(pix_loaded, 48 * n + 48)
                        need(act, patch_done, 6 * (n - 1))
                    act.activation(dst.rearrange("p (r c) -> p r c", c=GRID),
                                   pix_src.rearrange("p (r c) -> p r c", c=BLK)[:, :, dx:dx + GRID],
                                   ACT.Copy).then_inc(pix_hi, 1)

                act.wait_ge(tok_loaded, 16)
                act.activation(wt_h[:, :, :], raw_tok, ACT.Copy, scale=WS).then_inc(tok_split, 1)
                for k in range(3):
                    split_pixels_hi(0, 0, k)
                act.wait_ge(proj_loaded, 32)
                act.activation(wp_h[:, :, :], raw_proj, ACT.Copy, scale=WS).then_inc(proj_split, 1)
                act.wait_ge(cols_set, 1)
                for k in range(2):
                    act.activation(wo_h[:, k, :], raw_out[:, k, :], ACT.Copy, scale=colv[:, 1 + k:2 + k])\
                        .then_inc(proj_split, 1)

                def round_x(n, p, q):
                    i = (3 * p + q) % 2
                    act.wait_ge(xn_done, 6 * n + 2 * q + 2)
                    need(act, xt_done, 3 * n + q - 1)
                    act.activation(x16[i][:, :, 0:D], xn[i][:, :, :], ACT.Copy).then_inc(x_round, 1)

                def round_y(n, q):
                    act.wait_ge(y_done, 6 * n + 2 * q + 2)
                    need(act, yt_done, 3 * n + q)
                    act.activation(y16[:, :, 0:D], y[:, :, :], ACT.Copy).then_inc(y_round, 1)

                def copy_x_main(n, q):
                    act.wait_ge(xt_done, 3 * n + q + 1)
                    need(act, proj_done, 7 * n)
                    c = T2 * q
                    act.activation(x_hl[:, :, c:c + T2].rearrange("p h (c t) -> p h c t", c=2),
                                   turn_bank[:, 0:2, :, 0:CH], ACT.Copy).then_inc(xt_main, 1)

                def copy_y_main(n, p, q):
                    m = 3 * n + q
                    i = (3 * p + q) % 2
                    act.wait_ge(yt_done, m + 1)
                    need(act, out_done, m - 1)
                    act.activation(y_hl[i][:, :, 0:T2].rearrange("p h (c t) -> p h c t", c=2),
                                   y_bank[:, 0:2, :, 0:CH], ACT.Copy).then_inc(yt_main, 1)

                def num_copy(n, q):
                    act.wait_ge(num_done, 6 * n + 2 * q + 2)
                    need(act, y_done, 2 * (3 * n + q))
                    act.activation(num[:, :, :], num_bank[0:CH, 0:2 * (D + 1)].rearrange("p (c d) -> p c d", c=2),
                                   ACT.Copy).then_inc(num_out, 1)

                def take_qk(n, half):
                    s = slice(HALF * half, HALF * half + HALF)
                    act.wait_ge(proj_done, 7 * n + 2 * half + 1)
                    if half == 0:
                        need(act, qk_elu, n)
                    act.activation(qk[:, s], proj_bank[0][:, 0:HALF], ACT.Copy, scale=1.0 / WS).then_inc(proj_out, 1)

                def take_f(n, half):
                    s = slice(HALF * half, HALF * half + HALF)
                    act.wait_ge(proj_done, 7 * n + 2 * half + 2)
                    if half == 0:
                        need(act, q_done, 2 * n)
                        need(act, k_done, 2 * n)
                    act.activation(gate[:, s], proj_bank[1][:, 0:HALF], ACT.Exp, bias=forget_bias, scale=-1.0 / WS)\
                        .then_inc(proj_out, 1)

                def take_v(n, p, q):
                    act.wait_ge(proj_done, 7 * n + 5 + q)
                    if q == 0:
                        need(act, num_done, 6 * (n - 1))
                    act.activation(v[p][:, 2 * q:2 * q + 2, 0:D],
                                   proj_bank[q // 2][0:CH, 0:2 * D].rearrange("p (c d) -> p c d", c=2),
                                   ACT.Copy, scale=1.0 / WS).then_inc(proj_out, 1)

                def relu_qk(n):
                    act.wait_ge(proj_out, 7 * n + 4)
                    need(act, q_done, 2 * n)
                    need(act, k_done, 2 * n)
                    act.activation(qk_e[:, :], qk[:, :], ACT.Relu, scale=-1.0).then_inc(qk_relu_done, 1)

                def log_forget(n):
                    act.wait_ge(f_clamped, n + 1)
                    act.activation(gate[:, :], gate[:, :], ACT.Ln, bias=1.0).then_inc(f_logged, 1)

                def exp_qk(n):
                    act.wait_ge(qk_relu_done, n + 1)
                    act.activation(qk_e[:, :], qk_e[:, :], ACT.Exp, scale=-1.0).then_inc(qk_exp, 1)

                def gates(n):
                    act.wait_ge(f_clipped, n + 1)
                    act.activation(gate[:, :], gate[:, :], ACT.Exp, scale=gate_sign[:, 0:1]).then_inc(gate_done, 1)

                def mixed(n, p, front, back, before, extra=None):
                    part = (lambda k: extra(4 * n + k)) if extra else (lambda k: None)
                    m, r = n + 1, 1 - p
                    if back and has_image(n + 2):
                        split_pixels_hi(n + 2, p, 2)
                    if before:
                        copy_y_main(n - 1, r, 2)
                    if front:
                        round_x(m, r, 0)
                    part(0)
                    if back:
                        num_copy(n, 0)
                    part(1)
                    if front:
                        copy_x_main(m, 0)
                        round_x(m, r, 1)
                    part(2)
                    if back:
                        round_y(n, 0)
                    if front:
                        copy_x_main(m, 1)
                    if back:
                        num_copy(n, 1)
                        copy_y_main(n, p, 0)
                    part(3)
                    if front:
                        round_x(m, r, 2)
                    if back and has_image(n + 3):
                        split_pixels_hi(n + 3, r, 0)
                    if back:
                        round_y(n, 1)
                    if front:
                        take_qk(m, 0)
                    if back:
                        num_copy(n, 2)
                    if front:
                        copy_x_main(m, 2)
                        take_f(m, 0)
                    if back:
                        copy_y_main(n, p, 1)
                    if front:
                        take_qk(m, 1)
                        take_f(m, 1)
                        take_v(m, r, 0)
                        log_forget(m)
                    if back:
                        round_y(n, 2)
                    if front:
                        relu_qk(m)
                        exp_qk(m)
                        gates(m)
                        take_v(m, r, 1)
                        take_v(m, r, 2)
                    if not back:
                        split_pixels_hi(n + 3, r, 0)
                    if has_image(n + 3):
                        split_pixels_hi(n + 3, r, 1)

                def moe_high(k):
                    src, hi = moe_parts[k][0:2]
                    act.activation(src, src, ACT.Copy, scale=WS).then_inc(moe_scaled, 1)
                    act.wait_ge(moe_scaled, k + 1)
                    act.activation(hi, src, ACT.Copy).then_inc(moe_hi, 1)

                act.wait_ge(consts_set, 9)
                act.wait_ge(cols_set, 2)
                for k in range(3):
                    split_pixels_hi(1, 1, k)
                mixed(-1, 1, True, False, False)
                act.wait_ge(moe_loaded, 64)
                for n in range(4):
                    mixed(n, n % 2, True, True, n > 0, lambda k: moe_high(k // 2) if k % 2 else None)
                with act.Fori(2, BATCH // 2 - 2) as pair_of:
                    n = pair_of * 2
                    mixed(n, 0, True, True, True)
                    mixed(n + 1, 1, True, True, True)
                for n in range(BATCH - 4, BATCH - 1):
                    mixed(n, n % 2, True, True, True)

                def first_group(k):
                    if k % 4 == 0:
                        round_b(act, 0, 0)
                    if k % 4 == 2:
                        copy_gx_main(act, 0, 0, 0)
                    if k % 4 == 3:
                        copy_gx_main(act, 0, 0, 1)

                mixed(BATCH - 1, 1, False, True, True, first_group)
                gelu_router(act, 0)
                copy_y_main(BATCH - 1, 1, 2)

            @block.tensor
            def _(pe):
                def patch(n, p, c):
                    if c % 2 == 0:
                        pe.wait_ge(pix_lo, 3 * n + 3)
                    need(pe, patch_added, 6 * n + c - 1)
                    dst = tok_bank[c % 2][:, 0:D]
                    k = 0
                    for t in range(6):
                        dy = t // 2 if t < 4 else t - 4
                        a = CH * c + GRID * dy
                        if t < 4:
                            hi, lo = pa_h[p][:, t % 2, a:a + 128], pa_l[p][:, t % 2, a:a + 128]
                        else:
                            hi, lo = pb_h[p][:, a:a + 128], pb_l[p][:, a:a + 128]
                        for x, w in ((hi, wt_h), (hi, wt_l), (lo, wt_h)):
                            mm = pe.matmul(dst, x, w[:, t, :], start=(k == 0), stop=(k == 17))
                            k += 1
                    mm.then_inc(patch_done, 1)

                def turn_x(n, p, q):
                    pe.wait_ge(x_rest, 2 * (3 * n + q) + 2)
                    need(pe, xt_main, 3 * n + q)
                    need(pe, xt_side, 3 * n + q)
                    turn_tokens(pe, turn_bank, x16[(3 * p + q) % 2]).then_inc(xt_done, 1)

                def turn_y(n, q):
                    pe.wait_ge(y_rest, 2 * (3 * n + q) + 2)
                    need(pe, yt_main, 3 * n + q)
                    need(pe, yt_side, 3 * n + q)
                    turn_tokens(pe, y_bank, y16).then_inc(yt_done, 1)

                def proj_qk_f(n, half, js=(0, 1)):
                    if isinstance(n, int) and n == 0 and half == 0:
                        pe.wait_ge(proj_split, 6)
                        pe.wait_ge(beta_set, 1)
                    pe.wait_ge(xt_main, 3 * n + 2 + half)
                    pe.wait_ge(xt_side, 3 * n + 2 + half)
                    for j in js:
                        if half == 0:
                            need(pe, h_done, 3 * (n - 1) + j)
                        else:
                            pe.wait_ge(proj_out, 7 * n + j + 1)
                        mm_features(pe, proj_bank[j][:, 0:HALF], wp_h, wp_l, 128 * j, 128 * j + 128,
                                    x_hl, x_s, HALF * half, HALF * half + HALF).then_inc(proj_done, 1)

                def proj_v(n, qs):
                    for q in qs:
                        if q < 2:
                            pe.wait_ge(proj_out, 7 * n + (3, 5)[q])
                        elif isinstance(n, int) and n == 0:
                            pe.wait_ge(proj_out, 4)
                        else:
                            pe.wait_ge(h_done, 3 * (n - 1) + 2)
                        for c in range(2):
                            mm = mm_tokens(pe, proj_bank[q // 2][:, D * c:D * c + D], wp_h, wp_l,
                                           4 * M_DIM, NPROJ, x_hl, x_s, CH * (2 * q + c))
                        mm.then_inc(proj_done, 1)

                def core(n, p, c):
                    if c % 3 == 0:
                        pe.wait_ge(q_done, 2 * n + c // 3 + 1)
                        pe.wait_ge(k_done, 2 * n + c // 3 + 1)
                    need(pe, pk_done, 6 * n + c)
                    need(pe, state_done, 5 * n + max(c - 1, 0))
                    if c > 0:
                        if c == 1:
                            pe.wait_ge(proj_out, 7 * n + 7)
                        pe.matmul(core_bank[0:M_DIM, 256:256 + D + 1], pk[(c - 1) % 2][:, CH:CH + M_DIM],
                                  v[p][:, c - 1, :], start=True, stop=True)
                    s = slice(CH * c, CH * c + CH)
                    pe.matmul(core_bank[0:CH, 0:CH], kT[p][:, s], qT[p][:, s], start=True, stop=True)
                    pe.transpose(core_bank[0:CH, CH:CH + M_DIM], kT[p][:, s], ident[0:M_DIM, 0:M_DIM])\
                        .then_inc(core_done, 1)

                def numer(n, p, c):
                    pe.wait_ge(pk_done, 6 * n + c + 1)
                    if c == 0:
                        pe.wait_ge(proj_out, 7 * n + 7)
                    if c % 2 == 0:
                        need(pe, num_out, 3 * n + c // 2)
                    dst = num_bank[0:CH, (D + 1) * (c % 2):(D + 1) * (c % 2 + 1)]
                    mm = pe.matmul(dst, pk[c % 2][:, 0:CH], v[p][:, c, :], start=True, stop=(c == 0))
                    if c > 0:
                        pe.wait_ge(state_done, 5 * n + c)
                        mm = pe.matmul(dst, qT[p][:, CH * c:CH * c + CH], state[c % 2][:, :], start=False, stop=True)
                    mm.then_inc(num_done, 1)

                def project_out(n, p, q, bank):
                    i = (3 * p + q) % 2
                    pe.wait_ge(yt_main, 3 * n + q + 1)
                    pe.wait_ge(yt_side, 3 * n + q + 1)
                    for c in range(2):
                        mm = mm_tokens(pe, bank[:, D * c:D * c + D], wo_h, wo_l, 0, D,
                                       y_hl[i], y_s[i], CH * c)
                    mm.then_inc(out_done, 1)

                def beta_product():
                    pe.wait_ge(cols_set, 4)
                    pe.wait_ge(proj_loaded, 32)
                    pe.matmul(num_bank[0:CH, 0:D], beta_cols[:, 0, :], raw_out[:, 0, :], start=True, stop=False)
                    pe.matmul(num_bank[0:CH, 0:D], beta_cols[0:KB, 1, :], raw_out[0:KB, 1, :], start=False, stop=True)\
                        .then_inc(beta_mm, 1)

                def mixed(n, p, front, back, before):
                    m, r = n + 1, 1 - p
                    if front:
                        patch(m, r, 0)
                        patch(m, r, 1)
                    if before:
                        turn_y(n - 1, 2)
                    if back:
                        core(n, p, 0)
                    if front:
                        patch(m, r, 2)
                    if before:
                        pe.wait_ge(proj_out, 7 * n + 6)
                        project_out(n - 1, r, 2, proj_bank[0])
                    if back:
                        core(n, p, 1)
                        numer(n, p, 0)
                    else:
                        beta_product()
                    if front:
                        patch(m, r, 3)
                    if back:
                        core(n, p, 2)
                        numer(n, p, 1)
                    if front:
                        patch(m, r, 4)
                        turn_x(m, r, 0)
                    if not front:
                        pe.wait_ge(xt_main, 3 * BATCH)
                        pe.wait_ge(xt_side, 3 * BATCH)
                        turn(pe, 0, 0, 0)
                    if back:
                        core(n, p, 3)
                        numer(n, p, 2)
                    if not front:
                        turn(pe, 0, 0, 1)
                    if front:
                        patch(m, r, 5)
                    if back:
                        core(n, p, 4)
                    if front:
                        turn_x(m, r, 1)
                    if back:
                        numer(n, p, 3)
                        turn_y(n, 0)
                        core(n, p, 5)
                        if not front:
                            pe.wait_ge(patch_added, 6 * BATCH)
                            pe.wait_ge(moe_hi, 8)
                            pe.wait_ge(moe_lo, 8)
                            route1(pe, 0, 0)
                        pe.wait_ge(proj_out, 7 * n + 7)
                        numer(n, p, 4)
                        project_out(n, p, 0, proj_bank[1])
                        numer(n, p, 5)
                    if front:
                        proj_qk_f(m, 0, (0,))
                        turn_x(m, r, 2)
                        proj_qk_f(m, 0, (1,))
                    if back:
                        turn_y(n, 1)
                    if front:
                        proj_qk_f(m, 1)
                        proj_v(m, (0,))
                        if back:
                            pe.wait_ge(proj_out, 7 * m + 4)
                            project_out(n, p, 1, proj_bank[1])
                        proj_v(m, (1, 2))
                    else:
                        pe.wait_ge(h_done, 3 * n + 1)
                        project_out(n, p, 1, proj_bank[1])

                pe.wait_ge(ident_set, 3)
                pe.wait_ge(tok_split, 2)
                pe.wait_ge(pads_set, 24)
                mixed(-1, 1, True, False, False)
                mixed(0, 0, True, True, False)
                mixed(1, 1, True, True, True)
                with pe.Fori(1, BATCH // 2 - 1) as pair_of:
                    n = pair_of * 2
                    mixed(n, 0, True, True, True)
                    mixed(n + 1, 1, True, True, True)
                mixed(BATCH - 2, 0, True, True, True)
                mixed(BATCH - 1, 1, False, True, True)
                turn_y(BATCH - 1, 2)
                pe.wait_ge(h_done, 3 * BATCH - 3)
                project_out(BATCH - 1, 1, 2, proj_bank[0])
                route2(pe, 0)

            @block.vector
            def _(dve):
                dve.wait_ge(ids_loaded, 16)
                dve.tensor_scalar(idx_ok[:, :], idx[:, :], 0.0, None, ALU.is_ge).then_inc(ids_set, 1)
                dve.tensor_scalar(idx_hi[:, :], idx[:, :], float(VOCAB - 1), None, ALU.is_le).then_inc(ids_set, 1)
                dve.tensor_scalar(idx_c[:, :], idx[:, :], 0.0, float(VOCAB - 1), ALU.max, ALU.min).then_inc(ids_set, 1)
                dve.wait_ge(ids_set, 3)
                dve.tensor_tensor(idx_ok[:, :], idx_ok[:, :], idx_hi[:, :], ALU.mult).then_inc(ids_set, 2)
                def split_pixels_lo(n, p, k):
                    dve.wait_ge(pix_hi, 3 * n + k + 1)
                    src = (xa if k < 2 else xb)[:, :].rearrange("p (r c) -> p r c", c=BLK)
                    hi, lo = (pa_h[p][:, k, :], pa_l[p][:, k, :]) if k < 2 else (pb_h[p][:, :], pb_l[p][:, :])
                    dx = k if k < 2 else 0
                    dve.tensor_tensor(lo[:, 1:1 + BLK * GRID].rearrange("p (r c) -> p r c", c=GRID),
                                      src[:, :, dx:dx + GRID],
                                      hi[:, 1:1 + BLK * GRID].rearrange("p (r c) -> p r c", c=GRID),
                                      ALU.subtract).then_inc(pix_lo, 1)

                dve.wait_ge(tok_split, 1)
                dve.scalar_tensor_tensor(out=wt_l[:, :, :].rearrange("p k n -> p (k n)"),
                                         in0=raw_tok.rearrange("p k n -> p (k n)"), scalar=WS,
                                         in1=wt_h[:, :, :].rearrange("p k n -> p (k n)"), op0=ALU.mult,
                                         op1=ALU.subtract).then_inc(tok_split, 1)
                for k in (0, 2):
                    split_pixels_lo(0, 0, k)

                dve.wait_ge(small_loaded, 32)
                dve.wait_ge(consts_set, 6)
                dve.tensor_scalar(colv[:, 1:3], colv[:, 1:3], WS, None, ALU.mult).then_inc(cols_set, 1)
                dve.tensor_scalar(colv[:, 0:1], colv[:, 0:1], -1.0, None, ALU.mult).then_inc(cols_set, 1)
                for k in range(2):
                    dve.tensor_scalar(beta_cols[:, k, :], beta_cols[:, k, :], colv[:, 3 + k:4 + k], None, ALU.add)\
                        .then_inc(cols_set, 1)
                dve.wait_ge(pos_loaded, 64)
                dve.tensor_tensor(base[0:CH, 0, :], base[0:CH, 0, :], badd0[:, :], ALU.add).then_inc(base_set, 1)
                dve.tensor_tensor(base[0:CH, 1:5, :], base[0:CH, 1:5, :],
                                  tok_b.unsqueeze(1).broadcast_to([CH, 4, D]), ALU.add).then_inc(base_set, 1)
                dve.tensor_tensor(base[0:CH - TXT, 5, :], base[0:CH - TXT, 5, :], tok_b[0:CH - TXT, :], ALU.add)\
                    .then_inc(base_set, 1)
                dve.wait_ge(txt_gathered, 64)
                dve.wait_ge(ids_set, 5)
                for g in range(4):
                    dve.tensor_scalar(txt[:, g, :], txt[:, g, :], idx_ok[:, g:g + 1], None, ALU.mult)\
                        .then_inc(txt_masked, 1)

                def prepare_projections():
                    dve.wait_ge(proj_split, 3)
                    dve.scalar_tensor_tensor(out=wp_l[:, :, :], in0=raw_proj, scalar=WS, in1=wp_h[:, :, :], op0=ALU.mult,
                                             op1=ALU.subtract).then_inc(proj_split, 1)
                    dve.wait_ge(cols_set, 1)
                    for k in range(2):
                        dve.scalar_tensor_tensor(out=wo_l[:, k, :], in0=raw_out[:, k, :], scalar=colv[:, 1 + k:2 + k],
                                                 in1=wo_h[:, k, :], op0=ALU.mult, op1=ALU.subtract)\
                            .then_inc(proj_split, 1)

                def h_add(n, c):
                    dve.wait_ge(patch_done, 6 * n + c + 1)
                    rows_of = CH if c < 5 else CH - TXT
                    dst = H[0:rows_of, bass.ds(6 * n + c, 1), :].rearrange("p c d -> p (c d)")
                    dve.scalar_tensor_tensor(out=dst, in0=tok_bank[c % 2][0:rows_of, 0:D],
                                             scalar=patch_rows[0:rows_of, c:c + 1],
                                             in1=base[0:rows_of, c, :], op0=ALU.mult, op1=ALU.add).then_inc(patch_added, 1)

                def h_stat(n, c):
                    dve.wait_ge(patch_added, 6 * n + c + 1)
                    if c == 5 and isinstance(n, int) and n < 5:
                        dve.wait_ge(txt_first, 16 * 6)
                    elif c == 5:
                        dve.wait_ge(txt_others, 16 * (BATCH - 6))
                    need(dve, ln1_mv, 6 * n)
                    dve.nop(nofuse=True)
                    dve.bn_stats(stat1[:, c, :], H[0:CH, bass.ds(6 * n + c, 1), :].rearrange("p c d -> p (c d)"))\
                        .then_inc(ln1_stat, 1)

                def h_mv(n, c):
                    dve.wait_ge(ln1_stat, 6 * n + c + 1)
                    need(dve, ln1_rstd, 3 * n)
                    need(dve, xn_done, 6 * n)
                    dve.nop(nofuse=True)
                    dve.bn_aggr(mv1[:, c, :], stat1[:, c, :]).then_inc(ln1_mv, 1)

                def norm_x(n, p, q):
                    dve.wait_ge(ln1_rstd, 3 * n + q + 1)
                    need(dve, x_rest, 2 * (3 * n + q) - 2)
                    for c in range(2 * q, 2 * q + 2):
                        src = H[0:CH, bass.ds(6 * n + c, 1), :].rearrange("p c d -> p (c d)")
                        dve.tensor_scalar(xn[(3 * p + q) % 2][:, c % 2, :], src, mv1[:, c, 0:1], rstd1[:, c:c + 1],
                                          ALU.subtract, ALU.mult).then_inc(xn_done, 1)

                def copy_x_side(n, q):
                    dve.wait_ge(xt_main, 3 * n + q + 1)
                    c = T2 * q
                    dve.tensor_copy(x_s[:, c:c + T2].rearrange("p (c t) -> p c t", c=2), turn_bank[:, 2, :, 0:CH])\
                        .then_inc(xt_side, 1)

                def copy_y_side(n, p, q):
                    dve.wait_ge(yt_main, 3 * n + q + 1)
                    dve.tensor_copy(y_s[(3 * p + q) % 2][:, 0:T2].rearrange("p (c t) -> p c t", c=2),
                                    y_bank[:, 2, :, 0:CH]).then_inc(yt_side, 1)

                def take_core(n, c):
                    dve.wait_ge(core_done, 6 * n + c + 1)
                    need(dve, num_done, 6 * n + c - 1)
                    dve.tensor_tensor(pk[c % 2][:, :], core_bank[0:CH, 0:CH + M_DIM], causal[:, :],
                                      ALU.mult).then_inc(pk_done, 1)
                    if c == 1:
                        dve.tensor_copy(state[1][:, :], core_bank[0:M_DIM, 256:256 + D + 1]).then_inc(state_done, 1)
                    if c > 1:
                        dve.wait_ge(state_done, 5 * n + c - 1)
                        dve.tensor_tensor(state[c % 2][:, :], core_bank[0:M_DIM, 256:256 + D + 1],
                                          state[(c - 1) % 2][:, :], ALU.add).then_inc(state_done, 1)

                def num_stats(n, q):
                    m = 3 * n + q
                    s = slice(2 * q, 2 * q + 2)
                    dve.wait_ge(num_out, m + 1)
                    need(dve, ln2_scale, 3 * n)
                    need(dve, y_done, 6 * n)
                    dve.tensor_scalar(den[:, s], num[:, :, D], 1e-6, 1e-5 ** 0.5, ALU.add, ALU.mult)\
                        .then_inc(den_scaled, 1)
                    dve.nop(nofuse=True)
                    for c in range(2):
                        dve.bn_stats(stat2[:, 2 * q + c, :], num[:, c, 0:D]).then_inc(ln2_stat, 1)
                    for c in range(2):
                        dve.wait_ge(ln2_stat, 2 * m + c + 1)
                        dve.nop(nofuse=True)
                        dve.bn_aggr(mv2[:, 2 * q + c, :], stat2[:, 2 * q + c, :]).then_inc(ln2_mv, 1)

                def norm_y(n, q):
                    m = 3 * n + q
                    dve.wait_ge(ln2_scale, m + 1)
                    need(dve, y_rest, 2 * m)
                    for c in range(2):
                        dve.tensor_scalar(y[:, c, :], num[:, c, 0:D], mv2[:, 2 * q + c, 0:1],
                                          hscale[:, 2 * q + c:2 * q + c + 1], ALU.subtract, ALU.mult)\
                            .then_inc(y_done, 1)

                def add_out(n, q):
                    dve.wait_ge(out_done, 3 * n + q + 1)
                    dve.wait_ge(h_biased, 3 * n + q + 1)
                    dst = H[0:CH, bass.ds(6 * n + 2 * q, 2), :].rearrange("p c d -> p (c d)")
                    dve.scalar_tensor_tensor(out=dst, in0=proj_bank[1 if q < 2 else 0][0:CH, 0:2 * D], scalar=1.0 / WS, in1=dst,
                                             op0=ALU.mult, op1=ALU.add).then_inc(h_done, 1)

                def clamp(n):
                    dve.wait_ge(proj_out, 7 * n + 4)
                    dve.tensor_scalar(gate[:, :], gate[:, :], PROB_CLAMP, None, ALU.min).then_inc(f_clamped, 1)

                def scan(n):
                    dve.wait_ge(f_logged, n + 1)
                    dve.tensor_tensor_scan(gate[:, :], gate[:, :], gate[:, :], 0.0, ALU.add, ALU.max)\
                        .then_inc(f_summed, 1)
                    dve.wait_ge(f_summed, n + 1)
                    dve.tensor_scalar(gate[:, :], gate[:, :], 20.0, -20.0, ALU.min, ALU.max).then_inc(f_clipped, 1)

                def elu(n):
                    dve.wait_ge(qk_exp, n + 1)
                    dve.scalar_tensor_tensor(out=qk_e[:, :], in0=qk[:, :], scalar=0.0, in1=qk_e[:, :], op0=ALU.max,
                                             op1=ALU.add).then_inc(qk_elu, 1)

                def gate_qk(n, p, half):
                    s = slice(HALF * half, HALF * half + HALF)
                    if half == 0:
                        dve.wait_ge(gate_done, n + 1)
                        dve.wait_ge(qk_elu, n + 1)
                        need(dve, num_done, 6 * (n - 1))
                    dve.scalar_tensor_tensor(out=qT[p][:, s], in0=qk_e[0:64, s], scalar=M_DIM ** -0.5,
                                             in1=gate[0:64, s], op0=ALU.mult, op1=ALU.mult).then_inc(q_done, 1)
                    dve.tensor_tensor(kT[p][:, s], qk_e[64:128, s], gate[64:128, s], ALU.mult).then_inc(k_done, 1)

                def mixed(n, p, front, back, before):
                    m, r = n + 1, 1 - p
                    if back:
                        gate_qk(n, p, 0)
                    if front:
                        h_add(m, 0)
                        h_stat(m, 0)
                        h_add(m, 1)
                        h_mv(m, 0)
                    if before:
                        copy_y_side(n - 1, r, 2)
                    if front:
                        h_stat(m, 1)
                    if not front:
                        dve.wait_ge(h_done, 3 * BATCH - 4)
                        stats_b(dve, 0)
                    if back:
                        take_core(n, 0)
                    if front:
                        h_mv(m, 1)
                    if back:
                        gate_qk(n, p, 1)
                    else:
                        prepare_projections()
                    if front:
                        h_add(m, 2)
                    if back:
                        take_core(n, 1)
                    if front:
                        norm_x(m, r, 0)
                    if before:
                        add_out(n - 1, 2)
                    if not back:
                        dve.wait_ge(beta_mm, 1)
                        dve.tensor_copy(beta_out[:, :], num_bank[0:CH, 0:D]).then_inc(beta_set, 1)
                    if front:
                        h_stat(m, 2)
                    if front:
                        h_mv(m, 2)
                        h_add(m, 3)
                    if not front:
                        norm_b(dve, 0, 0)
                    if back:
                        take_core(n, 2)
                    if front:
                        h_stat(m, 3)
                    if front:
                        h_mv(m, 3)
                    if back:
                        num_stats(n, 0)
                    if front:
                        h_add(m, 4)
                        norm_x(m, r, 1)
                        copy_x_side(m, 0)
                    if back:
                        take_core(n, 3)
                    if front:
                        h_stat(m, 4)
                    if back:
                        norm_y(n, 0)
                    if front:
                        h_mv(m, 4)
                        h_add(m, 5)
                    if not front:
                        copy_gx_side(dve, 0, 0, 0)
                    if back:
                        take_core(n, 4)
                    if front:
                        h_stat(m, 5)
                        if not back:
                            h_mv(m, 5)
                        copy_x_side(m, 1)
                        if back:
                            h_mv(m, 5)
                    if back:
                        num_stats(n, 1)
                        copy_y_side(n, p, 0)
                        take_core(n, 5)
                    if front:
                        norm_x(m, r, 2)
                    if not front:
                        copy_gx_side(dve, 0, 0, 1)
                    if back:
                        add_out(n, 0)
                        norm_y(n, 1)
                    if front:
                        copy_x_side(m, 2)
                    if back:
                        num_stats(n, 2)
                        copy_y_side(n, p, 1)
                    if front:
                        clamp(m)
                    if back:
                        norm_y(n, 2)
                        add_out(n, 1)
                    if front:
                        scan(m)
                        elu(m)

                dve.wait_ge(base_set, 3)
                dve.wait_ge(consts_set, 9)
                mixed(-1, 1, True, False, False)
                for n in range(4):
                    mixed(n, n % 2, True, True, n > 0)
                with dve.Fori(2, BATCH // 2 - 1) as pair_of:
                    n = pair_of * 2
                    mixed(n, 0, True, True, True)
                    mixed(n + 1, 1, True, True, True)
                mixed(BATCH - 2, 0, True, True, True)
                mixed(BATCH - 1, 1, False, True, True)
                copy_y_side(BATCH - 1, 1, 2)
                add_out(BATCH - 1, 2)
                logits(dve, 0)
                dve.wait_ge(moe_lo, 8)
                dve.wait_ge(h_done, 3 * BATCH)

        ctxb = ExitStack()
        with ctxb:
            def sa(name, shape, dt=fp32):
                return sb(name, shape, dt, ctxb)

            def sema(name):
                return sem(name, ctxb)

            gx_hl.append(sa("gx_hl_odd", [128, 2, GT], fp16))
            gx_s.append(sa("gx_s_odd", [128, GT], fp16))
            x2.append(sa("x2_odd", [CH, GCH, D]))
            z32 = [sa(f"z32_{i}", [128, GT]) for i in range(Z_BANKS)]
            z_h = [sa(f"z_h{i}", [128, 2, 512], fp16) for i in range(Z_RING)]
            z_l = [sa(f"z_l{i}", [128, 2, 512], fp16) for i in range(Z_RING)]
            acc = [sa(f"acc{i}", [CH, GCH, D]) for i in range(2)]
            hb = sa("hb", [CH, GCH, D])
            res = [sa(f"res{i}", [CH, GCH, D]) for i in range(2)]
            cstat = sa("cstat", [CH, GCH, 6])
            cmv = sa("cmv", [CH, GCH, 2])
            crstd = sa("crstd", [CH, GCH])
            cvar = sa("cvar", [CH, GCH])
            shifted = sa("shifted", [CH, GCH, NE])
            euler = sa("euler", [CH, GCH, NE])
            expo = sa("expo", [CH, GCH, NE])
            esum = sa("esum", [CH, GCH])
            einv = sa("einv", [CH, GCH])
            prob = sa("prob", [CH, GCH, NE])
            top = sa("top", [CH, GCH, 8])
            above = sa("above", [CH, GCH, NE])
            equal = sa("equal", [CH, GCH, NE])
            resets = sa("resets", [CH, GCH, NE])
            rank = sa("rank", [CH, GCH, NE])
            first_above = sa("first_above", [CH, GCH])
            rank2 = sa("rank2", [CH, GCH, NE])
            taken = sa("taken", [CH, GCH, NE])
            picked = sa("picked", [CH, GCH, NE])
            weighted = sa("weighted", [CH, GCH, NE])
            tsum = sa("tsum", [CH, GCH])
            tscaled = sa("tscaled", [CH, GCH])
            tinv = sa("tinv", [CH, GCH])
            share = [sa(f"share{i}", [CH, GCH, NE]) for i in range(2)]

            z_bank = [banks[i] for i in (0, 2, 3, 4)]
            up_bank = [banks[5], ctxb.enter_context(nc.psum_tensor("last_bank", [128, 512], fp32))]

            block = ctxb.enter_context(nc.Block())

            @block.sync
            def _(sp):
                def store(g, p):
                    sp.wait_ge(res_done, g + 1)
                    dst = out[bass.ds(g * GT, GT), :].rearrange("(c p) d -> p c d", p=CH)
                    sp.dma_start(dst[0:112], res[p][0:112]).then_inc(stored[p], 16)
                    sp.dma_start(dst[112:CH], res[p][112:CH]).then_inc(stored[p], 16)

                with sp.Fori(0, NG // 2 - 1) as pair_of:
                    g = pair_of * 2
                    store(g, 0)
                    store(g + 1, 1)
                store(NG - 2, 0)
                last = out[(NG - 1) * GT:NG * GT, :].rearrange("(c p) d -> p c d", p=CH)
                for half in range(2):
                    sp.wait_ge(last_res, half + 1)
                    k = slice(2 * half, 2 * half + 2)
                    sp.dma_start(last[:, k, :], res[1][:, k, :]).then_inc(stored[1], 16)
                for p in range(2):
                    sp.wait_ge(stored[p], 16 * NG)

            @block.gpsimd
            def _(pool):
                for i in range(Z_RING):
                    for buf in (z_h[i], z_l[i]):
                        pool.memset(buf[:, :, GT:512], 0.0).then_inc(b_consts, 1)
                pool.memset(euler[:, :, :], 2.718281828459045).then_inc(b_consts, 1)
                pool.memset(resets[:, :, :], 1.0).then_inc(b_consts, 1)
                pool.wait_ge(b_consts, 10)
                pool.memset(resets[:, :, 0:1], 0.0).then_inc(b_consts, 1)

                def rsqrt_c(g):
                    pool.wait_ge(c_mv, 4 * g + 4)
                    need(pool, normed, 4 * g)
                    pool.tensor_tensor(cvar[:, :], cmv[:, :, 1], epsilon[:, 0:GCH], ALU.add).then_inc(c_var, 1)
                    pool.wait_ge(c_var, g + 1)
                    pool.tensor_tensor(crstd[:, :], cvar[:, :], minus_half[:, 0:GCH], ALU.pow).then_inc(c_rstd, 1)

                def wide(a):
                    return a.unsqueeze(2).broadcast_to([CH, GCH, NE])

                def softmax_exp(g):
                    pool.wait_ge(lmax_done, g + 1)
                    need(pool, expo_done, g)
                    pool.tensor_tensor(shifted[:, :, :], logit[:, :, :], wide(lmax[:, :]), ALU.subtract)\
                        .then_inc(shift_done, 1)
                    pool.wait_ge(shift_done, g + 1)
                    need(pool, prob_done, g)
                    pool.tensor_tensor(expo[:, :, :], euler[:, :, :], shifted[:, :, :], ALU.pow).then_inc(expo_done, 1)

                def probabilities(g):
                    pool.wait_ge(einv_done, g + 1)
                    need(pool, share_done, g)
                    pool.tensor_tensor(prob[:, :, :], expo[:, :, :], wide(einv[:, :]), ALU.mult).then_inc(prob_done, 1)

                def choose(g, p):
                    pool.wait_ge(picked_done, g + 1)
                    need(pool, share_done, g)
                    pool.tensor_tensor(weighted[:, :, :], picked[:, :, :], prob[:, :, :], ALU.mult)\
                        .then_inc(weighted_done, 1)
                    pool.wait_ge(weighted_done, g + 1)
                    pool.wait_ge(tinv_done, g + 1)
                    need(pool, acc_done, 32 * (g - 1))
                    pool.tensor_tensor(share[p][:, :, :], weighted[:, :, :], wide(tinv[:, :]), ALU.mult)\
                        .then_inc(share_done, 1)

                def add_beta(g):
                    need(pool, res_done, g)
                    pool.tensor_tensor(hb[:, :, :], H[0:CH, bass.ds(GCH * g, GCH), :],
                                       ffn_beta.unsqueeze(1).broadcast_to([CH, GCH, D]), ALU.add).then_inc(hb_done, 1)

                def finish(g, p):
                    pool.wait_ge(normed, 4 * g + 4)
                    pool.tensor_tensor(acc[p][:, :, :], acc[p][:, :, :],
                                       ffn_gamma.unsqueeze(1).broadcast_to([CH, GCH, D]), ALU.mult).then_inc(scaled, 1)
                    pool.wait_ge(scaled, g + 1)
                    pool.wait_ge(hb_done, g + 1)
                    need(pool, stored[p], 16 * (g - p))
                    pool.tensor_tensor(res[p][:, :, :], acc[p][:, :, :], hb[:, :, :], ALU.add).then_inc(res_done, 1)

                def group(g, p, prep, fin):
                    if prep:
                        rest_b(pool, g + 1, 1 - p)
                    if fin:
                        add_beta(g - 1)
                        rsqrt_c(g - 1)
                        finish(g - 1, 1 - p)
                    if prep:
                        softmax_exp(g + 1)
                        probabilities(g + 1)
                    if not (isinstance(g, int) and g + 2 >= NG):
                        rsqrt_b(pool, g + 2)
                    if prep:
                        choose(g + 1, 1 - p)

                softmax_exp(0)
                probabilities(0)
                rsqrt_b(pool, 1)
                choose(0, 0)
                group(0, 0, True, False)
                group(1, 1, True, True)
                group(2, 0, True, True)
                group(3, 1, True, True)
                with pool.Fori(2, NG // 2 - 1) as pair_of:
                    g = pair_of * 2
                    group(g, 0, True, True)
                    group(g + 1, 1, True, True)
                group(NG - 2, 0, True, True)
                group(NG - 1, 1, False, True)
                add_beta(NG - 1)
                for half in range(2):
                    k = slice(2 * half, 2 * half + 2)
                    pool.wait_ge(c_mv, 4 * (NG - 1) + 2 * half + 2)
                    if half == 0:
                        pool.wait_ge(normed, 4 * (NG - 1))
                    pool.tensor_tensor(cvar[:, k], cmv[:, k, 1], epsilon[:, 0:2], ALU.add).then_inc(c_var, 1)
                    pool.wait_ge(c_var, NG + half)
                    pool.tensor_tensor(crstd[:, k], cvar[:, k], minus_half[:, 0:2], ALU.pow).then_inc(c_rstd, 1)

            @block.scalar
            def _(act):
                def gelu_hidden(g, e):
                    for t in range(2):
                        n = 16 * g + 2 * e + t
                        i = (2 * e + t) % Z_BANKS
                        act.wait_ge(z_done, n + 1)
                        need(act, zl_done, n + 1 - Z_BANKS)
                        bias = down_b[:, 2 * e + t:2 * e + t + 1]
                        act.activation(z32[i][:, :], z_bank[i][:, 0:GT], ACT.Gelu, bias=bias, scale=1.0 / WS)\
                            .then_inc(z32_done, 1)
                        if t == 0:
                            need(act, up_done, 2 * (8 * g + e + 1 - Z_RING))
                        act.activation(z_h[e % Z_RING][:, t, 0:GT], z_bank[i][:, 0:GT], ACT.Gelu, bias=bias,
                                       scale=1.0 / WS).then_inc(zh_done, 1)

                def group(g, p, own, prep):
                    for e in range(NE):
                        if e < 6:
                            if own:
                                gelu_hidden(g, e + 2)
                        elif prep:
                            gelu_hidden(g + 1, e - 6)
                        if prep:
                            if e == 0:
                                round_b(act, g + 1, 1 - p)
                            if e == 1:
                                copy_gx_main(act, g + 1, 1 - p, 0)
                            if e == 2:
                                copy_gx_main(act, g + 1, 1 - p, 1)
                            if e == 3:
                                gelu_router(act, g + 1)

                gelu_hidden(0, 0)
                gelu_hidden(0, 1)
                group(0, 0, True, True)
                group(1, 1, True, True)
                with act.Fori(1, NG // 2 - 1) as pair_of:
                    g = pair_of * 2
                    group(g, 0, True, True)
                    group(g + 1, 1, True, True)
                group(NG - 2, 0, True, True)
                group(NG - 1, 1, True, False)

            @block.tensor
            def _(pe):
                def down(g, p, e):
                    if e == 0:
                        pe.wait_ge(gx_main, 2 * g + 2)
                        pe.wait_ge(gx_side, 2 * g + 2)
                    for t in range(2):
                        n = 16 * g + 2 * e + t
                        need(pe, zh_done, n + 1 - Z_BANKS)
                        lo = 128 * (2 * e + t)
                        mm_features(pe, z_bank[(2 * e + t) % Z_BANKS][:, 0:GT], down_h, down_l, lo, lo + 128,
                                    gx_hl[p], gx_s[p], 0, GT).then_inc(z_done, 1)

                def up(g, e):
                    s = 8 * g + e
                    i = e % Z_RING
                    pe.wait_ge(zh_done, 2 * s + 2)
                    pe.wait_ge(zl_done, 2 * s + 2)
                    for half in range(2):
                        need(pe, acc_done, 4 * s - 2 + 2 * half)
                        for c in range(2):
                            a = CH * (2 * half + c)
                            k = 0
                            for t in range(2):
                                z1, z0 = z_h[i][:, t, a:a + 128], z_l[i][:, t, a:a + 128]
                                for z, w in ((z1, up_h), (z1, up_l), (z0, up_h)):
                                    mm = pe.matmul(up_bank[half][:, D * c:D * c + D], z, w[:, 2 * e + t, :],
                                                   start=(k == 0), stop=(k == 5))
                                    k += 1
                        mm.then_inc(up_done, 1)

                def group(g, p, own, prep):
                    q = 1 - p
                    for e in range(NE):
                        if e < 6:
                            if own:
                                down(g, p, e + 2)
                        elif prep:
                            down(g + 1, q, e - 6)
                        if prep:
                            if e == 3:
                                route1(pe, g + 1, q)
                            if e == 4:
                                route2(pe, g + 1)
                        if own:
                            up(g, e)
                        if prep and e in (1, 2):
                            turn(pe, g + 1, q, e - 1)

                down(0, 0, 0)
                down(0, 0, 1)
                pe.wait_ge(b_consts, 8)
                group(0, 0, True, True)
                group(1, 1, True, True)
                with pe.Fori(1, NG // 2 - 1) as pair_of:
                    g = pair_of * 2
                    group(g, 0, True, True)
                    group(g + 1, 1, True, True)
                group(NG - 2, 0, True, True)
                group(NG - 1, 1, True, False)

            @block.vector
            def _(dve):
                def expo_sums(g):
                    dve.wait_ge(expo_done, g + 1)
                    need(dve, einv_done, g)
                    dve.tensor_reduce(esum[:, :], expo[:, :, :], AX, ALU.add).then_inc(esum_done, 1)
                    dve.wait_ge(esum_done, g + 1)
                    need(dve, prob_done, g)
                    dve.reciprocal(einv[:, :], esum[:, :]).then_inc(einv_done, 1)

                def tops(g):
                    dve.wait_ge(prob_done, g + 1)
                    need(dve, share_done, g)
                    dve.nop(nofuse=True)
                    for c in range(GCH):
                        dve.max(top[:, c, :], prob[:, c, :]).then_inc(top_done, 1)

                def compare(g):
                    dve.wait_ge(top_done, 4 * g + 4)
                    second = top[:, :, 1:2].broadcast_to([CH, GCH, NE])
                    dve.tensor_tensor(above[:, :, :], prob[:, :, :], second, ALU.is_gt).then_inc(above_done, 1)
                    dve.tensor_tensor(equal[:, :, :], prob[:, :, :], second, ALU.is_equal).then_inc(equal_done, 1)
                    dve.tensor_tensor(first_above[:, :], top[:, :, 0], top[:, :, 1], ALU.is_gt).then_inc(above_done, 1)
                    dve.tensor_tensor(tsum[:, :], top[:, :, 0], top[:, :, 1], ALU.add).then_inc(tsum_done, 1)

                def pick_two(g):
                    dve.wait_ge(equal_done, g + 1)
                    dve.tensor_tensor_scan(rank[:, :, :].rearrange("p c e -> p (c e)"),
                                           resets[:, :, :].rearrange("p c e -> p (c e)"),
                                           equal[:, :, :].rearrange("p c e -> p (c e)"),
                                           0.0, ALU.mult, ALU.add).then_inc(rank_done, 1)
                    dve.wait_ge(tsum_done, g + 1)
                    dve.tensor_scalar(tscaled[:, :], tsum[:, :], 1e-8, WS, ALU.add, ALU.mult).then_inc(tscaled_done, 1)
                    dve.wait_ge(rank_done, g + 1)
                    dve.wait_ge(above_done, 2 * g + 2)
                    dve.tensor_tensor(rank2[:, :, :], rank[:, :, :],
                                      first_above[:, :].unsqueeze(2).broadcast_to([CH, GCH, NE]), ALU.add)\
                        .then_inc(rank2_done, 1)
                    dve.wait_ge(tscaled_done, g + 1)
                    dve.reciprocal(tinv[:, :], tscaled[:, :]).then_inc(tinv_done, 1)
                    dve.wait_ge(rank2_done, g + 1)
                    dve.scalar_tensor_tensor(out=taken[:, :, :], in0=rank2[:, :, :], scalar=2.0, in1=equal[:, :, :],
                                             op0=ALU.is_le, op1=ALU.mult).then_inc(taken_done, 1)
                    dve.wait_ge(taken_done, g + 1)
                    dve.tensor_tensor(picked[:, :, :], taken[:, :, :], above[:, :, :], ALU.add).then_inc(picked_done, 1)

                def split_hidden(g, e):
                    for t in range(2):
                        n = 16 * g + 2 * e + t
                        dve.wait_ge(zh_done, n + 1)
                        if t == 0:
                            need(dve, up_done, 2 * (8 * g + e + 1 - Z_RING))
                        i = (2 * e + t) % Z_BANKS
                        dve.tensor_tensor(z_l[e % Z_RING][:, t, 0:GT], z32[i][:, :], z_h[e % Z_RING][:, t, 0:GT],
                                          ALU.subtract).then_inc(zl_done, 1)

                def accumulate(g, p, e):
                    s = 8 * g + e
                    if e == 0:
                        dve.wait_ge(share_done, g + 1)
                        need(dve, scaled, g - 1)
                        need(dve, res_done, g - 1)
                    for half in range(2):
                        dve.wait_ge(up_done, 2 * s + half + 1)
                        for c in range(2):
                            k = 2 * half + c
                            if e > 0:
                                dve.wait_ge(acc_done, 4 * s + k - 3)
                            dve.scalar_tensor_tensor(
                                out=acc[p][:, k, :], in0=up_bank[half][0:CH, D * c:D * c + D],
                                scalar=share[p][:, k, e:e + 1], in1=(x2 if e == 0 else acc)[p][:, k, :],
                                op0=ALU.mult, op1=ALU.add).then_inc(acc_done, 1)

                def stats_c(g, p):
                    need(dve, normed, 4 * g)
                    need(dve, c_mv, 4 * g)
                    dve.wait_ge(acc_done, 32 * g + 32)
                    dve.nop(nofuse=True)
                    for c in range(GCH):
                        dve.bn_stats(cstat[:, c, :], acc[p][:, c, :]).then_inc(c_stat, 1)
                    for c in range(GCH):
                        dve.wait_ge(c_stat, 4 * g + c + 1)
                        dve.nop(nofuse=True)
                        dve.bn_aggr(cmv[:, c, :], cstat[:, c, :]).then_inc(c_mv, 1)

                def norm_c(g, p):
                    dve.wait_ge(c_rstd, g + 1)
                    for c in range(GCH):
                        dve.tensor_scalar(acc[p][:, c, :], acc[p][:, c, :], cmv[:, c, 0:1], crstd[:, c:c + 1],
                                          ALU.subtract, ALU.mult).then_inc(normed, 1)

                def group(g, p, own, prep, fin):
                    q = 1 - p
                    for e in range(NE):
                        if prep and e == 6:
                            expo_sums(g + 1)
                        if prep and e == 0:
                            norm_b(dve, g + 1, q)
                        if e < 6:
                            if own:
                                split_hidden(g, e + 2)
                        elif prep:
                            split_hidden(g + 1, e - 6)
                        if prep:
                            if e == 6:
                                tops(g + 1)
                            if e == 7:
                                compare(g + 1)
                                pick_two(g + 1)
                        if own:
                            accumulate(g, p, e)
                        if prep and e in (1, 2):
                            copy_gx_side(dve, g + 1, q, e - 1)
                        if fin and e == 1:
                            stats_c(g - 1, q)
                        if fin and e == 2:
                            norm_c(g - 1, q)
                        if e == 5 and not (isinstance(g, int) and g + 2 >= NG):
                            stats_b(dve, g + 2)
                        if prep and e == 4:
                            logits(dve, g + 1)

                stats_b(dve, 1)
                split_hidden(0, 0)
                expo_sums(0)
                tops(0)
                split_hidden(0, 1)
                compare(0)
                pick_two(0)
                group(0, 0, True, True, False)
                group(1, 1, True, True, True)
                with dve.Fori(1, NG // 2 - 1) as pair_of:
                    g = pair_of * 2
                    group(g, 0, True, True, True)
                    group(g + 1, 1, True, True, True)
                group(NG - 2, 0, True, True, True)
                group(NG - 1, 1, True, False, True)
                dve.wait_ge(normed, 4 * (NG - 1))
                dve.wait_ge(c_mv, 4 * (NG - 1))
                for half in range(2):
                    two = range(2 * half, 2 * half + 2)
                    dve.wait_ge(acc_done, 32 * NG - 2 + 2 * half)
                    dve.nop(nofuse=True)
                    for c in two:
                        dve.bn_stats(cstat[:, c, :], acc[1][:, c, :]).then_inc(c_stat, 1)
                    for c in two:
                        dve.wait_ge(c_stat, 4 * (NG - 1) + c + 1)
                        dve.nop(nofuse=True)
                        dve.bn_aggr(cmv[:, c, :], cstat[:, c, :]).then_inc(c_mv, 1)
                dve.wait_ge(hb_done, NG)
                dve.wait_ge(stored[1], 16 * (NG - 2))
                for half in range(2):
                    k = slice(2 * half, 2 * half + 2)
                    dve.wait_ge(c_rstd, NG + half)
                    for c in range(2 * half, 2 * half + 2):
                        dve.tensor_scalar(acc[1][:, c, :], acc[1][:, c, :], cmv[:, c, 0:1], crstd[:, c:c + 1],
                                          ALU.subtract, ALU.mult).then_inc(normed, 1)
                    dve.wait_ge(normed, 4 * (NG - 1) + 2 * half + 2)
                    dve.tensor_tensor(acc[1][:, k, :], acc[1][:, k, :],
                                      ffn_gamma.unsqueeze(1).broadcast_to([CH, 2, D]), ALU.mult).then_inc(scaled, 1)
                    dve.wait_ge(scaled, NG + half)
                    dve.tensor_tensor(res[1][:, k, :], acc[1][:, k, :], hb[:, k, :], ALU.add).then_inc(last_res, 1)


def kernel(x, x_txt, L0_tok_w, L0_tok_b, L0_tok_cls_token, L0_tok_pos_embedding, L0_txt_W, L0_attn_Wq, L0_attn_Wk,
           L0_attn_Wv, L0_attn_Wf, L0_attn_bf, L0_attn_Wo, L0_attn_gamma, L0_attn_beta, L0_ffn_w1, L0_ffn_b1,
           L0_ffn_w2, L0_ffn_b2, L0_ffn_down_w, L0_ffn_down_b, L0_ffn_up_w, L0_ffn_gamma, L0_ffn_beta):
    import numpy as np
    import concourse.bacc as bacc
    from concourse.bass_utils import run_bass_kernel_spmd

    def arr(a):
        return np.asarray(a)

    def two_tiles(w):
        return np.stack([w[:KA], np.concatenate([w[KA:], w[KA:]], axis=0)], axis=1)

    def column(a):
        return np.concatenate([a[:KA, None], np.concatenate([a[KA:], a[KA:]])[:, None]], axis=1)

    img = arr(x).reshape(BATCH, 3, BLK, 8, BLK, 8).transpose(0, 1, 3, 5, 2, 4).reshape(BATCH, D, BLK * BLK)
    w = arr(L0_tok_w).reshape(D, 3, 2, 8, 2, 8).transpose(2, 4, 1, 3, 5, 0).reshape(2, 2, D, D)
    w_a = w[:, :, :KA].reshape(4, KA, D).transpose(1, 0, 2)
    w_b = w[:, :, KA:].reshape(2, 2 * KB, D).transpose(1, 0, 2)
    wf = arr(L0_attn_Wf)
    b1 = arr(L0_ffn_b1)
    ins = {
        "xblk": img,
        "ids": arr(x_txt).reshape(4, 128).T,
        "wtok": np.concatenate([w_a, w_b], axis=1),
        "pos": arr(L0_tok_pos_embedding)[0],
        "cls": arr(L0_tok_cls_token)[0],
        "rows": np.concatenate([arr(L0_tok_b), arr(L0_ffn_gamma), arr(L0_ffn_beta), arr(L0_ffn_b2)]),
        "cols": np.concatenate([np.concatenate([arr(L0_attn_bf)] * 2)[:, None], column(arr(L0_attn_gamma)),
                                column(arr(L0_attn_beta)), arr(L0_ffn_down_b).reshape(HT, 128).T,
                                np.concatenate([b1, b1])[:128, None]], axis=1),
        "table": arr(L0_txt_W),
        "wproj": two_tiles(np.concatenate([arr(L0_attn_Wq), arr(L0_attn_Wk), wf, wf, arr(L0_attn_Wv)], axis=1)),
        "wout": two_tiles(arr(L0_attn_Wo)),
        "wr1": two_tiles(arr(L0_ffn_w1)),
        "wr2": arr(L0_ffn_w2),
        "wdown": two_tiles(arr(L0_ffn_down_w).transpose(1, 0, 2).reshape(D, NE * DH)),
        "wup": arr(L0_ffn_up_w).reshape(HT, 128, D).transpose(1, 0, 2),
    }
    nc = bacc.Bacc("TRN2", target_bir_lowering=False, num_devices=1)
    arrays, args = {}, {}
    for name, a in ins.items():
        a = np.ascontiguousarray(a)
        arrays[f"in_{name}"] = a
        args[name] = nc.dram_tensor(f"in_{name}", a.shape, mybir.dt.from_np(a.dtype), kind="ExternalInput").ap()
    res = nc.dram_tensor("tokens_out", (BATCH * L, D), mybir.dt.float32, kind="ExternalOutput").ap()
    embed_fuse_moe(nc, out=res, **args)
    r = run_bass_kernel_spmd(nc, [arrays], core_ids=[0])
    return r.results[0]["tokens_out"].reshape(BATCH, L, D)
```
